# Optimizing a Trainium2 kernel written in Bass

```python
import numpy as np
import jax
import jax.numpy as jnp

def _softmax(x, axis=-1):
    return jax.nn.softmax(x, axis=axis)

def _gelu(x):
    return jax.nn.gelu(x, approximate=True)

def _silu(x):
    return jax.nn.silu(x)

def _sigmoid(x):
    return jax.nn.sigmoid(x)

def _layernorm(x, axis=-1, eps=1e-05):
    m = jnp.mean(x, axis=axis, keepdims=True)
    v = jnp.var(x, axis=axis, keepdims=True)
    return (x - m) / jnp.sqrt(v + eps)

def _scatter_add(tgt, idx, src, axis=0):
    return tgt.at[idx].add(src)

def _segment_sum(src, seg, n):
    return jax.ops.segment_sum(src, seg, n)
kernel_name = 'mk_sandwich_d1_jaxref_r4_604cac'

def setup_inputs(seed: int=0):
    np.random.seed(seed)
    _w = jnp.asarray

    def _L0_attn_setup():
        import jax, jax.numpy as jnp
        import numpy as np
        B, L, H, N = (4, 1024, 256, 64)
        LN_EPS = 1e-05

        def _s4d_kernel(log_A_real, A_imag, C_re, C_im, log_dt, length):
            A = -jnp.exp(log_A_real) + 1j * A_imag
            dt = jnp.exp(log_dt)[:, None]
            dtA = dt * A
            C = C_re + 1j * C_im
            Ct = C * (jnp.exp(dtA) - 1.0) / A
            l = jnp.arange(length, dtype=jnp.float32)
            V = jnp.exp(dtA[:, :, None] * l[None, None, :])
            K = 2.0 * jnp.real(jnp.einsum('hn,hnl->hl', Ct, V))
            return K
        key = jax.random.key(seed)
        ks = jax.random.split(key, 6)
        x = jax.random.normal(ks[0], (B, L, H), dtype=jnp.float32)
        log_A_real = jnp.log(0.5 * jnp.ones((H, N), dtype=jnp.float32))
        A_imag = jnp.broadcast_to(jnp.pi * jnp.arange(N, dtype=jnp.float32), (H, N))
        C_re = jax.random.normal(ks[1], (H, N), dtype=jnp.float32) * 0.5
        C_im = jax.random.normal(ks[2], (H, N), dtype=jnp.float32) * 0.5
        u = jax.random.uniform(ks[3], (H,), dtype=jnp.float32)
        log_dt = u * (jnp.log(0.1) - jnp.log(0.001)) + jnp.log(0.001)
        D = jax.random.normal(ks[4], (H,), dtype=jnp.float32)
        ln_w = jnp.ones((H,), dtype=jnp.float32)
        ln_b = jnp.zeros((H,), dtype=jnp.float32)
        return {'x': x, 'log_A_real': log_A_real, 'A_imag': A_imag, 'C_re': C_re, 'C_im': C_im, 'log_dt': log_dt, 'D': D, 'ln_w': ln_w, 'ln_b': ln_b}
    _L0_attn_in = _L0_attn_setup()

    def _L0_ffn_setup():
        import jax, jax.numpy as jnp
        import numpy as np
        E = 8
        TOP_K = 2
        LN_EPS = 1e-05

        def _layernorm(x, g, b):
            mu = jnp.mean(x, axis=-1, keepdims=True)
            var = jnp.var(x, axis=-1, keepdims=True)
            return (x - mu) * jax.lax.rsqrt(var + LN_EPS) * g + b
        key = jax.random.key(seed)
        ks = jax.random.split(key, 4)
        B, T, H, HF = (4, 512, 256, 512)
        s_in = 1.0 / np.sqrt(H)
        s_hid = 1.0 / np.sqrt(HF)
        return {'x': jax.random.normal(ks[0], (B, T, H), dtype=jnp.float32), 'ln_g': jnp.ones((H,), dtype=jnp.float32), 'ln_b': jnp.zeros((H,), dtype=jnp.float32), 'rW': jax.random.normal(ks[1], (H, E), dtype=jnp.float32) * s_in, 'rb': jnp.zeros((E,), dtype=jnp.float32), 'W1': jax.random.normal(ks[2], (E, H, HF), dtype=jnp.float32) * s_in, 'b1': jnp.zeros((E, HF), dtype=jnp.float32), 'W2': jax.random.normal(ks[3], (E, HF, H), dtype=jnp.float32) * s_hid, 'b2': jnp.zeros((E, H), dtype=jnp.float32)}
    _L0_ffn_in = _L0_ffn_setup()
    _d = {'L0_attn_x': _L0_attn_in['x'], 'L0_attn_log_A_real': _L0_attn_in['log_A_real'], 'L0_attn_A_imag': _L0_attn_in['A_imag'], 'L0_attn_C_re': _L0_attn_in['C_re'], 'L0_attn_C_im': _L0_attn_in['C_im'], 'L0_attn_log_dt': _L0_attn_in['log_dt'], 'L0_attn_D': _L0_attn_in['D'], 'L0_attn_ln_w': _L0_attn_in['ln_w'], 'L0_attn_ln_b': _L0_attn_in['ln_b'], 'L0_ffn_ln_g': _L0_ffn_in['ln_g'], 'L0_ffn_ln_b': _L0_ffn_in['ln_b'], 'L0_ffn_rW': _L0_ffn_in['rW'], 'L0_ffn_rb': _L0_ffn_in['rb'], 'L0_ffn_W1': _L0_ffn_in['W1'], 'L0_ffn_b1': _L0_ffn_in['b1'], 'L0_ffn_W2': _L0_ffn_in['W2'], 'L0_ffn_b2': _L0_ffn_in['b2']}
    _x0 = _d['L0_attn_x']
    _d['L0_attn_x'] = jax.random.normal(jax.random.fold_in(jax.random.key(seed), 1), (8, 512, 256), dtype=_x0.dtype)
    del _x0
    return _d

def reference(L0_attn_x, L0_attn_log_A_real, L0_attn_A_imag, L0_attn_C_re, L0_attn_C_im, L0_attn_log_dt, L0_attn_D, L0_attn_ln_w, L0_attn_ln_b, L0_ffn_ln_g, L0_ffn_ln_b, L0_ffn_rW, L0_ffn_rb, L0_ffn_W1, L0_ffn_b1, L0_ffn_W2, L0_ffn_b2):

    def _L0_attn_ref(x, log_A_real, A_imag, C_re, C_im, log_dt, D, ln_w, ln_b):
        import jax, jax.numpy as jnp
        import numpy as np
        B, L, H, N = (4, 1024, 256, 64)
        LN_EPS = 1e-05

        def _s4d_kernel(log_A_real, A_imag, C_re, C_im, log_dt, length):
            A = -jnp.exp(log_A_real) + 1j * A_imag
            dt = jnp.exp(log_dt)[:, None]
            dtA = dt * A
            C = C_re + 1j * C_im
            Ct = C * (jnp.exp(dtA) - 1.0) / A
            l = jnp.arange(length, dtype=jnp.float32)
            V = jnp.exp(dtA[:, :, None] * l[None, None, :])
            K = 2.0 * jnp.real(jnp.einsum('hn,hnl->hl', Ct, V))
            return K
        b, length, h = x.shape
        K = _s4d_kernel(log_A_real, A_imag, C_re, C_im, log_dt, length)
        n = 2 * length
        Xf = jnp.fft.rfft(x, n=n, axis=1)
        Kf = jnp.fft.rfft(K, n=n, axis=1)
        y = jnp.fft.irfft(Xf * Kf.T[None, :, :], n=n, axis=1)[:, :length, :]
        z = y + x * D[None, None, :]
        r = x + z
        mu = jnp.mean(r, axis=-1, keepdims=True)
        var = jnp.var(r, axis=-1, keepdims=True)
        out = (r - mu) * jax.lax.rsqrt(var + LN_EPS) * ln_w + ln_b
        return out

    def _L0_ffn_ref(x, ln_g, ln_b, rW, rb, W1, b1, W2, b2):
        import jax, jax.numpy as jnp
        import numpy as np
        E = 8
        TOP_K = 2
        LN_EPS = 1e-05

        def _layernorm(x, g, b):
            mu = jnp.mean(x, axis=-1, keepdims=True)
            var = jnp.var(x, axis=-1, keepdims=True)
            return (x - mu) * jax.lax.rsqrt(var + LN_EPS) * g + b
        z = _layernorm(x, ln_g, ln_b)
        logits = jnp.einsum('bth,he->bte', z, rW) + rb
        probs = jax.nn.softmax(logits, axis=-1)
        topv, topi = jax.lax.top_k(probs, TOP_K)
        mask = jnp.sum(jax.nn.one_hot(topi, E, dtype=probs.dtype) * topv[..., None], axis=-2)
        denom = jnp.maximum(jnp.sum(mask, axis=-1, keepdims=True), 1e-08)
        w = mask / denom
        hid = jax.nn.gelu(jnp.einsum('bth,ehf->btef', z, W1) + b1, approximate=False)
        outs = jnp.einsum('btef,efh->bteh', hid, W2) + b2
        mixed = jnp.sum(outs * w[..., None], axis=2)
        return x + mixed
    x = L0_attn_x
    x = x + _layernorm(_L0_attn_ref(_layernorm(x, axis=-1), L0_attn_log_A_real, L0_attn_A_imag, L0_attn_C_re, L0_attn_C_im, L0_attn_log_dt, L0_attn_D, L0_attn_ln_w, L0_attn_ln_b), axis=-1)
    x = x + _layernorm(_L0_ffn_ref(_layernorm(x, axis=-1), L0_ffn_ln_g, L0_ffn_ln_b, L0_ffn_rW, L0_ffn_rb, L0_ffn_W1, L0_ffn_b1, L0_ffn_W2, L0_ffn_b2), axis=-1)
    return x

_drawn_inputs = setup_inputs


def setup_inputs(seed=0):
    import zlib

    import numpy as np

    out = dict(_drawn_inputs(seed))
    spreads = {'L0_attn_log_A_real': (-0.6931471824645996, 0.535),
     'L0_attn_ln_w': (1.0, 0.2),
     'L0_attn_ln_b': (0.0, 0.1),
     'L0_ffn_ln_g': (1.0, 0.2),
     'L0_ffn_ln_b': (0.0, 0.1),
     'L0_ffn_rb': (0.0, 0.1),
     'L0_ffn_b1': (0.0, 0.488),
     'L0_ffn_b2': (0.0, 0.329)}
    factors = {}
    for name, (base, spread) in spreads.items():
        noise = np.random.default_rng([zlib.crc32(name.encode()), seed]).standard_normal(out[name].shape)
        drawn = base * np.exp(spread * noise) if base else spread * noise
        out[name] = jnp.asarray(drawn.astype(out[name].dtype))
    for name, factor in factors.items():
        out[name] = (out[name] * factor).astype(out[name].dtype)
    return out
```

```python
import concourse.bass as bass
from concourse import mybir
from concourse.alu_op_type import AluOpType as ALU

F32 = mybir.dt.float32
F32R = mybir.dt.float32r
BF16 = mybir.dt.bfloat16
I32 = mybir.dt.int32
U32 = mybir.dt.uint32
ACT = mybir.ActivationFunctionType
AX = mybir.AxisListType

P = 128
B, T, H, N = 8, 512, 256, 64
E, F = 8, 512
EPS = 1e-5
KT = T // P
QN, PN = 32, 16
SLOTS = QN + 2 * PN
REGION = B * T + P
LAG = 3
TILES = 2 * B * T // P + E - 1
ROWS = E * REGION + E * P
ROUND = 12582912.0
TURN = 6.283185
KB = 1024
BASE = 16512


class Seq:

    def __init__(self, eng, sem):
        self.eng, self.sem, self.n = eng, sem, 0

    def inc(self, ins):
        ins.then_inc(self.sem, 1)
        self.n += 1

    def wait(self):
        self.eng.wait_ge(self.sem, self.n)


def program(nc, x, fwd_tab, inv_tab, lag_tab, slot_scale, slot_off, ident_in, upper_in, tile_tab, lar, aim, cre, cim,
            ldt, d_skip, ln_w, ln_b, ffn_g, ffn_b, r_w, r_b, w1, b1, w2, b2, out, dbg=None):
    sems = {}

    def sem(name):
        if name not in sems:
            sems[name] = nc.alloc_semaphore(name)
        return sems[name]

    def at(name, shape, dt, off):
        return nc.alloc_sbuf_tensor_at(name, shape, dt, offset=BASE + off)

    v = at("v", [P, SLOTS, P], F32, 0)
    kr = at("kr", [P, SLOTS, P], F32, 32 * KB)
    mag = at("mag", [P, QN + PN, P], F32, 64 * KB)
    zn = [at(f"zn{i}", [P, 4, H], F32, (80 + 4 * i) * KB) for i in range(2)]
    xs = at("xs", [P, B, 4, H], F32, 88 * KB)
    kf = at("kf", [P, 2, KT, H], F32, 120 * KB)
    o0 = 128 * KB
    xn = at("xn", [P, 4, H], F32, o0)
    pm = [at(f"pm{i}", [P, 2, 2, H], F32, o0 + (4 + 4 * i) * KB) for i in range(2)]
    ft = at("ft", [P, 2, 2, T], F32, o0 + 12 * KB)
    it = at("it", [P, 2, KT, 2 * P], F32, o0 + 20 * KB)
    yf = [at(f"yf{i}", [P, 2, KT, H], F32, o0 + (28 + 8 * i) * KB) for i in range(2)]
    lag = at("lag", [P, KT, 2 * KT, P], F32, o0 + 28 * KB)
    tmp = [at(f"tmp{i}", [P, 2, 2, H], F32, o0 + (44 + 4 * i) * KB) for i in range(2)]
    s_sb = at("s_sb", [P, 2, H], F32, o0 + 52 * KB)
    r = at("r", [P, 4, H], F32, o0 + 54 * KB)
    o = at("o", [P, 4, H], F32, o0 + 58 * KB)
    dl = at("dl", [P, 4, H], F32, o0 + 62 * KB)
    zt = at("zt", [P, 2, T], F32, o0 + 66 * KB)
    lwb = at("lwb", [P, 2, H], F32, o0 + 70 * KB)
    lg = at("lg", [E, T], F32, o0 + 72 * KB)
    k_sb = at("k_sb", [P, 64 * QN], F32, o0 + 44 * KB)
    kh = at("kh", [P, 2, T], F32, o0 + 54 * KB)
    k_t = at("k_t", [P, KT, H], F32, o0 + 58 * KB)
    sm = at("sm", [P, 8, 2, N], F32, o0 + 62 * KB)
    quant = at("quant", [P, 4, 2, 2, N], F32, o0 + 66 * KB)
    sm2 = at("sm2", [P, 14, 2, N], F32, 64 * KB)
    qt = at("qt", [P, 4, H], F32, o0 + 0 * KB)
    raw = at("raw", [P, 4, 2, N], F32, o0 + 4 * KB)
    c0 = o0 + 74 * KB
    ident = at("ident", [P, P], F32, c0)
    upper = at("upper", [P, 2, P], BF16, c0 + 512)
    upper_f = at("upper_f", [P, 2, P], F32, o0 + 58 * KB)
    sc = at("sc", [P, SLOTS], F32, c0 + 1024)
    so = at("so", [P, SLOTS], F32, c0 + 1280)
    dtv = at("dtv", [P, 2, 2], F32, c0 + 1536)
    st = at("st", [P, 4, 4, 6], F32, c0 + 5568)
    mv = [at(f"mv{i}", [P, 4, 2], F32, c0 + 1664 + 32 * i) for i in range(4)]
    sd = at("sd", [P, 4, 4], F32, c0 + 1792)
    eps = at("eps", [P, 2], F32, c0 + 1856)
    rs = at("rs", [P, 4, 8], F32, c0 + 1920)
    gb = at("gb", [P, 2, 2], F32, c0 + 2048)
    rw_sb = at("rw_sb", [P, 2, E], F32, c0 + 2080)
    rb_sb = at("rb_sb", [E, 8], F32, c0 + 2144)
    mx = at("mx", [P, 4, 8], F32, c0 + 2176)
    mi = at("mi", [P, 4, 8], U32, c0 + 2304)
    mif = at("mif", [P, 2, 4], F32, c0 + 2432)
    oh = at("oh", [P, 2, 4, E], F32, c0 + 2464)
    mask = at("mask", [P, 4, E], BF16, c0 + 2720)
    msum = at("msum", [P, E], F32, c0 + 2784)
    carry = at("carry", [P, E], F32, c0 + 2816)
    carry_b = at("carry_b", [P, E], BF16, c0 + 2848)
    posf = at("posf", [P, 4, E], F32, c0 + 2880)
    prod = at("prod", [P, 2, 4, E], F32, c0 + 3008)
    posr = at("posr", [P, 2, 4], F32, c0 + 3264)
    pos = [at(f"pos{i}", [P, 2, 4], U32, c0 + 3296 + 32 * i) for i in range(2)]
    iota8 = at("iota8", [P, 2, E], F32, c0 + 3360)
    pos_all = at("pos_all", [P, B, 2, 4], F32, c0 + 3424)
    stat1 = at("stat1", [P, B, 2, 4], F32, c0 + 3680)
    mx_all = at("mx_all", [P, B, 4, E], F32, c0 + 3936)
    tab = at("tab", [1, 2, TILES + 1], I32, c0 + 4960)
    ws = at("ws", [P, E, 2, 2048], F32R, 0)
    w_raw = [at(f"w_raw{e}", [P, 2048], F32, (16 * e + 8) * KB) for e in range(E)]
    b1r = at("b1r", [P, E, F], F32, o0)
    b2r = at("b2r", [P, E, H], F32, o0 + 16 * KB)
    z_in = [at(f"z_in{i}", [P, H], F32, o0 + (24 + i) * KB) for i in range(2)]
    z_f = at("z_f", [P, 2, P], F32, o0 + 26 * KB)
    z_hl = [at(f"z_hl{i}", [P, 2, 2, P], F32R, o0 + (27 + 2 * i) * KB) for i in range(2)]
    hb = at("hb", [P, F], F32, o0 + 31 * KB)
    hg = [at(f"hg{i}", [P, F], F32, o0 + (33 + 2 * i) * KB) for i in range(2)]
    h_hl = [at(f"h_hl{i}", [P, 2, 4, P], F32R, o0 + (37 + 4 * i) * KB) for i in range(2)]
    y_sb = [at(f"y_sb{i}", [P, H], F32, o0 + (45 + i) * KB) for i in range(2)]
    ya = [at(f"ya{i}", [P, 2, 4, H], F32, o0 + 8 * i * KB) for i in range(2)]
    x1s = [at(f"x1s{i}", [P, 4, H], F32, (4 * i) * KB) for i in range(2)]
    acc = [at(f"acc{i}", [P, 4, H], F32, (8 + 4 * i) * KB) for i in range(2)]
    fin = [at(f"fin{i}", [P, 4, H], F32, (16 + 4 * i) * KB) for i in range(2)]
    m0 = o0 + 47 * KB
    cnt = at("cnt", [P, 8, E], F32, m0)
    tri = at("tri", [P, E, E], F32, m0 + 256)
    cmp_t = at("cmp_t", [1, TILES + 1, E], F32, m0 + KB)
    cmp_n = at("cmp_n", [1, TILES + 1, E], F32, m0 + 4 * KB)
    tf = at("tf", [1, 6, TILES + 1], F32, m0 + 7 * KB)
    iot = at("iot", [P, 2, TILES + 1], F32, m0 + 9 * KB)
    zpad = at("zpad", [P, E, H], F32, m0 + 10 * KB)
    padf = at("padf", [P, E], F32, m0 + 18 * KB)
    y_shift = at("y_shift", [P, B * 2 * 4], F32, m0 + 18 * KB + 128)
    padi = at("padi", [P, E], U32, m0 + 18 * KB + 32)
    pcol = at("pcol", [P, 1], F32, m0 + 18 * KB + 64)
    wsm = at("wsm", [P, B, 4, E], F32, m0 + 19 * KB)
    y_cmp = at("y_cmp", [P, B * 2 * 4, E], F32, o0 + 71 * KB)
    wgt = at("wgt", [P, 4, B, 4], F32, m0 + 20 * KB)
    rsm = at("rsm", [P, 4, B, 4], F32, m0 + 21 * KB)
    rm = at("rm", [P, 2, 4, 4], F32, m0 + 22 * KB)
    mvm = [at(f"mvm{i}", [P, 4, 2], F32, m0 + 23 * KB + 32 * i) for i in range(2)]
    d_rep = at("d_rep", [P, H], F32, o0 + 73 * KB)
    psum = nc.alloc_psum_tensor("psum", [P, 8 * 512], F32)

    def bank(n, w=1):
        return psum[:, 512 * n:512 * (n + w)]

    fw = [[bank(2 * i + c).rearrange("p (k h) -> p k h", k=2) for c in range(2)] for i in range(2)]
    iv = [bank(4 + c) for c in range(2)]
    tp = [bank(6), bank(7)]

    ps_z = [bank(7 * i)[:, 0:256].rearrange("p (k t) -> p k t", k=2) for i in range(2)]
    ps_h = [bank(1 + i) for i in range(2)]
    ps_t = [bank(3 + i).rearrange("p (k t) -> p k t", k=4) for i in range(2)]
    ps_y = [bank(5 + i)[:, 0:H] for i in range(2)]

    def w_at(e, c, at_, n):
        return ws[:, bass.ds(e, 1), c, at_:at_ + n].rearrange("p a n -> p (a n)")

    k_dram = nc.dram_tensor("k_dram", [4, PN, 64 * QN], F32, kind="Internal").ap()
    z_rows = nc.dram_tensor("z_rows", [ROWS, H], F32, kind="Internal").ap()
    y_rows = nc.dram_tensor("y_rows", [TILES * P, H], F32, kind="Internal").ap()
    x1_dram = nc.dram_tensor("x1_dram", [P, B, 4, H], F32, kind="Internal").ap()

    def rep(a, parts=P):
        return bass.AP(a.tensor, a.offset, [[0, parts]] + [list(q) for q in a.ap])

    def hn(a):
        return a.rearrange("(t p) n -> p t n", p=P)

    def steps(step):
        for n in range(-2, B + LAG):
            step(n)

    def gate(eng):
        eng.sem_inc(sem(f"gate_{eng.engine.name}"), 1)

    class Row:

        def __init__(self, n, k):
            self.b, self.live, self.par = n + k, 0 <= n + k < B, (n + k) % 2

        def first(self, n=1):
            return self.b < n

    def tiles(eng, part):
        for i in range(-2, 3):
            part(i, i % 2)
        with eng.Fori(0, (TILES - 5) // 2) as j:
            part(j * 2 + 3, 1)
            part(j * 2 + 4, 0)
        for i in range(TILES - 2, TILES + 1):
            part(i, i % 2)

    def load_expert(eng, e):
        eng.dma_start(w_raw[e][:, 0:1024].rearrange("p (k f) -> p k f", k=2),
                      w1[e].rearrange("(k p) f -> p k f", p=P)).then_inc(sem(f"in_w{e}"), 16)
        eng.dma_start(w_raw[e][:, 1024:2048].rearrange("p (k f) -> p k f", k=4),
                      w2[e].rearrange("(k p) f -> p k f", p=P)).then_inc(sem(f"in_w{e}"), 16)

    def live(t):
        return not isinstance(t, int) or 0 <= t < TILES

    def early(t, n=1):
        return isinstance(t, int) and t < n

    with nc.Block() as block:

        @block.sync
        def _(sp):
            sp.dma_start(raw[:, 0], hn(lar)).then_inc(sem("in_modes"), 16)
            sp.dma_start(raw[:, 1], hn(aim)).then_inc(sem("in_modes"), 16)
            sp.dma_start(raw[:, 2], hn(cre)).then_inc(sem("in_modes"), 16)
            sp.dma_start(raw[:, 3], hn(cim)).then_inc(sem("in_modes"), 16)
            sp.dma_start(dtv[:, 0, :], ldt.rearrange("(t p) -> p t", p=P),
                         allow_slow_non_contiguous=True).then_inc(sem("in_modes"), 16)
            sp.dma_start(sc[:, :], slot_scale).then_inc(sem("in_modes"), 16)
            sp.dma_start(so[:, :], slot_off).then_inc(sem("in_modes"), 16)
            sp.dma_start(ident[:, :], ident_in).then_inc(sem("in_modes"), 16)
            sp.dma_start(upper_f[:, :, :], upper_in).then_inc(sem("in_upper"), 16)
            sp.dma_start(xs[:, :, :, :], x).then_inc(sem("in_x"), 16)
            sp.dma_start(lag[:, :, :, :], lag_tab).then_inc(sem("in_lag"), 16)
            sp.dma_start(ft[:, :, :, :], fwd_tab).then_inc(sem("in_tab"), 16)
            sp.dma_start(it[:, :, :, :], inv_tab).then_inc(sem("in_tab"), 16)
            sp.dma_start(d_rep[:, :], rep(d_skip)).then_inc(sem("in_small"), 16)
            sp.dma_start(lwb[:, 0, :], rep(ln_w)).then_inc(sem("in_small"), 16)
            sp.dma_start(lwb[:, 1, :], rep(ln_b)).then_inc(sem("in_small"), 16)
            sp.dma_start(gb[:, 0, :], ffn_g.rearrange("(t p) -> p t", p=P),
                         allow_slow_non_contiguous=True).then_inc(sem("in_small"), 16)
            sp.dma_start(gb[:, 1, :], ffn_b.rearrange("(t p) -> p t", p=P),
                         allow_slow_non_contiguous=True).then_inc(sem("in_small"), 16)
            sp.dma_start(rw_sb[:, :, :], r_w.rearrange("(t p) e -> p t e", p=P)).then_inc(sem("in_small"), 16)
            sp.dma_start(rb_sb[:, 0:1], r_b.rearrange("(e a) -> e a", a=1)).then_inc(sem("in_small"), 16)
            for ht in range(2):
                sp.wait_ge(sem("k_evac"), 2 * ht + 2)
                for j in (2 * ht, 2 * ht + 1):
                    sp.dma_start(k_dram[j], k_sb[32 * j:32 * j + PN, :]).then_inc(sem(f"k_out{ht}"), 16)
                sp.wait_ge(sem(f"k_out{ht}"), 32)
                for j in (2 * ht, 2 * ht + 1):
                    sp.dma_start(kh[64 * (j % 2):64 * (j % 2) + 64, ht, :].rearrange("h (p q) -> h p q", p=PN),
                                 k_dram[j].rearrange("p (h q) -> h p q", q=QN)).then_inc(sem(f"k_in{ht}"), 16)
            sp.wait_ge(sem("k_mm"), 2)
            for e in range(5):
                load_expert(sp, e)
            for b in range(B):
                sp.wait_ge(sem("x1_ready"), b + 1)
                sp.dma_start(x1_dram[:, b], xs[:, b]).then_inc(sem("x1_stored"), 16)
            sp.wait_ge(sem("x1_stored"), 16 * B)
            sp.wait_ge(sem("c_done"), 1)
            sp.dma_start(tri[:, :, :], tile_tab[:, 0:E * E].rearrange("p (a b) -> p a b", a=E)).then_inc(sem("in_e"), 16)
            sp.dma_start(iot[:, :, :], tile_tab[:, E * E:E * E + 2 * (TILES + 1)].rearrange("p (a b) -> p a b", a=2)).then_inc(sem("in_e"), 16)
            sp.dma_start(pcol[:, :], tile_tab[:, E * E + 2 * (TILES + 1):],
                         allow_slow_non_contiguous=True).then_inc(sem("in_e"), 16)
            for par in range(2):
                sp.wait_ge(sem(f"scattered{par}"), 64 * B)
            for e in range(5, E):
                load_expert(sp, e)
            for e in range(E):
                sp.dma_start(b1r[:, e], rep(b1[e])).then_inc(sem("in_b"), 16)
                sp.dma_start(b2r[:, e], rep(b2[e])).then_inc(sem("in_b"), 16)
            sp.wait_ge(sem("zpad_set"), 1)
            sp.dma_start(z_rows[E * REGION:ROWS, :].rearrange("(p e) h -> p e h", p=P), zpad[:, :, :]).then_inc(sem("tail_rows"), 16)

            def load_z(t, par):
                row = sp.value_load(tab[0:1, 0, bass.ds(t, 1)], min_val=0, max_val=ROWS - P)
                if not (isinstance(t, int) and t < 2):
                    sp.wait_ge(sem("tz_mm"), t - 1)
                sp.dma_start(z_in[par][:, :], z_rows[bass.ds(row, P), :]).then_inc(sem(f"z_in{par}"), 16)

            sp.wait_ge(sem("tab_ready"), 1)
            sp.wait_ge(sem("tail_rows"), 16)
            sp.wait_ge(sem("pads"), 16 * E)
            load_z(0, 0)
            load_z(1, 1)
            with sp.Fori(0, (TILES - 3) // 2) as j:
                load_z(j * 2 + 2, 0)
                load_z(j * 2 + 3, 1)
            load_z(TILES - 1, 0)

            def move(b, par):
                if not (isinstance(b, int) and b < 2):
                    sp.wait_ge(sem("m_out"), b - 1)
                sp.dma_start(x1s[par][:, :, :], x1_dram[:, bass.ds(b, 1)].rearrange("p a k h -> p (a k) h")).then_inc(sem(f"x1_in{par}"), 16)

            def store(b, par):
                sp.wait_ge(sem("m_out"), b + 1)
                sp.dma_start(out[:, bass.ds(b, 1)].rearrange("p a k h -> p (a k) h"), fin[par][:, :, :]).then_inc(sem(f"stored{par}"), 16)

            sp.wait_ge(sem("l2_mm"), TILES)
            move(0, 0)
            move(1, 1)
            with sp.Fori(0, B // 2 - 1) as j:
                store(j * 2, 0)
                move(j * 2 + 2, 0)
                store(j * 2 + 1, 1)
                move(j * 2 + 3, 1)
            store(B - 2, 0)
            store(B - 1, 1)
            for par in range(2):
                sp.wait_ge(sem(f"stored{par}"), 16 * (B // 2))

        @block.scalar
        def _(act):
            seq = Seq(act, sem("act_seq"))
            act.wait_ge(sem("in_modes"), 128)
            nc.scalar.activation(dtv[:, 1, :], dtv[:, 0, :], ACT.Exp)
            nc.scalar.activation(sm[:, 0], raw[:, 0], ACT.Exp).then_inc(sem("k_exp"), 1)
            act.wait_ge(sem("k_ua"), 1)
            nc.scalar.activation(sm[:, 1], quant[:, 1, :, 0, :], ACT.Tanh, scale=0.5).then_inc(sem("k_tanh"), 1)
            act.wait_ge(sem("k_half"), 1)
            nc.scalar.activation(sm[:, 4:6], sm[:, 2:4], ACT.Sin, scale=TURN).then_inc(sem("k_trig"), 1)
            for ht in range(2):
                act.wait_ge(sem("k_aq"), ht + 1)
                nc.scalar.activation(mag[:, :, :], mag[:, :, :], ACT.Exp).then_inc(sem("k_mag"), 1)
                act.wait_ge(sem("k_v"), ht + 1)
                for g, (lo, hi, src) in enumerate(((QN + PN, SLOTS, QN), (QN, QN + PN, QN), (0, QN, 0))):
                    last = nc.scalar.activation(v[:, lo:hi], v[:, src:src + hi - lo], ACT.Identity,
                                                bias=so[:, lo:lo + 1])
                    if g == 0:
                        last.then_inc(sem("k_copy"), 1)
                        act.wait_ge(sem("k_copy"), ht + 1)
                last.then_inc(sem("k_off"), 1)
                act.wait_ge(sem("k_turns"), 2 * (ht + 1))
                nc.scalar.activation(kr[:, :, :], v[:, :, :], ACT.Sin, scale=TURN).then_inc(sem("k_sin"), 1)
                act.wait_ge(sem("k_mm"), ht + 1)
                for j in (2 * ht, 2 * ht + 1):
                    nc.scalar.copy(k_sb[32 * j:32 * j + PN, :],
                                   psum[32 * j:32 * j + PN, 4 * 512:8 * 512]).then_inc(sem("k_evac"), 1)
            act.wait_ge(sem("kt_mm"), 1)
            nc.scalar.copy(k_t[:, :, :], bank(0, 2).rearrange("p (l h) -> p l h", l=KT)).then_inc(sem("kt_evac"), 1)
            act.wait_ge(sem("kf_mm"), 1)
            nc.scalar.copy(kf[:, 1], bank(4, 2).rearrange("p (k h) -> p k h", k=KT)).then_inc(sem("kf_ready"), 1)

            def sigma(row, slot):
                act.wait_ge(sem(f"var{slot}"), row.b + 1)
                if not row.first():
                    act.wait_ge(sem(USES[slot]), row.b)
                nc.scalar.activation(sd[:, slot, :], mv[slot][:, :, 1], ACT.Sqrt, bias=eps[:, slot // 3:slot // 3 + 1],
                                     scale=1.0 + EPS if slot == 3 else 1.0).then_inc(sem(f"sd{slot}"), 1)

            def split_high(e):
                act.wait_ge(sem(f"in_w{e}"), 32)
                nc.scalar.copy(ws[:, e, 0], w_raw[e][:, :]).then_inc(sem("w_high"), 1)

            def step(n):
                new, inv, cur, mid, tail = (Row(n, k) for k in (2, 0, -1, -2, -LAG))
                if cur.live:
                    sigma(cur, 2)
                if new.live:
                    sigma(new, 0)
                if tail.live:
                    act.wait_ge(sem("zt_mm"), tail.b + 1)
                    if not tail.first():
                        act.wait_ge(sem("lg_mm"), tail.b)
                    for k in range(2):
                        nc.scalar.activation(zt[:, k, :], tp[k], ACT.Identity, bias=gb[:, 1, k:k + 1],
                                             scale=gb[:, 0, k:k + 1]).then_inc(sem("zt_ready"), 1)
                if cur.live:
                    sigma(cur, 1)
                    act.wait_ge(sem("st_o"), cur.b + 1)
                    if not cur.first():
                        act.wait_ge(sem("x1_ready"), cur.b)
                    for k in range(4):
                        last = nc.scalar.activation(dl[:, k], o[:, k], ACT.Identity, bias=rs[:, 1, 4 + k:5 + k],
                                                    scale=rs[:, 1, k:k + 1])
                    last.then_inc(sem("dl_ready"), 1)
                if tail.live:
                    act.wait_ge(sem("lg_mm"), tail.b + 1)
                    if not tail.first():
                        act.wait_ge(sem("lt_mm"), tail.b)
                    nc.scalar.activation(lg[:, :], tp[0][0:E, :], ACT.Identity,
                                         bias=rb_sb[:, 0:1]).then_inc(sem("lg_ready"), 1)
                if 0 <= n < 5:
                    split_high(n)
                if mid.live:
                    sigma(mid, 3)
                    act.wait_ge(sem("st_x1"), mid.b + 1)
                    if not mid.first(2):
                        act.wait_ge(sem(f"scattered{mid.par}"), 64 * (mid.b - mid.par))
                    for k in range(4):
                        last = nc.scalar.activation(zn[mid.par][:, k], xs[:, mid.b, k],
                                                    ACT.Identity, bias=rs[:, 3, 4 + k:5 + k], scale=rs[:, 3, k:k + 1])
                    last.then_inc(sem("zn_ready"), 1)
                if inv.live:
                    act.wait_ge(sem("inv_mm"), inv.b + 1)
                    if not inv.first():
                        act.wait_ge(sem("r_ready"), inv.b)
                    nc.scalar.copy(s_sb[:, :, :], iv[1].rearrange("p (j h) -> p j h", j=2)).then_inc(sem("s_copied"), 1)

            act.wait_ge(sem("in_small"), 112)
            steps(step)

            act.wait_ge(sem("c_done"), 1)
            nc.scalar.activation(rsm[:, 0], stat1[:, :, 1, :], ACT.Sqrt, bias=eps[:, 0:1]).then_inc(sem("rsm_sd"), 1)
            for e in range(5, E):
                split_high(e)
            act.wait_ge(sem("wsm_sub"), 1)
            nc.scalar.activation(wsm[:, :, :, :], wsm[:, :, :, :], ACT.Exp).then_inc(sem("wsm_exp"), 1)

            def part(i, par):
                t, q = i + 2, par
                if live(t):
                    act.wait_ge(sem("tz_mm"), t + 1)
                    if not early(t):
                        act.wait_ge(sem("z_split"), t)
                    for k in range(2):
                        last = nc.scalar.activation(z_f[:, k], ps_z[q][:, k], ACT.Identity, bias=gb[:, 1, k:k + 1],
                                                    scale=gb[:, 0, k:k + 1])
                    last.then_inc(sem("zf_ready"), 1)
                t, q = i, par
                if live(t):
                    act.wait_ge(sem("th_mm"), t + 1)
                    if not early(t, 2):
                        act.wait_ge(sem("l2_mm"), t - 1)
                    nc.scalar.copy(h_hl[q][:, 0], ps_t[q]).then_inc(sem("h_high"), 1)
                t, q = i + 1, 1 - par
                if live(t):
                    act.wait_ge(sem("hb_ready"), t + 1)
                    if not early(t, 2):
                        act.wait_ge(sem("th_mm"), t - 1)
                    nc.scalar.activation(hg[q][:, :], hb[:, :], ACT.Gelu).then_inc(sem("hg_ready"), 1)

            tiles(act, part)

            def mix(b, par):
                act.wait_ge(sem(f"x1_in{par}"), (b - par) * 8 + 16)
                if not early(b, 2):
                    act.wait_ge(sem("m_fin"), b - 1)
                for k in range(4):
                    last = nc.scalar.activation(acc[par][:, k], x1s[par][:, k], ACT.Identity,
                                                bias=rsm[:, 1, bass.ds(b, 1), k], scale=rsm[:, 0, bass.ds(b, 1), k])
                last.then_inc(sem("m_base"), 1)

            def close(b, par):
                act.wait_ge(sem("m_var"), b + 1)
                nc.scalar.activation(rm[:, par, 0, :], mvm[par][:, :, 1], ACT.Sqrt, bias=eps[:, 0:1]).then_inc(sem("m_sd"), 1)
                act.wait_ge(sem("m_rs"), b + 1)
                if not early(b, 2):
                    act.wait_ge(sem(f"stored{par}"), (b - par) * 8)
                for k in range(4):
                    last = nc.scalar.activation(fin[par][:, k], acc[par][:, k], ACT.Identity,
                                                bias=rm[:, par, 2, k:k + 1], scale=rm[:, par, 1, k:k + 1])
                last.then_inc(sem("m_fin"), 1)

            act.wait_ge(sem("rsm_ready"), 1)
            mix(0, 0)
            for b in range(2):
                mix(b + 1, 1 - b)
                close(b, b)
            with act.Fori(0, B // 2 - 2) as j:
                mix(j * 2 + 3, 1)
                close(j * 2 + 2, 0)
                mix(j * 2 + 4, 0)
                close(j * 2 + 3, 1)
            mix(B - 1, 1)
            close(B - 2, 0)
            close(B - 1, 1)

        @block.vector
        def _(dve):
            seq = Seq(dve, sem("dve_seq"))
            V = nc.vector

            def do(ins):
                seq.inc(ins)
                seq.wait()

            def stats(src, slot):
                for k in range(4):
                    last = V.bn_stats(st[:, slot, k, :], src(k))
                do(last)
                for k in range(4):
                    last = V.bn_aggr(mv[slot][:, k, :], st[:, slot, k, :])
                last.then_inc(sem(f"var{slot}"), 1)

            V.memset(eps[:, 0:1], EPS)
            V.memset(eps[:, 1:2], EPS * EPS).then_inc(sem("one"), 1)
            V.memset(carry[:, :], 0.0)
            seq.inc(V.memset(carry_b[:, :], 0.0))
            for e in range(E):
                V.memset(iota8[:, 0, e:e + 1], float(e))
                V.memset(iota8[:, 1, e:e + 1], float(e * REGION))
            dve.wait_ge(sem("in_upper"), 16)
            do(V.tensor_copy(upper[:, :, :], upper_f[:, :, :]))
            dve.wait_ge(sem("k_exp"), 1)
            for ht in range(2):
                for dup in range(2):
                    V.tensor_scalar(quant[:, 0, ht, dup], raw[:, 1, ht], dtv[:, 1, ht:ht + 1], 0.15915494309189535,
                                    ALU.mult, ALU.mult)
                    last = V.tensor_scalar(quant[:, 1, ht, dup], sm[:, 0, ht], dtv[:, 1, ht:ht + 1], -1.0,
                                           ALU.mult, ALU.mult)
            last.then_inc(sem("k_ua"), 1)
            dve.wait_ge(sem("k_ua"), 1)
            do(V.tensor_scalar(sm[:, 2], quant[:, 0, :, 0], 0.5, None, ALU.mult))
            do(V.tensor_scalar(sm[:, 3], sm[:, 2], 0.25, None, ALU.add))
            do(V.tensor_scalar(sm2[:, 0:2], sm[:, 2:4], ROUND, ROUND, ALU.add, ALU.subtract))
            V.tensor_tensor(sm[:, 2:4], sm[:, 2:4], sm2[:, 0:2], ALU.subtract).then_inc(sem("k_half"), 1)
            dve.wait_ge(sem("k_tanh"), 1)
            em1, t1, t2, t3 = sm2[:, 2], sm2[:, 3], sm2[:, 4], sm2[:, 5]
            do(V.tensor_scalar(t1, sm[:, 1], -1.0, 1.0, ALU.mult, ALU.add))
            do(V.reciprocal(t2, t1))
            do(V.scalar_tensor_tensor(em1, sm[:, 1], 2.0, t2, ALU.mult, ALU.mult))
            ea, ai, cr, ci = sm[:, 0], raw[:, 1], raw[:, 2], raw[:, 3]
            dve.wait_ge(sem("k_trig"), 1)
            sn, cs = sm[:, 4], sm[:, 5]
            ere, eim, nre, nim = sm2[:, 6], sm2[:, 7], sm2[:, 8], sm2[:, 9]
            do(V.tensor_tensor(t1, sn, sn, ALU.mult))
            do(V.tensor_scalar(t2, t1, -2.0, 1.0, ALU.mult, ALU.add))
            do(V.tensor_tensor(t2, em1, t2, ALU.mult))
            do(V.scalar_tensor_tensor(ere, t1, -2.0, t2, ALU.mult, ALU.add))
            do(V.tensor_tensor(t3, sn, cs, ALU.mult))
            do(V.scalar_tensor_tensor(t1, em1, 1.0, t3, ALU.add, ALU.mult))
            do(V.tensor_scalar(eim, t1, 2.0, None, ALU.mult))
            do(V.tensor_tensor(t1, cr, ere, ALU.mult))
            do(V.tensor_tensor(t2, ci, eim, ALU.mult))
            do(V.tensor_tensor(nre, t1, t2, ALU.subtract))
            do(V.tensor_tensor(t1, cr, eim, ALU.mult))
            do(V.tensor_tensor(t2, ci, ere, ALU.mult))
            do(V.tensor_tensor(nim, t1, t2, ALU.add))
            do(V.tensor_tensor(t1, ea, ea, ALU.mult))
            do(V.tensor_tensor(t2, ai, ai, ALU.mult))
            do(V.tensor_tensor(t1, t1, t2, ALU.add))
            do(V.reciprocal(t3, t1))
            do(V.tensor_tensor(t1, nim, ai, ALU.mult))
            do(V.tensor_tensor(t2, nre, ea, ALU.mult))
            do(V.tensor_tensor(t1, t1, t2, ALU.subtract))
            for dup in range(2):
                do(V.scalar_tensor_tensor(quant[:, 2, :, dup], t1, 2.0, t3, ALU.mult, ALU.mult))
            do(V.tensor_tensor(t1, nim, ea, ALU.mult))
            do(V.tensor_tensor(t2, nre, ai, ALU.mult))
            do(V.tensor_tensor(t1, t1, t2, ALU.add))
            for dup in range(2):
                last = V.scalar_tensor_tensor(quant[:, 3, :, dup], t1, -2.0, t3, ALU.mult, ALU.mult)
            last.then_inc(sem("k_quant"), 1)
            dve.wait_ge(sem("k_tr"), 1)
            V.tensor_copy(qt[:, :, :], bank(0, 2).rearrange("p (q h) -> p q h", q=4)).then_inc(sem("k_qt"), 1)
            dve.wait_ge(sem("k_qt"), 1)
            G0, G1 = QN, QN + PN
            for ht in range(2):
                if ht:
                    dve.wait_ge(sem("k_mm"), ht)
                hs = slice(ht * P, ht * P + P)
                V.tensor_tensor(v[:, 0:G1], qt[:, 0, hs].unsqueeze(1).to_broadcast([P, G1, P]),
                                sc[:, 0:G1].unsqueeze(2).to_broadcast([P, G1, P]), ALU.mult).then_inc(sem("k_v"), 1)
                dve.wait_ge(sem("k_off"), ht + 1)
                V.tensor_scalar(kr[:, :, :], v[:, :, :], ROUND, ROUND, ALU.add, ALU.subtract).then_inc(sem("k_round"), 1)
                dve.wait_ge(sem("k_round"), ht + 1)
                V.tensor_tensor(v[:, 0:G0], v[:, 0:G0], kr[:, 0:G0], ALU.subtract).then_inc(sem("k_turns"), 1)
                dve.wait_ge(sem("k_sin"), ht + 1)
                dve.wait_ge(sem("k_mag"), ht + 1)

                def wide(q):
                    return qt[:, q, hs].unsqueeze(1).to_broadcast([P, PN, P])

                V.tensor_tensor(v[:, 0:G0], kr[:, 0:G0], mag[:, 0:G0], ALU.mult)
                do(V.tensor_tensor(kr[:, G0:G1], kr[:, G0:G1], wide(2), ALU.mult))
                dve.wait_ge(sem("k_g2"), ht + 1)
                do(V.tensor_tensor(kr[:, G0:G1], kr[:, G0:G1], kr[:, G1:SLOTS], ALU.add))
                V.tensor_tensor(v[:, G0:G1], kr[:, G0:G1], mag[:, G0:G1], ALU.mult).then_inc(sem("k_factors"), 1)
            dve.wait_ge(sem("in_small"), 112)
            do(V.tensor_scalar(d_rep[:, :], d_rep[:, :], 1.0, None, ALU.add))
            dve.wait_ge(sem("kf_mm"), 1)
            for k in range(KT):
                last = V.tensor_tensor(kf[:, 0, k], bank(2, 2)[:, k * H:(k + 1) * H], d_rep[:, :], ALU.add)
            last.then_inc(sem("kf_ready"), 1)
            dve.wait_ge(sem("kf_ready"), 2)
            dve.wait_ge(sem("in_x"), 16)

            def xrow(b, k):
                return xs[:, b, k] if isinstance(b, int) else xs[:, bass.ds(b, 1), k].rearrange("p a h -> p (a h)")

            def mult(row, u):
                n, par = row.b * 2 + u, row.par
                dve.wait_ge(sem("fwd_mm"), n + 1)
                if not row.first():
                    dve.wait_ge(sem("yf_ready"), 2 * n - 2)
                if not row.first(2):
                    dve.wait_ge(sem("inv_mm"), row.b - 1)
                re, im = fw[u]
                ks = slice(2 * u, 2 * u + 2)
                V.tensor_tensor(yf[par][:, 0, ks], re, kf[:, 0, ks], ALU.mult)
                V.tensor_tensor(tmp[u][:, 0], im, kf[:, 1, ks], ALU.mult)
                V.tensor_tensor(yf[par][:, 1, ks], re, kf[:, 1, ks], ALU.mult)
                V.tensor_tensor(tmp[u][:, 1], im, kf[:, 0, ks], ALU.mult).then_inc(sem("mult_done"), 1)

            def inverse(row, slot):
                dve.wait_ge(sem(f"sd{slot}"), row.b + 1)
                return V.reciprocal(rs[:, slot, 0:4], sd[:, slot, :])

            def split_low(e):
                dve.wait_ge(sem("w_high"), e + 1)
                V.tensor_tensor(ws[:, e, 1], w_raw[e][:, :], ws[:, e, 0].bitcast(F32), ALU.subtract).then_inc(sem("w_low"), 1)

            def choose(row):
                dve.wait_ge(sem("lt_mm"), row.b + 1)
                for k in range(4):
                    last = V.max(mx_all[:, row.b, k], tp[1][:, k * E:(k + 1) * E])
                do(last)
                for k in range(4):
                    last = V.max_index(mi[:, k], mx_all[:, row.b, k], tp[1][:, k * E:(k + 1) * E])
                do(last)
                do(V.tensor_copy(mif[:, :, :], mi[:, :, 0:2].rearrange("p t c -> p c t")))
                for c in range(2):
                    last = V.tensor_tensor(oh[:, c], iota8[:, 0].unsqueeze(1).to_broadcast([P, 4, E]),
                                           mif[:, c].unsqueeze(2).to_broadcast([P, 4, E]), ALU.is_equal)
                do(last)
                V.tensor_tensor(mask[:, :, :], oh[:, 0], oh[:, 1], ALU.add).then_inc(sem("mask_ready"), 1)

            def place(row):
                dve.wait_ge(sem("rank_mm"), row.b + 1)
                V.tensor_reduce(msum[:, :], mask[:, :, :].rearrange("p t e -> p e t"), AX.X, ALU.add)
                do(V.tensor_tensor(posf[:, :, :], tp[1][:, 64:96].rearrange("p (t e) -> p t e", t=4),
                                   iota8[:, 1].unsqueeze(1).to_broadcast([P, 4, E]), ALU.add))
                V.tensor_tensor(carry[:, :], carry[:, :], msum[:, :], ALU.add)
                for c in range(2):
                    last = V.tensor_tensor(prod[:, c], oh[:, c], posf[:, :, :], ALU.mult)
                do(last)
                V.tensor_copy(carry_b[:, :], carry[:, :]).then_inc(sem("carry_ready"), 1)
                do(V.tensor_reduce(posr[:, :, :], prod[:, :, :, :], AX.X, ALU.add))
                if not row.first(2):
                    dve.wait_ge(sem(f"scattered{row.par}"), 64 * (row.b - row.par))
                V.tensor_copy(pos_all[:, row.b], posr[:, :, :])
                V.tensor_copy(pos[row.par][:, :, :], posr[:, :, :]).then_inc(sem("pos_ready"), 1)

            def step(n):
                new, nxt, cur, mid, tail = (Row(n, k) for k in (2, 1, -1, -2, -LAG))
                if cur.live:
                    dve.wait_ge(sem("s_copied"), cur.b + 1)
                    c = iv[0].rearrange("p (j h) -> p j h", j=2)
                    V.tensor_tensor(r[:, 0:2], c, s_sb[:, :, :], ALU.add)
                    V.tensor_tensor(r[:, 2:4], c, s_sb[:, :, :], ALU.subtract).then_inc(sem("r_ready"), 1)
                    dve.wait_ge(sem("r_ready"), cur.b + 1)
                    stats(lambda k: r[:, k], 2)
                if new.live:
                    stats(lambda k: xs[:, new.b, k], 0)
                if nxt.live:
                    mult(nxt, 0)
                if cur.live:
                    do(inverse(cur, 2))
                    for k in range(4):
                        last = V.tensor_scalar(r[:, k], r[:, k], mv[2][:, k, 0:1], rs[:, 2, k:k + 1],
                                               ALU.subtract, ALU.mult)
                    last.then_inc(sem("o_norm"), 1)
                    dve.wait_ge(sem("o_norm"), cur.b + 1)
                    if not cur.first():
                        dve.wait_ge(sem("dl_ready"), cur.b)
                    do(V.tensor_tensor(o[:, :, :], r[:, :, :], lwb[:, 0].unsqueeze(1).to_broadcast([P, 4, H]),
                                       ALU.mult))
                    do(V.tensor_tensor(o[:, :, :], o[:, :, :], lwb[:, 1].unsqueeze(1).to_broadcast([P, 4, H]),
                                       ALU.add))
                    stats(lambda k: o[:, k], 1)
                if new.live:
                    do(inverse(new, 0))
                    if not new.first():
                        dve.wait_ge(sem("pm_ready"), 2 * new.b)
                    for k in range(4):
                        last = V.tensor_scalar(xn[:, k], xs[:, new.b, k], mv[0][:, k, 0:1], rs[:, 0, k:k + 1],
                                               ALU.subtract, ALU.mult)
                    last.then_inc(sem("xn_ready"), 1)
                if cur.live:
                    do(inverse(cur, 1))
                    V.scalar_tensor_tensor(rs[:, 1, 4:8], mv[1][:, :, 0], -1.0, rs[:, 1, 0:4], ALU.mult,
                                           ALU.mult).then_inc(sem("st_o"), 1)
                if nxt.live:
                    mult(nxt, 1)
                if mid.live:
                    dve.wait_ge(sem("x1_ready"), mid.b + 1)
                    stats(lambda k: xs[:, mid.b, k], 3)
                if 0 <= n < 5:
                    split_low(n)
                if mid.live:
                    if not mid.first():
                        dve.wait_ge(sem("zn_ready"), mid.b)
                    do(inverse(mid, 3))
                    V.tensor_copy(stat1[:, mid.b], mv[3][:, :, :].rearrange("p k c -> p c k"))
                    V.scalar_tensor_tensor(rs[:, 3, 4:8], mv[3][:, :, 0], -1.0, rs[:, 3, 0:4], ALU.mult,
                                           ALU.mult).then_inc(sem("st_x1"), 1)
                if tail.live:
                    choose(tail)
                    place(tail)

            steps(step)

            dve.wait_ge(sem("zn_ready"), B)
            dve.wait_ge(sem("cnt_mm"), 1)
            do(V.tensor_copy(cnt[:, 0], tp[1][:, 0:E]))
            V.tensor_scalar(cnt[:, 1], cnt[:, 0], 1.0 / P, (P - 1) / (2.0 * P), ALU.mult, ALU.add)
            V.memset(zpad[:, :, :], 0.0).then_inc(sem("c_done"), 1)
            dve.wait_ge(sem("c_done"), 1)
            dve.wait_ge(sem("in_e"), 48)
            do(V.tensor_scalar(cnt[:, 1], cnt[:, 1], ROUND, ROUND, ALU.add, ALU.subtract))
            do(V.tensor_tensor(padf[:, :], cnt[:, 0], iota8[:, 1], ALU.add))
            V.tensor_scalar(padi[:, :], padf[:, :], pcol[:, 0:1], None, ALU.add).then_inc(sem("zpad_set"), 1)
            do(V.tensor_tensor(tri[:, :, :], tri[:, :, :], cnt[:, 1].unsqueeze(1).to_broadcast([P, E, E]), ALU.mult))
            do(V.tensor_reduce(cnt[:, 2], tri[:, :, :], AX.X, ALU.add))
            NT = TILES + 1
            do(V.tensor_tensor(cmp_t[:, :, :], cnt[0:1, 2].unsqueeze(1).to_broadcast([1, NT, E]),
                               iot[0:1, 0].unsqueeze(2).to_broadcast([1, NT, E]), ALU.is_le))
            do(V.tensor_tensor(cmp_n[:, :, :], cmp_t[:, :, :], cnt[0:1, 1].unsqueeze(1).to_broadcast([1, NT, E]), ALU.mult))
            V.tensor_reduce(tf[:, 0], cmp_t[:, :, :], AX.X, ALU.add)
            do(V.tensor_reduce(tf[:, 1], cmp_n[:, :, :], AX.X, ALU.add))
            V.tensor_scalar(tab[:, 1], tf[:, 0], float(E - 1), None, ALU.min)
            do(V.scalar_tensor_tensor(tf[:, 2], tf[:, 0], float(REGION), iot[0:1, 1], ALU.mult, ALU.add))
            V.scalar_tensor_tensor(tab[:, 0], tf[:, 1], -float(P), tf[:, 2], ALU.mult, ALU.add).then_inc(sem("tab_ready"), 1)
            for e in range(5, E):
                split_low(e)
            V.memset(cnt[:, 3, 0:1], 0.0)
            V.tensor_scalar(cnt[:, 3, 1:E], cnt[:, 1, 0:E - 1], float(P), float(-REGION), ALU.mult, ALU.add)
            every = pos_all[:, :, :, :].rearrange("p b c k -> p (b c k)")
            do(V.tensor_tensor(y_cmp[:, :, :], every.unsqueeze(2).to_broadcast([P, 64, E]),
                               iota8[:, 1].unsqueeze(1).to_broadcast([P, 64, E]), ALU.is_ge))
            do(V.tensor_tensor(y_cmp[:, :, :], y_cmp[:, :, :], cnt[:, 3].unsqueeze(1).to_broadcast([P, 64, E]),
                               ALU.mult))
            do(V.tensor_reduce(y_shift[:, :], y_cmp[:, :, :], AX.X, ALU.add))
            do(V.tensor_tensor(every, every, y_shift[:, :], ALU.add))
            V.tensor_tensor(wsm[:, :, :, :], mx_all[:, :, :, :], mx_all[:, :, :, 0:1].to_broadcast([P, B, 4, E]),
                            ALU.subtract).then_inc(sem("wsm_sub"), 1)
            dve.wait_ge(sem("rsm_sd"), 1)
            do(V.reciprocal(rsm[:, 0], rsm[:, 0]))
            do(V.scalar_tensor_tensor(rsm[:, 1], stat1[:, :, 0, :], -1.0, rsm[:, 0], ALU.mult, ALU.mult))
            dve.wait_ge(sem("wsm_exp"), 1)
            do(V.tensor_reduce(rsm[:, 2], wsm[:, :, :, :], AX.X, ALU.add))
            do(V.reciprocal(rsm[:, 3], rsm[:, 2]))
            for c in range(2):
                last = V.tensor_tensor(wgt[:, c], wsm[:, :, :, c], rsm[:, 3], ALU.mult)
            do(last)
            do(V.tensor_tensor(wgt[:, 2], wgt[:, 0], wgt[:, 1], ALU.add))
            do(V.tensor_scalar(wgt[:, 2], wgt[:, 2], 1e-8, None, ALU.max))
            do(V.reciprocal(wgt[:, 3], wgt[:, 2]))
            for c in range(2):
                last = V.tensor_tensor(wgt[:, c], wgt[:, c], wgt[:, 3], ALU.mult)
            last.then_inc(sem("rsm_ready"), 1)
            dve.wait_ge(sem("rsm_ready"), 1)

            dve.wait_ge(sem("in_b"), 32 * E)

            def part(i, par):
                t, q = i + 2, par
                if live(t):
                    dve.wait_ge(sem("zf_ready"), t + 1)
                    if not early(t, 2):
                        dve.wait_ge(sem("l1_mm"), t - 1)
                    V.tensor_copy(z_hl[q][:, 0], z_f[:, :, :]).then_inc(sem("z_high"), 1)
                    dve.wait_ge(sem("z_high"), t + 1)
                    V.tensor_tensor(z_hl[q][:, 1], z_f[:, :, :], z_hl[q][:, 0].bitcast(F32),
                                    ALU.subtract).then_inc(sem("z_split"), 1)
                t, q = i + 1, 1 - par
                if live(t):
                    e = dve.value_load(tab[0:1, 1, bass.ds(t, 1)], min_val=0, max_val=E - 1)
                    dve.wait_ge(sem("l1_mm"), t + 1)
                    if not early(t):
                        dve.wait_ge(sem("hg_ready"), t)
                    V.tensor_tensor(hb[:, :], ps_h[q], b1r[:, bass.ds(e, 1)].rearrange("p a f -> p (a f)"),
                                    ALU.add).then_inc(sem("hb_ready"), 1)
                t, q = i, par
                if live(t):
                    dve.wait_ge(sem("h_high"), t + 1)
                    V.tensor_tensor(h_hl[q][:, 1], ps_t[q], h_hl[q][:, 0].bitcast(F32),
                                    ALU.subtract).then_inc(sem("h_split"), 1)
                t, q = i - 1, 1 - par
                if live(t):
                    e = dve.value_load(tab[0:1, 1, bass.ds(t, 1)], min_val=0, max_val=E - 1)
                    dve.wait_ge(sem("l2_mm"), t + 1)
                    if not early(t, 2):
                        dve.wait_ge(sem(f"y_out{q}"), (t - q) * 8)
                    V.tensor_tensor(y_sb[q][:, :], ps_y[q], b2r[:, bass.ds(e, 1)].rearrange("p a f -> p (a f)"),
                                    ALU.add).then_inc(sem("y_ready"), 1)

            tiles(dve, part)

            def mix(b, par):
                dve.wait_ge(sem(f"gathered{par}"), (b - par) * 64 + 128)
                dve.wait_ge(sem("m_base"), b + 1)
                for c in range(2):
                    for k in range(4):
                        last = V.scalar_tensor_tensor(acc[par][:, k], ya[par][:, c, k], wgt[:, c, bass.ds(b, 1), k],
                                                      acc[par][:, k], ALU.mult, ALU.add)
                    last.then_inc(sem("m_mixed"), 1)
                    dve.wait_ge(sem("m_mixed"), b * 2 + c + 1)
                for k in range(4):
                    last = V.bn_stats(st[:, par, k, :], acc[par][:, k])
                last.then_inc(sem("m_stat"), 1)
                dve.wait_ge(sem("m_stat"), b + 1)
                gate(dve)
                for k in range(4):
                    last = V.bn_aggr(mvm[par][:, k, :], st[:, par, k, :])
                last.then_inc(sem("m_var"), 1)

            def scale(b, par):
                dve.wait_ge(sem("m_sd"), b + 1)
                V.reciprocal(rm[:, par, 1, :], rm[:, par, 0, :]).then_inc(sem("m_inv"), 1)
                dve.wait_ge(sem("m_inv"), b + 1)
                V.scalar_tensor_tensor(rm[:, par, 2, :], mvm[par][:, :, 0], -1.0, rm[:, par, 1, :], ALU.mult,
                                       ALU.mult).then_inc(sem("m_rs"), 1)

            def add(b, par):
                dve.wait_ge(sem("m_fin"), b + 1)
                V.tensor_tensor(fin[par][:, :, :], fin[par][:, :, :], x1s[par][:, :, :], ALU.add).then_inc(sem("m_out"), 1)

            mix(0, 0)
            scale(0, 0)
            with dve.Fori(0, B // 2 - 1) as j:
                mix(j * 2 + 1, 1)
                add(j * 2, 0)
                scale(j * 2 + 1, 1)
                mix(j * 2 + 2, 0)
                add(j * 2 + 1, 1)
                scale(j * 2 + 2, 0)
            mix(B - 1, 1)
            add(B - 2, 0)
            scale(B - 1, 1)
            add(B - 1, 1)

        @block.gpsimd
        def _(pool):
            G = nc.gpsimd
            G0, G1 = QN, QN + PN
            pool.wait_ge(sem("k_qt"), 1)
            for ht in range(2):
                if ht:
                    pool.wait_ge(sem("k_factors"), ht)
                G.tensor_tensor(mag[:, :, :], qt[:, 1, ht * P:ht * P + P].unsqueeze(1).to_broadcast([P, G1, P]),
                                sc[:, 0:G1].unsqueeze(2).to_broadcast([P, G1, P]), ALU.mult).then_inc(sem("k_aq"), 1)
                pool.wait_ge(sem("k_round"), ht + 1)
                G.tensor_tensor(v[:, G0:SLOTS], v[:, G0:SLOTS], kr[:, G0:SLOTS],
                                ALU.subtract).then_inc(sem("k_turns"), 1)
                pool.wait_ge(sem("k_sin"), ht + 1)
                G.tensor_tensor(kr[:, G1:SLOTS], kr[:, G1:SLOTS],
                                qt[:, 3, ht * P:ht * P + P].unsqueeze(1).to_broadcast([P, PN, P]),
                                ALU.mult).then_inc(sem("k_g2"), 1)

            def combine(row, u):
                n, par = row.b * 2 + u, row.par
                pool.wait_ge(sem("mult_done"), n + 1)
                ks = slice(2 * u, 2 * u + 2)
                G.tensor_tensor(yf[par][:, 0, ks], yf[par][:, 0, ks], tmp[u][:, 0],
                                ALU.subtract).then_inc(sem("yf_ready"), 1)
                G.tensor_tensor(yf[par][:, 1, ks], yf[par][:, 1, ks], tmp[u][:, 1],
                                ALU.add).then_inc(sem("yf_ready"), 1)

            def step(n):
                new, nxt, cur, tail = (Row(n, k) for k in (2, 1, -1, -LAG))
                if nxt.live:
                    combine(nxt, 0)
                if new.live:
                    pool.wait_ge(sem("xn_ready"), new.b + 1)
                    if not new.first(2):
                        pool.wait_ge(sem("fwd_mm"), 2 * (new.b - 1))
                    G.tensor_tensor(pm[new.par][:, 0], xn[:, 0:2], xn[:, 2:4], ALU.add).then_inc(sem("pm_ready"), 1)
                    G.tensor_tensor(pm[new.par][:, 1], xn[:, 0:2], xn[:, 2:4], ALU.subtract).then_inc(sem("pm_ready"), 1)
                if nxt.live:
                    combine(nxt, 1)
                if cur.live:
                    pool.wait_ge(sem("dl_ready"), cur.b + 1)
                    G.tensor_tensor(xs[:, cur.b], xs[:, cur.b], dl[:, :, :], ALU.add).then_inc(sem("x1_ready"), 1)
                if tail.live:
                    pool.wait_ge(sem("pos_ready"), tail.b + 1)
                    pool.wait_ge(sem("zn_ready"), tail.b + 1)
                    for c in range(2):
                        for k in range(4):
                            pool.indirect_dma_start(
                                z_rows, bass.IndirectOffsetOnAxis(ap=pos[tail.par][:, c, k:k + 1], axis=0),
                                zn[tail.par][:, k], None).then_inc(sem(f"scattered{tail.par}"), 16)

            steps(step)
            for par in range(2):
                pool.wait_ge(sem(f"scattered{par}"), 64 * B)
            pool.wait_ge(sem("zpad_set"), 1)
            for e in range(E):
                pool.indirect_dma_start(z_rows, bass.IndirectOffsetOnAxis(ap=padi[:, e:e + 1], axis=0),
                                        zpad[:, e], None).then_inc(sem("pads"), 16)
            pool.wait_ge(sem("tab_ready"), 1)

            def store(t, q):
                pool.wait_ge(sem("y_ready"), t + 1)
                pool.dma_start(y_rows[bass.ds(t * P, P), :], y_sb[q][:, :]).then_inc(sem(f"y_out{q}"), 16)

            with pool.Fori(0, (TILES - 1) // 2) as j:
                store(j * 2, 0)
                store(j * 2 + 1, 1)
            store(TILES - 1, 0)
            pool.wait_ge(sem("rsm_ready"), 1)
            pool.wait_ge(sem("y_out0"), 16 * ((TILES + 1) // 2))
            pool.wait_ge(sem("y_out1"), 16 * (TILES // 2))

            def gather(b, par):
                if not early(b, 2):
                    pool.wait_ge(sem(f"gathered{par}"), (b - par) * 64)
                G.tensor_copy(pos[par][:, :, :], pos_all[:, bass.ds(b, 1)].rearrange("p a c k -> p (a c) k")).then_inc(sem("m_pos"), 1)
                pool.wait_ge(sem("m_pos"), b + 1)
                if not early(b, 2):
                    pool.wait_ge(sem("m_var"), b - 1)
                gate(pool)
                for c in range(2):
                    for k in range(4):
                        pool.indirect_dma_start(ya[par][:, c, k], None, y_rows,
                                                bass.IndirectOffsetOnAxis(ap=pos[par][:, c, k:k + 1], axis=0)
                                                ).then_inc(sem(f"gathered{par}"), 16)

            gather(0, 0)
            gather(1, 1)
            with pool.Fori(0, B // 2 - 1) as j:
                gather(j * 2 + 2, 0)
                gather(j * 2 + 3, 1)

        @block.tensor
        def _(pe):
            TE = nc.tensor
            pe.wait_ge(sem("k_quant"), 1)
            for q in range(4):
                for ht in range(2):
                    last = TE.transpose(bank(0, 2)[:, q * H + ht * P:q * H + ht * P + P],
                                        quant[:, q, ht].rearrange("p d n -> p (d n)"), ident[:, :])
            last.then_inc(sem("k_tr"), 1)
            for ht in range(2):
                pe.wait_ge(sem("k_factors"), ht + 1)
                for hh in range(P):
                    j, i = 2 * ht + hh // 64, hh % 64
                    last = TE.matmul(psum[32 * j:32 * j + PN, 2048 + i * QN:2048 + (i + 1) * QN],
                                     v[:, QN:QN + PN, hh], v[:, 0:QN, hh], start=True, stop=True)
                last.then_inc(sem("k_mm"), 1)
            for ht in range(2):
                pe.wait_ge(sem(f"k_in{ht}"), 32)
                for l in range(KT):
                    last = TE.transpose(bank(0, 2)[:, l * H + ht * P:l * H + ht * P + P], kh[:, ht, l * P:(l + 1) * P],
                                        ident[:, :])
            last.then_inc(sem("kt_mm"), 1)
            pe.wait_ge(sem("kt_evac"), 1)
            pe.wait_ge(sem("in_lag"), 16)
            pe.wait_ge(sem("k_evac"), 4)
            for g in range(2 * KT):
                for l in range(KT):
                    last = TE.matmul(bank(2, 4)[:, g * H:(g + 1) * H], lag[:, l, g, :], k_t[:, l, :],
                                     start=l == 0, stop=l == KT - 1)
            last.then_inc(sem("kf_mm"), 1)
            pe.wait_ge(sem("in_tab"), 32)
            pe.wait_ge(sem("kf_ready"), 2)

            def fwd(row, u):
                n = row.b * 2 + u
                pe.wait_ge(sem("pm_ready"), 2 * row.b + 2)
                if not row.first():
                    pe.wait_ge(sem("mult_done"), n - 1)
                for c in range(2):
                    for k in range(2):
                        kt = 2 * u + k
                        for t in range(2):
                            last = TE.matmul(fw[u][c][:, k], ft[:, c, t, kt * P:(kt + 1) * P], pm[row.par][:, c, t],
                                             start=t == 0, stop=t == 1)
                last.then_inc(sem("fwd_mm"), 1)

            def inverse(row, j):
                pe.wait_ge(sem("yf_ready"), 4 * row.b + 4)
                if not row.first():
                    pe.wait_ge(sem("r_ready"), row.b)
                for c in range(2):
                    for k in range(KT):
                        last = TE.matmul(iv[c][:, j * H:(j + 1) * H], it[:, c, k, j * P:(j + 1) * P],
                                         yf[row.par][:, c, k], start=k == 0, stop=k == KT - 1)
                if j == 1:
                    last.then_inc(sem("inv_mm"), 1)

            def step(n):
                nxt, cur, tail = Row(n, 1), Row(n, 0), Row(n, -LAG)
                if nxt.live:
                    fwd(nxt, 0)
                if tail.live:
                    pe.wait_ge(sem("zn_ready"), tail.b + 1)
                    if not tail.first():
                        pe.wait_ge(sem("pos_ready"), tail.b)
                    for k in range(2):
                        for q in range(4):
                            last = TE.transpose(tp[k][:, q * P:(q + 1) * P], zn[tail.par][:, q, k * P:(k + 1) * P], ident[:, :])
                    last.then_inc(sem("zt_mm"), 1)
                if nxt.live:
                    fwd(nxt, 1)
                if tail.live:
                    pe.wait_ge(sem("zt_ready"), 2 * tail.b + 2)
                    for k in range(2):
                        last = TE.matmul(tp[0][0:E, :], rw_sb[:, k, :], zt[:, k, :], start=k == 0, stop=k == 1)
                    last.then_inc(sem("lg_mm"), 1)
                if cur.live:
                    inverse(cur, 0)
                if tail.live:
                    pe.wait_ge(sem("lg_ready"), tail.b + 1)
                    for q in range(4):
                        last = TE.transpose(tp[1][:, q * E:(q + 1) * E], lg[:, q * P:(q + 1) * P], ident[0:E, 0:E])
                    last.then_inc(sem("lt_mm"), 1)
                if cur.live:
                    inverse(cur, 1)
                if tail.live:
                    pe.wait_ge(sem("mask_ready"), tail.b + 1)
                    rank = tp[1][:, 64:96]
                    m = mask[:, :, :].rearrange("p t e -> p (t e)")
                    TE.matmul(rank, upper[:, 0, :], m, start=True, stop=False)
                    for q in range(1, 4):
                        TE.matmul(rank[:, q * E:4 * E], upper[:, 1, :], m[:, 0:(4 - q) * E], start=False, stop=False)
                    if not tail.first():
                        pe.wait_ge(sem("carry_ready"), tail.b)
                    TE.matmul(rank.rearrange("p (t e) -> p t e", t=4), upper[:, 1, :],
                              carry_b[:, :].unsqueeze(1).to_broadcast([P, 4, E]), start=False,
                              stop=True).then_inc(sem("rank_mm"), 1)

            steps(step)
            pe.wait_ge(sem("pos_ready"), B)
            pe.wait_ge(sem("carry_ready"), B)
            TE.matmul(tp[1][:, 0:E], upper[:, 1, :], carry_b[:, :], start=True, stop=True).then_inc(sem("cnt_mm"), 1)

            def part(i, par):
                t, q = i + 2, par
                if live(t):
                    pe.wait_ge(sem(f"z_in{q}"), (t - q) * 8 + 16)
                    if not early(t, 2):
                        pe.wait_ge(sem("zf_ready"), t - 1)
                    for k in range(2):
                        last = TE.transpose(ps_z[q][:, k], z_in[q][:, k * P:(k + 1) * P], ident[:, :])
                    last.then_inc(sem("tz_mm"), 1)
                t, q = i + 1, 1 - par
                if live(t):
                    e = pe.value_load(tab[0:1, 1, bass.ds(t, 1)], min_val=0, max_val=E - 1)
                    pe.wait_ge(sem("z_split"), t + 1)
                    if not early(t, 2):
                        pe.wait_ge(sem("hb_ready"), t - 1)
                    n = 0
                    for k in range(2):
                        for a, c in ((0, 0), (0, 1), (1, 0)):
                            last = TE.matmul(ps_h[q], z_hl[q][:, a, k], w_at(e, c, k * F, F), start=n == 0, stop=n == 5)
                            n += 1
                    last.then_inc(sem("l1_mm"), 1)
                t, q = i, par
                if live(t):
                    pe.wait_ge(sem("hg_ready"), t + 1)
                    if not early(t, 2):
                        pe.wait_ge(sem("h_split"), t - 1)
                    for k in range(4):
                        last = TE.transpose(ps_t[q][:, k], hg[q][:, k * P:(k + 1) * P], ident[:, :])
                    last.then_inc(sem("th_mm"), 1)
                t, q = i - 1, 1 - par
                if live(t):
                    e = pe.value_load(tab[0:1, 1, bass.ds(t, 1)], min_val=0, max_val=E - 1)
                    pe.wait_ge(sem("h_split"), t + 1)
                    if not early(t, 2):
                        pe.wait_ge(sem("y_ready"), t - 1)
                    n = 0
                    for k in range(4):
                        for a, c in ((0, 0), (0, 1), (1, 0)):
                            last = TE.matmul(ps_y[q], h_hl[q][:, a, k], w_at(e, c, 1024 + k * H, H), start=n == 0, stop=n == 11)
                            n += 1
                    last.then_inc(sem("l2_mm"), 1)

            pe.wait_ge(sem("tab_ready"), 1)
            pe.wait_ge(sem("w_low"), E)
            tiles(pe, part)


USES = ("xn_ready", "st_o", "o_norm", "st_x1")


def consts():
    import numpy as np
    t = np.arange(T // 2)
    k = np.arange(T)
    ang = np.pi / 2048 * (((2 * k[None, :] + 1) * (2 * t[:, None] - 511)) % 4096)
    f = np.stack([np.cos(ang), -np.sin(ang)])
    fwd = f.reshape(2, 2, P, T).transpose(2, 0, 1, 3)
    inv = (f / T).transpose(0, 2, 1).reshape(2, KT, P, T // 2).transpose(2, 0, 1, 3)
    l = np.arange(T)
    a2 = np.pi / 1024 * (((2 * k[None, :] + 1) * l[:, None]) % 2048)
    g = np.stack([np.cos(a2), -np.sin(a2)])
    lag = g.reshape(2, KT, P, KT, P).transpose(2, 1, 0, 3, 4).reshape(P, KT, 2 * KT, P)
    s = np.concatenate([np.arange(QN), QN * np.arange(PN), QN * np.arange(PN)])
    scale = np.broadcast_to(s, (P, SLOTS))
    off = np.zeros((P, SLOTS))
    off[:N, :QN], off[N:, :QN] = .25, 0
    off[:N, QN:QN + PN], off[N:, QN:QN + PN] = .25, .5
    off[:N, QN + PN:], off[N:, QN + PN:] = .5, .75
    up = np.stack([np.triu(np.ones((P, P)), 1), np.ones((P, P))], 1)
    nt = TILES + 1
    tile = np.concatenate([np.tile(np.concatenate([np.tril(np.ones((E, E))).ravel(), np.arange(nt), P * np.arange(nt)]),
                                   (P, 1)), np.arange(P)[:, None]], 1)
    return [np.ascontiguousarray(a, dtype=np.float32) for a in (fwd, inv, lag, scale, off, np.eye(P), up, tile)]


_INS = ["log_A_real", "A_imag", "C_re", "C_im", "log_dt", "D", "ln_w", "ln_b"]
_FFN = ["ln_g", "ln_b", "rW", "rb", "W1", "b1", "W2", "b2"]


def kernel(**inputs):
    import numpy as np
    import concourse.bacc as bacc
    from concourse.bass_utils import run_bass_kernel_spmd

    x = np.asarray(inputs["L0_attn_x"])
    half = [x[:, :T // 2], x[:, :T // 2 - 1:-1]]
    x = np.concatenate([a.reshape(B, 2, P, H) for a in half], 1).transpose(2, 0, 1, 3)
    arrays = [x, *consts()]
    arrays += [inputs[f"L0_attn_{n}"] for n in _INS] + [inputs[f"L0_ffn_{n}"] for n in _FFN]
    nc = bacc.Bacc("TRN2", target_bir_lowering=False, num_devices=1)
    given, args = {}, []
    for i, a in enumerate(arrays):
        name = f"in_{i}_dram"
        given[name] = np.ascontiguousarray(a)
        args.append(nc.dram_tensor(name, given[name].shape, mybir.dt.from_np(given[name].dtype), kind="ExternalInput").ap())
    out = nc.dram_tensor("out_dram", (P, B, 4, H), F32, kind="ExternalOutput").ap()
    program(nc, *args, out)
    r = run_bass_kernel_spmd(nc, [given], core_ids=[0])
    y = r.results[0]["out_dram"].transpose(1, 2, 0, 3)
    return np.concatenate([y[:, :2].reshape(B, T // 2, H), y[:, 2:].reshape(B, T // 2, H)[:, ::-1]], 1)
```

```python
import concourse.bass as bass
from concourse import mybir
from concourse.alu_op_type import AluOpType as ALU

F32 = mybir.dt.float32
F32R = mybir.dt.float32r
BF16 = mybir.dt.bfloat16
I32 = mybir.dt.int32
U32 = mybir.dt.uint32
ACT = mybir.ActivationFunctionType
AX = mybir.AxisListType

P = 128
B, T, H, N = 8, 512, 256, 64
E, F = 8, 512
EPS = 1e-5
KT = T // P
QN, PN = 32, 16
SLOTS = QN + 2 * PN
REGION = B * T + P
LAG = 3
TILES = 2 * B * T // P + E - 1
ROWS = E * REGION
ROUND = 12582912.0
TURN = 6.283185
W = H + 2
TRASH = 2 * B * T
UNROLL = 6
KB = 1024
BASE = 16512


class Seq:

    def __init__(self, eng, sem):
        self.eng, self.sem, self.n = eng, sem, 0

    def inc(self, ins):
        ins.then_inc(self.sem, 1)
        self.n += 1

    def wait(self):
        self.eng.wait_ge(self.sem, self.n)


TAB = E * E + 2 * (TILES + 1)


def program(nc, x, fwd_tab, inv_tab, lag_tab, slot_scale, slot_off, ident_in, upper_in, tile_tab, lar, aim, cre, cim,
            ldt, d_skip, ln_w, ln_b, ffn_g, ffn_b, r_w, r_b, w1, b1, w2, b2, out, dbg=None):
    sems = {}

    def sem(name):
        if name not in sems:
            sems[name] = nc.alloc_semaphore(name)
        return sems[name]

    def at(name, shape, dt, off):
        return nc.alloc_sbuf_tensor_at(name, shape, dt, offset=BASE + off)

    v = at("v", [P, SLOTS, H], F32, 0)
    mag = at("mag", [P, QN + PN, H], F32, 64 * KB)
    xs = [at(f"xs{b}", [P, 4, H], F32, k * KB) for b, k in enumerate((88, 92, 80, 84, 96, 100, 112, 116))]
    kf = at("kf", [P, 2, KT, H], F32, 104 * KB)
    zn = [at(f"zn{i}", [P, 4, W], F32, 120 * KB + 4 * i * 4 * W) for i in range(2)]
    o0 = 128 * KB + 64
    zn += [at(f"zn{i}", [P, 4, W], F32, o0 + 4 * (i - 2) * 4 * W) for i in (2, 3)]
    xn = at("xn", [P, 4, H], F32, o0)
    pm = [at(f"pm{i}", [P, 2, 2, H], F32, o0 + (4 + 4 * i) * KB) for i in range(2)]
    ft = at("ft", [P, 2, 2, T], F32, o0 + 12 * KB)
    it = at("it", [P, 2, KT, 2 * P], F32, o0 + 20 * KB)
    yf = [at(f"yf{i}", [P, 2, KT, H], F32, o0 + (28 + 8 * i) * KB) for i in range(2)]
    lag = at("lag", [P, KT, 2 * KT, P], F32, o0 + 28 * KB)
    tmp = [at(f"tmp{i}", [P, 2, 2, H], F32, o0 + (44 + 4 * i) * KB) for i in range(2)]
    s_sb = at("s_sb", [P, 2, H], F32, o0 + 52 * KB)
    r = at("r", [P, 4, H], F32, o0 + 54 * KB)
    o = at("o", [P, 4, H], F32, o0 + 58 * KB)
    dl = at("dl", [P, 4, H], F32, o0 + 62 * KB)
    zt = at("zt", [P, 2, T], F32, o0 + 66 * KB)
    lwb = at("lwb", [P, 2, H], F32, o0 + 70 * KB)
    k_sb = at("k_sb", [P, 64 * QN], F32, o0 + 44 * KB)
    kh = at("kh", [P, 2, T], F32, o0 + 54 * KB)
    k_t = at("k_t", [P, KT, H], F32, o0 + 58 * KB)
    sm = at("sm", [P, 8, 2, N], F32, o0 + 62 * KB)
    quant = at("quant", [P, 4, 2, 2, N], F32, o0 + 66 * KB)
    sm2 = at("sm2", [P, 14, 2, N], F32, 112 * KB)
    kr = [at(f"kr{i}", [P, PN, H], F32, k) for i, k in enumerate((112 * KB, o0 + 12 * KB))]
    qt = at("qt", [P, 4, H], F32, o0 + 0 * KB)
    raw = at("raw", [P, 4, 2, N], F32, o0 + 4 * KB)
    c0 = o0 + 73 * KB
    ident = at("ident", [P, P], F32, c0)
    upper = at("upper", [P, 2, P], BF16, c0 + 512)
    upper_f = at("upper_f", [P, 2, P], F32, o0 + 58 * KB)
    sc = at("sc", [P, SLOTS], F32, c0 + 1024)
    so = at("so", [P, SLOTS], F32, c0 + 1280)
    dtv = at("dtv", [P, 2, 2], F32, c0 + 1536)
    st = at("st", [P, 4, 4, 6], F32, c0 + 5568)
    mv = [at(f"mv{i}", [P, 4, 2], F32, c0 + 1664 + 32 * i) for i in range(4)]
    sd = at("sd", [P, 4, 4], F32, c0 + 1792)
    eps = at("eps", [P, 2], F32, c0 + 1856)
    rs = at("rs", [P, 4, 8], F32, c0 + 1920)
    gb = at("gb", [P, 2, 2], F32, c0 + 2048)
    rw_sb = at("rw_sb", [P, 2, E], F32, c0 + 2080)
    rb_sb = at("rb_sb", [P, E], F32, c0 + 2144)
    mx = at("mx", [P, 4, 8], F32, c0 + 2176)
    mi = at("mi", [P, 4, 8], U32, c0 + 2304)
    mif = at("mif", [P, 2, 4], F32, c0 + 2432)
    oh = at("oh", [P, 2, 4, E], F32, c0 + 2464)
    mask = at("mask", [P, 4, E], BF16, c0 + 2720)
    msum = at("msum", [P, E], F32, c0 + 2784)
    carry = at("carry", [P, E], F32, c0 + 2816)
    carry_b = at("carry_b", [P, E], BF16, c0 + 2848)
    posf = at("posf", [P, 4, E], F32, c0 + 2880)
    prod = at("prod", [P, 2, 4, E], F32, c0 + 3008)
    posr = at("posr", [P, 2, 4], F32, c0 + 3264)
    pos = [at(f"pos{i}", [P, 2, 4], U32, c0 + 3296 + 32 * i) for i in range(2)]
    iota8 = at("iota8", [P, 2, E], F32, c0 + 3360)
    lgs = at("lgs", [P, 4, E], F32, c0 + 3424)
    tok = at("tok", [P, B, 4], F32, c0 + 3552)
    stat1 = at("stat1", [P, B, 2, 4], F32, c0 + 3680)
    mx_all = at("mx_all", [P, B, 4, E], F32, c0 + 3936)
    tab = at("tab", [1, 2, TILES + 1], I32, c0 + 4960)
    d_rep = at("d_rep", [P, H], F32, o0 + 72 * KB)
    tab_e = at("tab_e", [P, TILES + 1], F32, c0 + 5952)
    dest = at("dest", [P, TILES + 1], U32, c0 + 6240)
    dst = [at(f"dst{i}", [P, 1], U32, c0 + 6528 + 32 * i) for i in range(2)]
    flag = at("flag", [P, 1], F32, c0 + 6592)
    ws = at("ws", [P, E, 2, 2048], F32R, 0)
    w_raw = [at(f"w_raw{e}", [P, 2048], F32, (16 * e + 8) * KB) for e in range(E)]
    x1m = at("x1m", [P, B, 4, H], F32, 112 * KB + 64)
    b2r = at("b2r", [P, E, H], F32, o0 + 16 * KB)
    z_in = [at(f"z_in{i}", [P, W], F32, o0 + 24 * KB + 1056 * i) for i in range(2)]
    z_f = at("z_f", [P, 2, P], F32, o0 + 27 * KB)
    b1r = at("b1r", [P, E, F], F32, o0 + 28 * KB)
    y_sb = [at(f"y_sb{i}", [P, H], F32, o0 + (44 + i) * KB) for i in range(2)]
    hb = at("hb", [P, F], F32, o0 + 46 * KB)
    z_hl = [at(f"z_hl{i}", [P, 2, 2, P], F32R, o0 + (53 + 2 * i) * KB) for i in range(2)]
    hg = [at(f"hg{i}", [P, F], F32, o0 + (57 + 2 * i) * KB) for i in range(2)]
    h_hl = [at(f"h_hl{i}", [P, 2, 4, P], F32R, o0 + (61 + 4 * i) * KB) for i in range(2)]
    m0 = o0 + 48 * KB
    cnt = at("cnt", [P, 8, E], F32, m0)
    tri = at("tri", [P, E, E], F32, m0 + 256)
    padi = at("padi", [1, E], I32, m0 + 512)
    padf = at("padf", [1, E], F32, m0 + 544)
    rm = at("rm", [P, 2, 4, 4], F32, m0 + 576)
    mvm = [at(f"mvm{i}", [P, 4, 2], F32, m0 + 704 + 32 * i) for i in range(2)]
    wsm = at("wsm", [P, B, 4, E], F32, m0 + KB)
    wgt = at("wgt", [P, 4, B, 4], F32, m0 + 2 * KB)
    rsm = at("rsm", [P, 4, B, 4], F32, m0 + 2 * KB + 512)
    zpad = at("zpad", [P, W], F32, m0 + 3 * KB)
    cmp_t = at("cmp_t", [P, TILES + 1, E], F32, o0 + 57 * KB)
    cmp_n = at("cmp_n", [P, TILES + 1, E], F32, o0 + 60 * KB)
    tf = at("tf", [P, 3, TILES + 1], F32, o0 + 63 * KB)
    iot = at("iot", [P, 2, TILES + 1], F32, o0 + 65 * KB)
    ya = at("ya", [P, B, 2, 4, H], F32, 0)
    acc = at("acc", [P, B, 4, H], F32, 64 * KB)
    psum = nc.alloc_psum_tensor("psum", [P, 8 * 512], F32)

    def bank(n, w=1):
        return psum[:, 512 * n:512 * (n + w)]

    fw = [[bank(2 * i + c).rearrange("p (k h) -> p k h", k=2) for c in range(2)] for i in range(2)]
    iv = [bank(4 + c) for c in range(2)]
    tp = [bank(6), bank(7)]
    tp_last = [bank(0), bank(1)]

    ps_z = [bank(7 * i)[:, 0:256].rearrange("p (k t) -> p k t", k=2) for i in range(2)]
    ps_h = [bank(1 + i) for i in range(2)]
    ps_t = [bank(3 + i).rearrange("p (k t) -> p k t", k=4) for i in range(2)]
    ps_y = [bank(5 + i)[:, 0:H] for i in range(2)]

    def w_at(e, c, at_, n):
        return ws[:, bass.ds(e, 1), c, at_:at_ + n].rearrange("p a n -> p (a n)")

    k_dram = nc.dram_tensor("k_dram", [4, PN, 64 * QN], F32, kind="Internal").ap()
    z_rows = nc.dram_tensor("z_rows", [ROWS, W], F32, kind="Internal").ap()
    y_rows = nc.dram_tensor("y_rows", [TRASH + P, H], F32, kind="Internal").ap()
    x1_dram = nc.dram_tensor("x1_dram", [P, B, 4, H], F32, kind="Internal").ap()

    def rep(a, parts=P):
        return bass.AP(a.tensor, a.offset, [[0, parts]] + [list(q) for q in a.ap])

    def hn(a):
        return a.rearrange("(t p) n -> p t n", p=P)

    def steps(step):
        for n in range(-1, B + LAG):
            step(n)

    def gate(eng):
        eng.sem_inc(sem(f"gate_{eng.engine.name}"), 1)

    class Row:

        def __init__(self, n, k):
            self.b, self.live, self.par = n + k, 0 <= n + k < B, (n + k) % 2

        def first(self, n=1):
            return self.b < n

    loaded = {}

    def tiles(eng, part):
        loaded[eng.engine.name] = {}
        for i in range(-2, 3):
            part(i, i % 2, i)
        with eng.Fori(0, (TILES - 5) // UNROLL) as j:
            loaded[eng.engine.name] = {}
            for u in range(UNROLL):
                part(j * UNROLL + (3 + u), (1 + u) % 2, u)
        loaded[eng.engine.name] = {}
        for i in range(TILES - 2, TILES + 1):
            part(i, i % 2, i)

    def load_expert(eng, e):
        eng.dma_start(w_raw[e][:, 0:1024].rearrange("p (k f) -> p k f", k=2),
                      w1[e].rearrange("(k p) f -> p k f", p=P)).then_inc(sem(f"in_w{e}"), 16)
        eng.dma_start(w_raw[e][:, 1024:2048].rearrange("p (k f) -> p k f", k=4),
                      w2[e].rearrange("(k p) f -> p k f", p=P)).then_inc(sem(f"in_w{e}"), 16)

    def back(n):
        return n * -1 + (B - 1)

    def route(b):
        return tp_last if b == B - 1 else tp

    def buf(b):
        return b % 2 if b < 6 else b - 4

    def live(t):
        return not isinstance(t, int) or 0 <= t < TILES

    def expert(eng, t, u):
        if u not in loaded[eng.engine.name]:
            loaded[eng.engine.name][u] = eng.value_load(tab[0:1, 1, bass.ds(t, 1)], min_val=0, max_val=E - 1)
        return loaded[eng.engine.name][u]

    def early(t, n=1):
        return isinstance(t, int) and t < n

    with nc.Block() as block:

        @block.sync
        def _(sp):
            sp.dma_start(dtv[:, 0, :], ldt.rearrange("(t p) -> p t", p=P),
                         allow_slow_non_contiguous=True).then_inc(sem("in_modes"), 16)
            sp.dma_start(raw[:, 0], hn(lar)).then_inc(sem("in_modes"), 16)
            sp.dma_start(raw[:, 1], hn(aim)).then_inc(sem("in_modes"), 16)
            sp.dma_start(ident[:, :], ident_in).then_inc(sem("in_modes"), 16)
            sp.dma_start(so[:, :], slot_off).then_inc(sem("in_slots"), 16)
            sp.dma_start(sc[:, :], slot_scale).then_inc(sem("in_slots"), 16)
            sp.dma_start(raw[:, 2], hn(cre)).then_inc(sem("in_coef"), 16)
            sp.dma_start(raw[:, 3], hn(cim)).then_inc(sem("in_coef"), 16)
            sp.dma_start(upper_f[:, :, :], upper_in).then_inc(sem("in_upper"), 16)
            sp.dma_start(lag[:, :, :, :], lag_tab).then_inc(sem("in_lag"), 16)
            sp.dma_start(d_rep[:, :], rep(d_skip)).then_inc(sem("in_small"), 16)
            sp.dma_start(lwb[:, 0, :], rep(ln_w)).then_inc(sem("in_small"), 16)
            sp.dma_start(lwb[:, 1, :], rep(ln_b)).then_inc(sem("in_small"), 16)
            sp.dma_start(gb[:, 0, :], ffn_g.rearrange("(t p) -> p t", p=P),
                         allow_slow_non_contiguous=True).then_inc(sem("in_small"), 16)
            sp.dma_start(gb[:, 1, :], ffn_b.rearrange("(t p) -> p t", p=P),
                         allow_slow_non_contiguous=True).then_inc(sem("in_small"), 16)
            sp.dma_start(rw_sb[:, :, :], r_w.rearrange("(t p) e -> p t e", p=P)).then_inc(sem("in_small"), 16)
            sp.dma_start(rb_sb[:, :], rep(r_b)).then_inc(sem("in_small"), 16)
            sp.dma_start(tok[:, :, :], tile_tab[:, TAB:].rearrange("p (b k) -> p b k", b=B)).then_inc(sem("in_small"), 16)
            sp.wait_ge(sem(f"k_frac{PN}"), 1)
            sp.wait_ge(sem(f"k_frac{QN + PN}"), 1)
            sp.dma_start(ft[:, :, :, :], fwd_tab).then_inc(sem("in_tab"), 16)
            sp.dma_start(it[:, :, :, :], inv_tab).then_inc(sem("in_tab"), 16)
            sp.wait_ge(sem("k_pf"), 2)
            sp.wait_ge(sem("k_qf"), 2)
            for b in range(B):
                if b == 2:
                    sp.wait_ge(sem("k_in0"), 32)
                    sp.wait_ge(sem("k_in1"), 32)
                sp.dma_start(xs[b][:, :, :], x[:, b]).then_inc(sem("in_x" if b < 2 else "in_x2"), 16)
            sp.wait_ge(sem("k_mm"), 2)
            for e in range(5):
                load_expert(sp, e)

            def store_x1(lo, hi):
                for b in range(lo, hi):
                    sp.wait_ge(sem("x1_ready"), b + 1)
                    sp.dma_start(x1_dram[:, b], xs[b][:, :, :]).then_inc(sem("x1_stored"), 16)
                sp.wait_ge(sem("x1_stored"), 16 * hi)

            store_x1(0, 4)
            sp.wait_ge(sem("zn_ready"), 4)
            load_expert(sp, 5)
            store_x1(4, 6)
            sp.wait_ge(sem("zn_ready"), 6)
            sp.wait_ge(sem("mult_done"), 2 * B)
            load_expert(sp, 6)
            sp.wait_ge(sem("inv_mm"), B)
            for e in range(E):
                sp.dma_start(b1r[:, e], rep(b1[e])).then_inc(sem("in_b"), 16)
            for e in range(E):
                sp.dma_start(b2r[:, e], rep(b2[e])).then_inc(sem("in_b"), 16)
            store_x1(6, 8)
            sp.wait_ge(sem("zn_ready"), B)
            sp.wait_ge(sem("x1_ready"), B)
            sp.dma_start(tri[:, :, :], tile_tab[:, 0:E * E].rearrange("p (a b) -> p a b", a=E)).then_inc(sem("in_e"), 16)
            sp.dma_start(iot[:, :, :], tile_tab[:, E * E:TAB].rearrange("p (a b) -> p a b", a=2)).then_inc(sem("in_e"), 16)
            for par in range(2):
                sp.wait_ge(sem(f"scattered{par}"), 64 * 6)
            load_expert(sp, 7)
            sp.wait_ge(sem("pad_set"), 1)
            behind = [sp.value_load(padi[0:1, e:e + 1], min_val=0, max_val=ROWS - P) for e in range(E)]
            for i in (2, 3):
                sp.wait_ge(sem(f"scattered{i}"), 128)
            for e in range(E):
                sp.dma_start(z_rows[bass.ds(behind[e], P), :], zpad[:, :]).then_inc(sem("pads"), 16)

            def load_z(t, par):
                row = sp.value_load(tab[0:1, 0, bass.ds(t, 1)], min_val=0, max_val=ROWS - P)
                if not (isinstance(t, int) and t < 2):
                    sp.wait_ge(sem("tz_mm"), t - 1)
                    sp.wait_ge(sem("dest_ready"), t - 1)
                sp.dma_start(z_in[par][:, :], z_rows[bass.ds(row, P), :]).then_inc(sem(f"z_in{par}"), 16)

            sp.wait_ge(sem("tab_ready"), 1)
            sp.wait_ge(sem("pads"), 16 * E)
            load_z(0, 0)
            load_z(1, 1)
            sp.dma_start(x1m[:, 4:8], x1_dram[:, 4:8]).then_inc(sem("x1_in"), 16)
            with sp.Fori(0, (TILES - 3) // 2) as j:
                load_z(j * 2 + 2, 0)
                load_z(j * 2 + 3, 1)
            load_z(TILES - 1, 0)

            sp.wait_ge(sem("l2_mm"), TILES)
            sp.wait_ge(sem("x1_in"), 16)
            sp.wait_ge(sem("y_out0"), 16 * ((TILES + 1) // 2))
            sp.wait_ge(sem("y_out1"), 16 * (TILES // 2))
            y_tok = y_rows[0:TRASH, :].rearrange("(c p b k) h -> p b c (k h)", c=2, b=B, k=4)
            for n in range(B):
                if n >= 2:
                    sp.wait_ge(sem(f"y_in{n % 2}"), 16 * (n // 2))
                if n == 3:
                    sp.dma_start(x1m[:, 0:4], x1_dram[:, 0:4]).then_inc(sem("x1_in"), 16)
                sp.dma_start(ya[:, n].rearrange("p c k h -> p c (k h)"), y_tok[:, B - 1 - n]).then_inc(sem(f"y_in{n % 2}"), 16)
            for n in range(B):
                sp.wait_ge(sem("m_out"), n + 1)
                sp.dma_start(out[:, B - 1 - n], acc[:, n]).then_inc(sem("stored"), 16)
            sp.wait_ge(sem("stored"), 16 * B)

        @block.scalar
        def _(act):
            seq = Seq(act, sem("act_seq"))
            act.wait_ge(sem("in_modes"), 64)
            nc.scalar.activation(dtv[:, 1, :], dtv[:, 0, :], ACT.Exp)
            nc.scalar.activation(sm[:, 0], raw[:, 0], ACT.Exp).then_inc(sem("k_exp"), 1)
            act.wait_ge(sem("k_ua"), 1)
            nc.scalar.activation(sm[:, 1], quant[:, 1, :, 0, :], ACT.Tanh, scale=0.5).then_inc(sem("k_tanh"), 1)
            act.wait_ge(sem("k_half"), 1)
            nc.scalar.activation(sm[:, 4:6], sm[:, 2:4], ACT.Sin, scale=TURN).then_inc(sem("k_trig"), 1)
            act.wait_ge(sem("k_tr"), 1)
            nc.scalar.copy(qt[:, 0:2], bank(0).rearrange("p (q h) -> p q h", q=2)).then_inc(sem("k_qt"), 1)
            act.wait_ge(sem("k_qt"), 1)
            act.wait_ge(sem("in_slots"), 32)
            for q in range(QN):
                last = nc.scalar.activation(v[:, q], qt[:, 0], ACT.Identity, bias=so[:, 0:1], scale=float(q))
                if q % PN == PN - 1:
                    last.then_inc(sem("k_turned"), 1)
            for u, g in enumerate(MAGS):
                act.wait_ge(sem("k_aq"), u + 1)
                nc.scalar.activation(mag[:, g:g + PN], mag[:, g:g + PN], ACT.Exp).then_inc(sem("k_mag"), 1)
            for g in SINES:
                act.wait_ge(sem(f"k_frac{g}"), 1)
                nc.scalar.activation(v[:, g:g + PN], v[:, g:g + PN], ACT.Sin, scale=TURN).then_inc(sem("k_sin"), 1)
            for ht in range(2):
                act.wait_ge(sem("k_mm"), ht + 1)
                for j in (2 * ht, 2 * ht + 1):
                    nc.scalar.copy(k_sb[32 * j:32 * j + PN, :],
                                   psum[32 * j:32 * j + PN, 4 * 512:8 * 512]).then_inc(sem("k_evac"), 1)
                act.wait_ge(sem("k_evac"), 2 * ht + 2)
                for j in (2 * ht, 2 * ht + 1):
                    act.dma_start(k_dram[j], k_sb[32 * j:32 * j + PN, :]).then_inc(sem(f"k_out{ht}"), 16)
            for ht in range(2):
                act.wait_ge(sem(f"k_out{ht}"), 32)
                for j in (2 * ht, 2 * ht + 1):
                    act.dma_start(kh[64 * (j % 2):64 * (j % 2) + 64, ht, :].rearrange("h (p q) -> h p q", p=PN),
                                  k_dram[j].rearrange("p (h q) -> h p q", q=QN)).then_inc(sem(f"k_in{ht}"), 16)
            act.wait_ge(sem("upper_set"), 1)
            for ht in range(2):
                act.wait_ge(sem("kt_mm"), ht + 1)
                nc.scalar.copy(k_t[:, :, ht * P:ht * P + P],
                               bank(ht).rearrange("p (l h) -> p l h", l=KT)).then_inc(sem("kt_evac"), 1)

            def sigma(row, slot):
                act.wait_ge(sem(f"var{slot}"), row.b + 1)
                if not row.first():
                    act.wait_ge(sem(USES[slot]), row.b)
                nc.scalar.activation(sd[:, slot, :], mv[slot][:, :, 1], ACT.Sqrt, bias=eps[:, slot // 3:slot // 3 + 1],
                                     scale=1.0 + EPS if slot == 3 else 1.0).then_inc(sem(f"sd{slot}"), 1)

            def split_high(e):
                act.wait_ge(sem(f"in_w{e}"), 32)
                nc.scalar.copy(ws[:, e, 0], w_raw[e][:, :]).then_inc(sem("w_high"), 1)

            def step(n):
                new, inv, cur, mid, tail = (Row(n, k) for k in (2, 0, -1, -2, -LAG))
                if cur.live:
                    sigma(cur, 2)
                if new.live:
                    sigma(new, 0)
                if tail.live:
                    act.wait_ge(sem("zt_mm"), tail.b + 1)
                    if not tail.first():
                        act.wait_ge(sem("lg_mm"), tail.b)
                    for k in range(2):
                        nc.scalar.activation(zt[:, k, :], route(tail.b)[k], ACT.Identity, bias=gb[:, 1, k:k + 1],
                                             scale=gb[:, 0, k:k + 1]).then_inc(sem("zt_ready"), 1)
                if new.live:
                    act.wait_ge(sem("st_x"), new.b + 1)
                    if not new.first():
                        act.wait_ge(sem("pm_ready"), 2 * new.b)
                    for k in range(4):
                        last = nc.scalar.activation(xn[:, k], xs[new.b][:, k], ACT.Identity, bias=rs[:, 0, 4 + k:5 + k],
                                                    scale=rs[:, 0, k:k + 1])
                    last.then_inc(sem("xn_ready"), 1)
                if cur.live:
                    sigma(cur, 1)
                    act.wait_ge(sem("st_o"), cur.b + 1)
                    if not cur.first():
                        act.wait_ge(sem("x1_ready"), cur.b)
                    for k in range(4):
                        last = nc.scalar.activation(dl[:, k], o[:, k], ACT.Identity, bias=rs[:, 1, 4 + k:5 + k],
                                                    scale=rs[:, 1, k:k + 1])
                    last.then_inc(sem("dl_ready"), 1)
                if inv.live:
                    act.wait_ge(sem("inv_mm"), inv.b + 1)
                    if not inv.first():
                        act.wait_ge(sem("r_ready"), inv.b)
                    nc.scalar.copy(s_sb[:, :, :], iv[1].rearrange("p (j h) -> p j h", j=2)).then_inc(sem("s_copied"), 1)
                if mid.live:
                    sigma(mid, 3)
                    act.wait_ge(sem("st_x1"), mid.b + 1)
                    if 2 <= mid.b < 6:
                        act.wait_ge(sem(f"scattered{mid.par}"), 64 * (mid.b - mid.par))
                    elif mid.b == 6:
                        act.wait_ge(sem("fwd_mm"), 2 * B)
                    for k in range(4):
                        last = nc.scalar.activation(zn[buf(mid.b)][:, k, 0:H], xs[mid.b][:, k],
                                                    ACT.Identity, bias=rs[:, 3, 4 + k:5 + k], scale=rs[:, 3, k:k + 1])
                    last.then_inc(sem("zn_ready"), 1)
                for e in HIGH.get(n, ()):
                    split_high(e)

            act.wait_ge(sem("in_small"), 128)
            step(-2)
            act.wait_ge(sem("kf_mm"), 1)
            nc.scalar.copy(kf[:, 1], bank(4, 2).rearrange("p (k h) -> p k h", k=KT)).then_inc(sem("kf_ready"), 1)
            steps(step)

            act.wait_ge(sem("pad_set"), 1)
            nc.scalar.activation(rsm[:, 0], stat1[:, :, 1, :], ACT.Sqrt, bias=eps[:, 0:1]).then_inc(sem("rsm_sd"), 1)
            split_high(E - 1)
            act.wait_ge(sem("wsm_sub"), 1)
            nc.scalar.activation(wsm[:, :, :, :], wsm[:, :, :, :], ACT.Exp).then_inc(sem("wsm_exp"), 1)

            def part(i, par, u):
                t, q = i + 2, par
                if live(t):
                    act.wait_ge(sem("tz_mm"), t + 1)
                    if not early(t):
                        act.wait_ge(sem("z_split"), t)
                    for k in range(2):
                        last = nc.scalar.activation(z_f[:, k], ps_z[q][:, k], ACT.Identity, bias=gb[:, 1, k:k + 1],
                                                    scale=gb[:, 0, k:k + 1])
                    last.then_inc(sem("zf_ready"), 1)
                t, q = i, par
                if live(t):
                    act.wait_ge(sem("th_mm"), t + 1)
                    if not early(t, 2):
                        act.wait_ge(sem("l2_mm"), t - 1)
                    nc.scalar.copy(h_hl[q][:, 0], ps_t[q]).then_inc(sem("h_high"), 1)
                t, q = i + 1, 1 - par
                if live(t):
                    act.wait_ge(sem("hb_ready"), t + 1)
                    if not early(t, 2):
                        act.wait_ge(sem("th_mm"), t - 1)
                    nc.scalar.activation(hg[q][:, :], hb[:, :], ACT.Gelu).then_inc(sem("hg_ready"), 1)

            tiles(act, part)

            def base(n):
                b = back(n)
                for k in range(4):
                    last = nc.scalar.activation(acc[:, bass.ds(n, 1), k].rearrange("p a h -> p (a h)"),
                                                x1m[:, bass.ds(b, 1), k].rearrange("p a h -> p (a h)"), ACT.Identity,
                                                bias=rsm[:, 1, bass.ds(b, 1), k], scale=rsm[:, 0, bass.ds(b, 1), k])
                last.then_inc(sem("m_base"), 1)

            def close(b, par):
                act.wait_ge(sem("m_var"), b + 1)
                nc.scalar.activation(rm[:, par, 0, :], mvm[par][:, :, 1], ACT.Sqrt, bias=eps[:, 0:1]).then_inc(sem("m_sd"), 1)
                act.wait_ge(sem("m_rs"), b + 1)
                for k in range(4):
                    row = acc[:, bass.ds(b, 1), k].rearrange("p a h -> p (a h)")
                    last = nc.scalar.activation(row, row, ACT.Identity,
                                                bias=rm[:, par, 2, k:k + 1], scale=rm[:, par, 1, k:k + 1])
                last.then_inc(sem("m_fin"), 1)

            act.wait_ge(sem("rsm_ready"), 1)
            act.wait_ge(sem("l2_mm"), TILES)
            act.wait_ge(sem("x1_in"), 16)
            base(0)
            base(1)
            with act.Fori(0, 1) as j:
                base(j * 2 + 2)
                close(j * 2, 0)
                base(j * 2 + 3)
                close(j * 2 + 1, 1)
            act.wait_ge(sem("x1_in"), 32)
            with act.Fori(1, B // 2 - 1) as j:
                base(j * 2 + 2)
                close(j * 2, 0)
                base(j * 2 + 3)
                close(j * 2 + 1, 1)
            close(6, 0)
            close(7, 1)

        @block.vector
        def _(dve):
            seq = Seq(dve, sem("dve_seq"))
            V = nc.vector

            def do(ins, fill=iter(())):
                seq.inc(ins)
                for other in fill:
                    other()
                    break
                seq.wait()

            def stats(src, slot):
                for k in range(4):
                    last = V.bn_stats(st[:, slot, k, :], src(k))
                do(last)
                for k in range(4):
                    last = V.bn_aggr(mv[slot][:, k, :], st[:, slot, k, :])
                last.then_inc(sem(f"var{slot}"), 1)

            V.memset(eps[:, 0:1], EPS)
            V.memset(eps[:, 1:2], EPS * EPS).then_inc(sem("one"), 1)
            V.memset(carry[:, :], 0.0)
            seq.inc(V.memset(carry_b[:, :], 0.0))
            for e in range(E):
                V.memset(iota8[:, 0, e:e + 1], float(e))
                V.memset(iota8[:, 1, e:e + 1], float(e * REGION))
            dve.wait_ge(sem("k_exp"), 1)
            for ht in range(2):
                for dup in range(2):
                    V.tensor_scalar(quant[:, 0, ht, dup], raw[:, 1, ht], dtv[:, 1, ht:ht + 1], 0.15915494309189535,
                                    ALU.mult, ALU.mult)
                    last = V.tensor_scalar(quant[:, 1, ht, dup], sm[:, 0, ht], dtv[:, 1, ht:ht + 1], -1.0,
                                           ALU.mult, ALU.mult)
            last.then_inc(sem("k_ua"), 1)
            dve.wait_ge(sem("k_ua"), 1)
            do(V.tensor_scalar(sm[:, 2], quant[:, 0, :, 0], 0.5, None, ALU.mult))
            do(V.tensor_scalar(sm[:, 3], sm[:, 2], 0.25, None, ALU.add))
            do(V.tensor_scalar(sm2[:, 0:2], sm[:, 2:4], ROUND, ROUND, ALU.add, ALU.subtract))
            V.tensor_tensor(sm[:, 2:4], sm[:, 2:4], sm2[:, 0:2], ALU.subtract).then_inc(sem("k_half"), 1)
            dve.wait_ge(sem("k_tanh"), 1)
            em1, t1, t2, t3 = sm2[:, 2], sm2[:, 3], sm2[:, 4], sm2[:, 5]
            do(V.tensor_scalar(t1, sm[:, 1], -1.0, 1.0, ALU.mult, ALU.add))
            do(V.reciprocal(t2, t1))
            do(V.scalar_tensor_tensor(em1, sm[:, 1], 2.0, t2, ALU.mult, ALU.mult))
            ea, ai, cr, ci = sm[:, 0], raw[:, 1], raw[:, 2], raw[:, 3]
            dve.wait_ge(sem("k_trig"), 1)
            sn, cs = sm[:, 4], sm[:, 5]
            ere, eim, nre, nim = sm2[:, 6], sm2[:, 7], sm2[:, 8], sm2[:, 9]
            do(V.tensor_tensor(t1, sn, sn, ALU.mult))
            do(V.tensor_scalar(t2, t1, -2.0, 1.0, ALU.mult, ALU.add))
            do(V.tensor_tensor(t2, em1, t2, ALU.mult))
            do(V.scalar_tensor_tensor(ere, t1, -2.0, t2, ALU.mult, ALU.add))
            do(V.tensor_tensor(t3, sn, cs, ALU.mult))
            do(V.scalar_tensor_tensor(t1, em1, 1.0, t3, ALU.add, ALU.mult))
            do(V.tensor_scalar(eim, t1, 2.0, None, ALU.mult))
            dve.wait_ge(sem("in_coef"), 32)
            do(V.tensor_tensor(t1, cr, ere, ALU.mult))
            do(V.tensor_tensor(t2, ci, eim, ALU.mult))
            do(V.tensor_tensor(nre, t1, t2, ALU.subtract))
            do(V.tensor_tensor(t1, cr, eim, ALU.mult))
            do(V.tensor_tensor(t2, ci, ere, ALU.mult))
            do(V.tensor_tensor(nim, t1, t2, ALU.add))
            do(V.tensor_tensor(t1, ea, ea, ALU.mult))
            do(V.tensor_tensor(t2, ai, ai, ALU.mult))
            do(V.tensor_tensor(t1, t1, t2, ALU.add))
            do(V.reciprocal(t3, t1))
            do(V.tensor_tensor(t1, nim, ai, ALU.mult))
            do(V.tensor_tensor(t2, nre, ea, ALU.mult))
            do(V.tensor_tensor(t1, t1, t2, ALU.subtract))
            for dup in range(2):
                do(V.scalar_tensor_tensor(quant[:, 2, :, dup], t1, 2.0, t3, ALU.mult, ALU.mult))
            do(V.tensor_tensor(t1, nim, ea, ALU.mult))
            do(V.tensor_tensor(t2, nre, ai, ALU.mult))
            do(V.tensor_tensor(t1, t1, t2, ALU.add))
            for dup in range(2):
                last = V.scalar_tensor_tensor(quant[:, 3, :, dup], t1, -2.0, t3, ALU.mult, ALU.mult)
            last.then_inc(sem("k_quant"), 1)
            G1, G2 = QN, QN + PN
            dve.wait_ge(sem("k_qt"), 1)
            dve.wait_ge(sem("in_slots"), 32)

            def turns(g):
                for p in range(PN):
                    last = V.tensor_scalar(v[:, g + p], qt[:, 0], float(QN * p), so[:, g:g + 1], ALU.mult, ALU.add)
                do(last)

            def whole(g, i):
                V.tensor_scalar(kr[i][:, :, :], v[:, g:g + PN], ROUND, ROUND, ALU.add,
                                ALU.subtract).then_inc(sem(f"k_round{g}"), 1)

            def fraction(g, i):
                dve.wait_ge(sem(f"k_round{g}"), 1)
                V.tensor_tensor(v[:, g:g + PN], v[:, g:g + PN], kr[i][:, :, :], ALU.subtract).then_inc(sem(f"k_frac{g}"), 1)

            def wide(q, hs=slice(0, H)):
                return qt[:, q, hs].unsqueeze(1).to_broadcast([P, PN, hs.stop - hs.start])

            turns(G2)
            whole(G2, 1)
            turns(G1)
            whole(G1, 0)
            fraction(G1, 0)
            dve.wait_ge(sem("k_tr"), 2)
            V.tensor_copy(qt[:, 2:4], bank(1).rearrange("p (q h) -> p q h", q=2)).then_inc(sem("k_qt"), 1)
            dve.wait_ge(sem("k_frac%d" % G1), 1)
            dve.wait_ge(sem("k_turned"), 1)
            whole(0, 0)
            fraction(0, 0)
            dve.wait_ge(sem("k_frac%d" % G2), 1)
            dve.wait_ge(sem("k_turned"), 2)
            whole(PN, 1)
            fraction(PN, 1)
            dve.wait_ge(sem("k_qt"), 2)
            dve.wait_ge(sem("k_sin"), SINES.index(G1) + 1)
            do(V.tensor_tensor(v[:, G1:G2], v[:, G1:G2], wide(2), ALU.mult))
            dve.wait_ge(sem("k_sin"), SINES.index(0) + 1)
            dve.wait_ge(sem("k_mag"), MAGS.index(0) + 1)
            V.tensor_tensor(v[:, 0:PN], v[:, 0:PN], mag[:, 0:PN], ALU.mult)
            dve.wait_ge(sem("k_g2"), 1)
            do(V.tensor_tensor(v[:, G1:G2], v[:, G1:G2], v[:, G2:SLOTS], ALU.add))
            dve.wait_ge(sem("k_mag"), MAGS.index(G1) + 1)
            for ht in range(2):
                hs = slice(ht * P, ht * P + P)
                V.tensor_tensor(v[:, G1:G2, hs], v[:, G1:G2, hs], mag[:, G1:G2, hs], ALU.mult).then_inc(sem("k_pf"), 1)
            dve.wait_ge(sem("in_upper"), 16)
            V.tensor_copy(upper[:, :, :], upper_f[:, :, :]).then_inc(sem("upper_set"), 1)
            def mult(row, u):
                n, par = row.b * 2 + u, row.par
                dve.wait_ge(sem("fwd_mm"), n + 1)
                if not row.first():
                    dve.wait_ge(sem("yf_ready"), 2 * n - 2)
                if not row.first(2):
                    dve.wait_ge(sem("inv_mm"), row.b - 1)
                re, im = fw[u]
                ks = slice(2 * u, 2 * u + 2)
                V.tensor_tensor(yf[par][:, 0, ks], re, kf[:, 0, ks], ALU.mult)
                V.tensor_tensor(tmp[u][:, 0], im, kf[:, 1, ks], ALU.mult)
                V.tensor_tensor(yf[par][:, 1, ks], re, kf[:, 1, ks], ALU.mult)
                V.tensor_tensor(tmp[u][:, 1], im, kf[:, 0, ks], ALU.mult).then_inc(sem("mult_done"), 1)

            def inverse(row, slot):
                dve.wait_ge(sem(f"sd{slot}"), row.b + 1)
                return V.reciprocal(rs[:, slot, 0:4], sd[:, slot, :])

            def split_low(e):
                dve.wait_ge(sem("w_high"), e + 1)
                V.tensor_tensor(ws[:, e, 1], w_raw[e][:, :], ws[:, e, 0].bitcast(F32), ALU.subtract).then_inc(sem("w_low"), 1)

            def choose(row, fill):
                dve.wait_ge(sem("lg_mm"), row.b + 1)
                do(V.tensor_tensor(lgs[:, :, :], route(row.b)[1][:, 0:32].rearrange("p (k e) -> p k e", k=4),
                                   rb_sb[:, :].unsqueeze(1).to_broadcast([P, 4, E]), ALU.add), fill)
                for k in range(4):
                    last = V.max(mx_all[:, row.b, k], lgs[:, k])
                do(last, fill)
                for k in range(4):
                    last = V.max_index(mi[:, k], mx_all[:, row.b, k], lgs[:, k])
                do(last, fill)
                do(V.tensor_copy(mif[:, :, :], mi[:, :, 0:2].rearrange("p t c -> p c t")), fill)
                for c in range(2):
                    last = V.tensor_tensor(oh[:, c], iota8[:, 0].unsqueeze(1).to_broadcast([P, 4, E]),
                                           mif[:, c].unsqueeze(2).to_broadcast([P, 4, E]), ALU.is_equal)
                do(last)
                V.tensor_tensor(mask[:, :, :], oh[:, 0], oh[:, 1], ALU.add).then_inc(sem("mask_ready"), 1)

            def place(row):
                dve.wait_ge(sem("rank_mm"), row.b + 1)
                V.tensor_reduce(msum[:, :], mask[:, :, :].rearrange("p t e -> p e t"), AX.X, ALU.add)
                do(V.tensor_tensor(posf[:, :, :], route(row.b)[1][:, 64:96].rearrange("p (t e) -> p t e", t=4),
                                   iota8[:, 1].unsqueeze(1).to_broadcast([P, 4, E]), ALU.add))
                V.tensor_tensor(carry[:, :], carry[:, :], msum[:, :], ALU.add)
                for c in range(2):
                    last = V.tensor_tensor(prod[:, c], oh[:, c], posf[:, :, :], ALU.mult)
                do(last)
                V.tensor_copy(carry_b[:, :], carry[:, :]).then_inc(sem("carry_ready"), 1)
                do(V.tensor_reduce(posr[:, :, :], prod[:, :, :, :], AX.X, ALU.add))
                if not row.first(2):
                    dve.wait_ge(sem(f"scattered{row.par}"), 64 * min(row.b - row.par, 6))
                V.tensor_copy(zn[buf(row.b)][:, :, H], tok[:, row.b])
                V.tensor_copy(zn[buf(row.b)][:, :, H + 1], mif[:, 1])
                V.tensor_copy(pos[row.par][:, :, :], posr[:, :, :]).then_inc(sem("pos_ready"), 1)

            def step(n):
                new, nxt, cur, mid, tail = (Row(n, k) for k in (2, 1, -1, -2, -LAG))
                if cur.live:
                    dve.wait_ge(sem("s_copied"), cur.b + 1)
                    c = iv[0].rearrange("p (j h) -> p j h", j=2)
                    V.tensor_tensor(r[:, 0:2], c, s_sb[:, :, :], ALU.add)
                    V.tensor_tensor(r[:, 2:4], c, s_sb[:, :, :], ALU.subtract).then_inc(sem("r_ready"), 1)
                    dve.wait_ge(sem("r_ready"), cur.b + 1)
                    stats(lambda k: r[:, k], 2)
                if new.live:
                    if new.b == 2:
                        dve.wait_ge(sem("in_x2"), 96)
                    stats(lambda k: xs[new.b][:, k], 0)
                if nxt.live:
                    mult(nxt, 0)
                if cur.live:
                    seq.inc(inverse(cur, 2))
                if new.live:
                    if not new.first():
                        dve.wait_ge(sem("xn_ready"), new.b)
                    do(inverse(new, 0))
                    V.scalar_tensor_tensor(rs[:, 0, 4:8], mv[0][:, :, 0], -1.0, rs[:, 0, 0:4], ALU.mult,
                                           ALU.mult).then_inc(sem("st_x"), 1)
                if cur.live:
                    if not cur.first():
                        dve.wait_ge(sem("dl_ready"), cur.b)
                    for k in range(4):
                        last = V.scalar_tensor_tensor(o[:, k], r[:, k], mv[2][:, k, 0:1], lwb[:, 0], ALU.subtract,
                                                      ALU.mult)
                    last.then_inc(sem("o_norm"), 1)
                    dve.wait_ge(sem("o_norm"), cur.b + 1)
                    for k in range(4):
                        last = V.scalar_tensor_tensor(o[:, k], o[:, k], rs[:, 2, k:k + 1], lwb[:, 1], ALU.mult, ALU.add)
                    do(last)
                    stats(lambda k: o[:, k], 1)
                if nxt.live:
                    mult(nxt, 1)
                if cur.live:
                    do(inverse(cur, 1))
                    V.scalar_tensor_tensor(rs[:, 1, 4:8], mv[1][:, :, 0], -1.0, rs[:, 1, 0:4], ALU.mult,
                                           ALU.mult).then_inc(sem("st_o"), 1)

                def mid_statistics():
                    for k in range(4):
                        last = V.bn_aggr(mv[3][:, k, :], st[:, 3, k, :])
                    last.then_inc(sem("var3"), 1)

                def mid_scales():
                    if not mid.first():
                        dve.wait_ge(sem("zn_ready"), mid.b)
                    do(inverse(mid, 3))
                    V.tensor_copy(stat1[:, mid.b], mv[3][:, :, :].rearrange("p k c -> p c k"))
                    V.scalar_tensor_tensor(rs[:, 3, 4:8], mv[3][:, :, 0], -1.0, rs[:, 3, 0:4], ALU.mult,
                                           ALU.mult).then_inc(sem("st_x1"), 1)

                fill = []
                if mid.live:
                    dve.wait_ge(sem("x1_ready"), mid.b + 1)
                    fill = [lambda k=k: V.bn_stats(st[:, 3, k, :], xs[mid.b][:, k]) for k in range(4)]
                if mid.live and (n > B or not tail.live):
                    for f in fill:
                        last = f()
                    do(last)
                    mid_statistics()
                    mid_scales()
                    fill = []
                for e in LOW.get(n, ()):
                    split_low(e)
                if tail.live:
                    choose(tail, iter(fill))
                    if fill:
                        mid_statistics()
                    place(tail)
                    if fill:
                        mid_scales()

            dve.wait_ge(sem("in_small"), 128)
            seq.inc(V.tensor_scalar(d_rep[:, :], d_rep[:, :], 1.0, None, ALU.add))
            dve.wait_ge(sem("in_x"), 32)
            step(-2)
            dve.wait_ge(sem("kf_mm"), 1)
            for k in range(KT):
                last = V.tensor_tensor(kf[:, 0, k], bank(2, 2)[:, k * H:(k + 1) * H], d_rep[:, :], ALU.add)
            last.then_inc(sem("kf_ready"), 1)
            dve.wait_ge(sem("kf_ready"), 2)

            steps(step)

            dve.wait_ge(sem("zn_ready"), B)
            dve.wait_ge(sem("cnt_mm"), 1)
            do(V.tensor_copy(cnt[:, 0], tp[1][:, 0:E]))
            V.memset(zpad[:, 0:H], 0.0)
            V.memset(zpad[:, H + 1:W], -1.0)
            V.tensor_scalar(zpad[:, H:H + 1], tok[:, 0, 0:1], 1.0 / (4 * B), float(TRASH), ALU.mult, ALU.add)
            V.tensor_scalar(cnt[:, 1], cnt[:, 0], 1.0 / P, (P - 1) / (2.0 * P), ALU.mult, ALU.add)
            V.tensor_tensor(padf[:, :], cnt[0:1, 0], iota8[0:1, 1], ALU.add)
            V.tensor_tensor(padi[:, :], cnt[0:1, 0], iota8[0:1, 1], ALU.add).then_inc(sem("pad_set"), 1)
            dve.wait_ge(sem("pad_set"), 1)
            do(V.tensor_scalar(cnt[:, 1], cnt[:, 1], ROUND, ROUND, ALU.add, ALU.subtract))
            dve.wait_ge(sem("in_e"), 32)
            do(V.tensor_tensor(tri[:, :, :], tri[:, :, :], cnt[:, 1].unsqueeze(1).to_broadcast([P, E, E]), ALU.mult))
            do(V.tensor_reduce(cnt[:, 2], tri[:, :, :], AX.X, ALU.add))
            NT = TILES + 1
            do(V.tensor_tensor(cmp_t[:, :, :], cnt[:, 2].unsqueeze(1).to_broadcast([P, NT, E]),
                               iot[:, 0].unsqueeze(2).to_broadcast([P, NT, E]), ALU.is_le))
            do(V.tensor_tensor(cmp_n[:, :, :], cmp_t[:, :, :], cnt[:, 1].unsqueeze(1).to_broadcast([P, NT, E]), ALU.mult))
            V.tensor_reduce(tf[:, 0], cmp_t[:, :, :], AX.X, ALU.add)
            do(V.tensor_reduce(tf[:, 1], cmp_n[:, :, :], AX.X, ALU.add))
            V.tensor_scalar(tab[:, 1], tf[0:1, 0], float(E - 1), None, ALU.min)
            V.tensor_scalar(tab_e[:, :], tf[:, 0], float(E - 1), None, ALU.min)
            do(V.scalar_tensor_tensor(tf[:, 2], tf[:, 0], float(REGION), iot[:, 1], ALU.mult, ALU.add))
            do(V.scalar_tensor_tensor(tf[0:1, 0], tf[0:1, 1], -float(P), tf[0:1, 2], ALU.mult, ALU.add))
            V.tensor_scalar(tab[:, 0], tf[0:1, 0], padf[:, E - 1:E], None, ALU.min).then_inc(sem("tab_ready"), 1)
            for e in LOW[B + LAG]:
                split_low(e)
            V.tensor_tensor(wsm[:, :, :, :], mx_all[:, :, :, :], mx_all[:, :, :, 0:1].to_broadcast([P, B, 4, E]),
                            ALU.subtract).then_inc(sem("wsm_sub"), 1)
            dve.wait_ge(sem("rsm_sd"), 1)
            do(V.reciprocal(rsm[:, 0], rsm[:, 0]))
            do(V.scalar_tensor_tensor(rsm[:, 1], stat1[:, :, 0, :], -1.0, rsm[:, 0], ALU.mult, ALU.mult))
            dve.wait_ge(sem("wsm_exp"), 1)
            do(V.tensor_reduce(rsm[:, 2], wsm[:, :, :, :], AX.X, ALU.add))
            do(V.reciprocal(rsm[:, 3], rsm[:, 2]))
            for c in range(2):
                last = V.tensor_tensor(wgt[:, c], wsm[:, :, :, c], rsm[:, 3], ALU.mult)
            do(last)
            do(V.tensor_tensor(wgt[:, 2], wgt[:, 0], wgt[:, 1], ALU.add))
            do(V.tensor_scalar(wgt[:, 2], wgt[:, 2], 1e-8, None, ALU.max))
            do(V.reciprocal(wgt[:, 3], wgt[:, 2]))
            for c in range(2):
                last = V.tensor_tensor(wgt[:, c], wgt[:, c], wgt[:, 3], ALU.mult)
            last.then_inc(sem("rsm_ready"), 1)
            dve.wait_ge(sem("rsm_ready"), 1)

            dve.wait_ge(sem("in_b"), 32 * E)

            def part(i, par, u):
                t, q = i + 2, par
                if live(t):
                    dve.wait_ge(sem(f"z_in{q}"), (t - q) * 8 + 16)
                    V.tensor_scalar(flag[:, :], z_in[q][:, H + 1:W], tab_e[:, bass.ds(t, 1)], float(B * T),
                                    ALU.is_equal, ALU.mult).then_inc(sem("flag_set"), 1)
                    dve.wait_ge(sem("flag_set"), t + 1)
                    V.tensor_tensor(dest[:, bass.ds(t, 1)], z_in[q][:, H:H + 1], flag[:, :],
                                    ALU.add).then_inc(sem("dest_ready"), 1)
                    dve.wait_ge(sem("zf_ready"), t + 1)
                    if not early(t, 2):
                        dve.wait_ge(sem("l1_mm"), t - 1)
                    V.tensor_copy(z_hl[q][:, 0], z_f[:, :, :]).then_inc(sem("z_high"), 1)
                    dve.wait_ge(sem("z_high"), t + 1)
                    V.tensor_tensor(z_hl[q][:, 1], z_f[:, :, :], z_hl[q][:, 0].bitcast(F32),
                                    ALU.subtract).then_inc(sem("z_split"), 1)
                t, q = i + 1, 1 - par
                if live(t):
                    e = expert(dve, t, u + 1)
                    dve.wait_ge(sem("l1_mm"), t + 1)
                    if not early(t):
                        dve.wait_ge(sem("hg_ready"), t)
                    V.tensor_tensor(hb[:, :], ps_h[q], b1r[:, bass.ds(e, 1)].rearrange("p a f -> p (a f)"),
                                    ALU.add).then_inc(sem("hb_ready"), 1)
                t, q = i, par
                if live(t):
                    dve.wait_ge(sem("h_high"), t + 1)
                    V.tensor_tensor(h_hl[q][:, 1], ps_t[q], h_hl[q][:, 0].bitcast(F32),
                                    ALU.subtract).then_inc(sem("h_split"), 1)
                t, q = i - 1, 1 - par
                if live(t):
                    e = expert(dve, t, u - 1)
                    dve.wait_ge(sem("l2_mm"), t + 1)
                    if not early(t, 2):
                        dve.wait_ge(sem(f"y_out{q}"), (t - q) * 8)
                    gate(dve)
                    V.tensor_copy(dst[q][:, :], dest[:, bass.ds(t, 1)])
                    V.tensor_tensor(y_sb[q][:, :], ps_y[q], b2r[:, bass.ds(e, 1)].rearrange("p a f -> p (a f)"),
                                    ALU.add).then_inc(sem("y_ready"), 1)

            tiles(dve, part)

            def mix(b, par):
                dve.wait_ge(sem(f"y_in{par}"), b * 8 + 16 - 8 * par)
                dve.wait_ge(sem("m_base"), b + 1)
                for k in range(4):
                    row = acc[:, bass.ds(b, 1), k].rearrange("p a h -> p (a h)")
                    last = V.scalar_tensor_tensor(row, ya[:, bass.ds(b, 1), 1, k].rearrange("p a h -> p (a h)"),
                                                  wgt[:, 1, bass.ds(back(b), 1), k], row, ALU.mult, ALU.add)
                last.then_inc(sem("m_second"), 1)
                dve.wait_ge(sem("m_second"), b + 1)
                dve.wait_ge(sem("m_first"), b + 1)
                row = acc[:, bass.ds(b, 1)]
                V.tensor_tensor(row, row, ya[:, bass.ds(b, 1), 0], ALU.add).then_inc(sem("m_mixed"), 1)
                dve.wait_ge(sem("m_mixed"), b + 1)
                gate(dve)
                for k in range(4):
                    last = V.bn_stats(st[:, par, k, :], acc[:, bass.ds(b, 1), k].rearrange("p a h -> p (a h)"))
                last.then_inc(sem("m_stat"), 1)
                dve.wait_ge(sem("m_stat"), b + 1)
                gate(dve)
                for k in range(4):
                    last = V.bn_aggr(mvm[par][:, k, :], st[:, par, k, :])
                last.then_inc(sem("m_var"), 1)

            def scale(b, par):
                dve.wait_ge(sem("m_sd"), b + 1)
                V.reciprocal(rm[:, par, 1, :], rm[:, par, 0, :]).then_inc(sem("m_inv"), 1)
                dve.wait_ge(sem("m_inv"), b + 1)
                V.scalar_tensor_tensor(rm[:, par, 2, :], mvm[par][:, :, 0], -1.0, rm[:, par, 1, :], ALU.mult,
                                       ALU.mult).then_inc(sem("m_rs"), 1)

            mix(0, 0)
            with dve.Fori(0, B // 2 - 1) as j:
                mix(j * 2 + 1, 1)
                scale(j * 2, 0)
                mix(j * 2 + 2, 0)
                scale(j * 2 + 1, 1)
            mix(B - 1, 1)
            scale(B - 2, 0)
            scale(B - 1, 1)

        @block.gpsimd
        def _(pool):
            G = nc.gpsimd
            G2 = QN + PN
            pool.wait_ge(sem("k_qt"), 1)
            pool.wait_ge(sem("in_slots"), 32)
            for g in MAGS:
                G.tensor_tensor(mag[:, g:g + PN], qt[:, 1].unsqueeze(1).to_broadcast([P, PN, H]),
                                sc[:, g:g + PN].unsqueeze(2).to_broadcast([P, PN, H]), ALU.mult).then_inc(sem("k_aq"), 1)
                if g == MAGS[0]:
                    pool.wait_ge(sem(f"k_round{G2}"), 1)
                    G.tensor_tensor(v[:, G2:SLOTS], v[:, G2:SLOTS], kr[1][:, :, :],
                                    ALU.subtract).then_inc(sem(f"k_frac{G2}"), 1)
            pool.wait_ge(sem("k_sin"), SINES.index(G2) + 1)
            pool.wait_ge(sem("k_qt"), 2)
            G.tensor_tensor(v[:, G2:SLOTS], v[:, G2:SLOTS], qt[:, 3].unsqueeze(1).to_broadcast([P, PN, H]),
                            ALU.mult).then_inc(sem("k_g2"), 1)
            pool.wait_ge(sem("k_sin"), SINES.index(PN) + 1)
            pool.wait_ge(sem("k_mag"), MAGS.index(PN) + 1)
            for ht in range(2):
                hs = slice(ht * P, ht * P + P)
                G.tensor_tensor(v[:, PN:QN, hs], v[:, PN:QN, hs], mag[:, PN:QN, hs], ALU.mult).then_inc(sem("k_qf"), 1)

            def combine(row, u):
                n, par = row.b * 2 + u, row.par
                pool.wait_ge(sem("mult_done"), n + 1)
                ks = slice(2 * u, 2 * u + 2)
                G.tensor_tensor(yf[par][:, 0, ks], yf[par][:, 0, ks], tmp[u][:, 0],
                                ALU.subtract).then_inc(sem("yf_ready"), 1)
                G.tensor_tensor(yf[par][:, 1, ks], yf[par][:, 1, ks], tmp[u][:, 1],
                                ALU.add).then_inc(sem("yf_ready"), 1)

            def split_low(e):
                pool.wait_ge(sem("w_high"), e + 1)
                G.tensor_tensor(ws[:, e, 1], w_raw[e][:, :], ws[:, e, 0].bitcast(F32), ALU.subtract).then_inc(sem("w_low"), 1)

            def step(n):
                new, nxt, cur, tail = (Row(n, k) for k in (2, 1, -1, -LAG))
                if nxt.live:
                    combine(nxt, 0)
                if new.live:
                    pool.wait_ge(sem("xn_ready"), new.b + 1)
                    if not new.first(2):
                        pool.wait_ge(sem("fwd_mm"), 2 * (new.b - 1))
                    G.tensor_tensor(pm[new.par][:, 0], xn[:, 0:2], xn[:, 2:4], ALU.add).then_inc(sem("pm_ready"), 1)
                    G.tensor_tensor(pm[new.par][:, 1], xn[:, 0:2], xn[:, 2:4], ALU.subtract).then_inc(sem("pm_ready"), 1)
                if nxt.live:
                    combine(nxt, 1)
                if cur.live:
                    pool.wait_ge(sem("dl_ready"), cur.b + 1)
                    G.tensor_tensor(xs[cur.b][:, :, :], xs[cur.b][:, :, :], dl[:, :, :], ALU.add).then_inc(sem("x1_ready"), 1)
                for e in LOW_POOL.get(n, ()):
                    split_low(e)
                if tail.live:
                    pool.wait_ge(sem("pos_ready"), tail.b + 1)
                    pool.wait_ge(sem("zn_ready"), tail.b + 1)
                    for c in range(2):
                        for k in range(4):
                            pool.indirect_dma_start(
                                z_rows, bass.IndirectOffsetOnAxis(ap=pos[tail.par][:, c, k:k + 1], axis=0),
                                zn[buf(tail.b)][:, k], None).then_inc(sem(f"scattered{buf(tail.b)}"), 16)

            step(-2)
            steps(step)

            for e in LOW_POOL[B + LAG]:
                split_low(e)

            def scatter_y(t, q):
                pool.wait_ge(sem("y_ready"), t + 1)
                if not early(t):
                    pool.wait_ge(sem(f"y_out{1 - q}"), (t + q) * 8)
                gate(pool)
                pool.indirect_dma_start(y_rows, bass.IndirectOffsetOnAxis(ap=dst[q][:, 0:1], axis=0),
                                        y_sb[q][:, :], None).then_inc(sem(f"y_out{q}"), 16)

            scatter_y(0, 0)
            with pool.Fori(0, (TILES - 1) // 2) as j:
                scatter_y(j * 2 + 1, 1)
                scatter_y(j * 2 + 2, 0)

            def mix(n, par):
                pool.wait_ge(sem(f"y_in{par}"), n * 8 + 16 - 8 * par)
                row = ya[:, bass.ds(n, 1), 0].rearrange("p a k h -> p (a k) h")
                w = wgt[:, 0, bass.ds(back(n), 1)].rearrange("p a k -> p (a k)")
                G.tensor_tensor(row, row, w.unsqueeze(2).to_broadcast([P, 4, H]), ALU.mult).then_inc(sem("m_first"), 1)

            def add(n):
                pool.wait_ge(sem("m_fin"), n + 1)
                row = acc[:, bass.ds(n, 1)]
                G.tensor_tensor(row, row, x1m[:, bass.ds(back(n), 1)], ALU.add).then_inc(sem("m_out"), 1)

            mix(0, 0)
            mix(1, 1)
            mix(2, 0)
            add(0)
            mix(3, 1)
            add(1)
            pool.wait_ge(sem("x1_in"), 32)
            with pool.Fori(1, B // 2 - 1) as j:
                mix(j * 2 + 2, 0)
                add(j * 2)
                mix(j * 2 + 3, 1)
                add(j * 2 + 1)
            add(B - 2)
            add(B - 1)

        @block.tensor
        def _(pe):
            TE = nc.tensor
            for q in range(4):
                if q % 2 == 0:
                    pe.wait_ge(sem("k_quant" if q else "k_ua"), 1)
                for ht in range(2):
                    last = TE.transpose(bank(0, 2)[:, q * H + ht * P:q * H + ht * P + P],
                                        quant[:, q, ht].rearrange("p d n -> p (d n)"), ident[:, :])
                if q % 2:
                    last.then_inc(sem("k_tr"), 1)
            for ht in range(2):
                pe.wait_ge(sem("k_pf"), ht + 1)
                pe.wait_ge(sem("k_qf"), ht + 1)
                for hh in range(P):
                    j, i = 2 * ht + hh // 64, hh % 64
                    last = TE.matmul(psum[32 * j:32 * j + PN, 2048 + i * QN:2048 + (i + 1) * QN],
                                     v[:, QN:QN + PN, ht * P + hh], v[:, 0:QN, ht * P + hh], start=True, stop=True)
                last.then_inc(sem("k_mm"), 1)
            for ht in range(2):
                pe.wait_ge(sem(f"k_in{ht}"), 32)
                for l in range(KT):
                    last = TE.transpose(bank(ht)[:, l * P:(l + 1) * P], kh[:, ht, l * P:(l + 1) * P], ident[:, :])
                last.then_inc(sem("kt_mm"), 1)
            pe.wait_ge(sem("in_lag"), 16)
            pe.wait_ge(sem("k_evac"), 4)
            for ht in range(2):
                pe.wait_ge(sem("kt_evac"), ht + 1)
                for g in range(2 * KT):
                    for l in range(KT):
                        last = TE.matmul(bank(2, 4)[:, g * H + ht * P:g * H + ht * P + P], lag[:, l, g, :],
                                         k_t[:, l, ht * P:ht * P + P], start=l == 0, stop=l == KT - 1)
            last.then_inc(sem("kf_mm"), 1)
            pe.wait_ge(sem("in_tab"), 32)
            pe.wait_ge(sem("kf_ready"), 2)

            def fwd(row, u):
                n = row.b * 2 + u
                pe.wait_ge(sem("pm_ready"), 2 * row.b + 2)
                if not row.first():
                    pe.wait_ge(sem("mult_done"), n - 1)
                for c in range(2):
                    for k in range(2):
                        kt = 2 * u + k
                        for t in range(2):
                            last = TE.matmul(fw[u][c][:, k], ft[:, c, t, kt * P:(kt + 1) * P], pm[row.par][:, c, t],
                                             start=t == 0, stop=t == 1)
                last.then_inc(sem("fwd_mm"), 1)

            def inverse(row, j):
                pe.wait_ge(sem("yf_ready"), 4 * row.b + 4)
                if not row.first():
                    pe.wait_ge(sem("r_ready"), row.b)
                for c in range(2):
                    for k in range(KT):
                        last = TE.matmul(iv[c][:, j * H:(j + 1) * H], it[:, c, k, j * P:(j + 1) * P],
                                         yf[row.par][:, c, k], start=k == 0, stop=k == KT - 1)
                if j == 1:
                    last.then_inc(sem("inv_mm"), 1)

            def turn(row):
                pe.wait_ge(sem("zn_ready"), row.b + 1)
                if 0 < row.b < B - 1:
                    pe.wait_ge(sem("pos_ready"), row.b)
                for k in range(2):
                    for q in range(4):
                        last = TE.transpose(route(row.b)[k][:, q * P:(q + 1) * P],
                                            zn[buf(row.b)][:, q, k * P:(k + 1) * P], ident[:, :])
                last.then_inc(sem("zt_mm"), 1)

            def step(n):
                nxt, cur, tail = Row(n, 1), Row(n, 0), Row(n, -LAG)
                if nxt.live:
                    fwd(nxt, 0)
                if tail.live and tail.b < B - 1:
                    turn(tail)
                if nxt.live:
                    fwd(nxt, 1)
                if cur.live:
                    inverse(cur, 0)
                if tail.live:
                    pe.wait_ge(sem("zt_ready"), 2 * tail.b + 2)
                    for q in range(4):
                        for k in range(2):
                            last = TE.matmul(route(tail.b)[1][:, q * E:(q + 1) * E], zt[:, k, q * P:(q + 1) * P], rw_sb[:, k, :],
                                             start=k == 0, stop=k == 1)
                    last.then_inc(sem("lg_mm"), 1)
                if cur.live:
                    inverse(cur, 1)
                if n == B + 1:
                    turn(Row(n, -2))
                if tail.live:
                    pe.wait_ge(sem("mask_ready"), tail.b + 1)
                    rank = route(tail.b)[1][:, 64:96]
                    m = mask[:, :, :].rearrange("p t e -> p (t e)")
                    TE.matmul(rank, upper[:, 0, :], m, start=True, stop=False)
                    for q in range(1, 4):
                        TE.matmul(rank[:, q * E:4 * E], upper[:, 1, :], m[:, 0:(4 - q) * E], start=False, stop=False)
                    if not tail.first():
                        pe.wait_ge(sem("carry_ready"), tail.b)
                    TE.matmul(rank.rearrange("p (t e) -> p t e", t=4), upper[:, 1, :],
                              carry_b[:, :].unsqueeze(1).to_broadcast([P, 4, E]), start=False,
                              stop=True).then_inc(sem("rank_mm"), 1)

            step(-2)
            steps(step)
            pe.wait_ge(sem("pos_ready"), B)
            pe.wait_ge(sem("carry_ready"), B)
            TE.matmul(tp[1][:, 0:E], upper[:, 1, :], carry_b[:, :], start=True, stop=True).then_inc(sem("cnt_mm"), 1)

            def part(i, par, u):
                e1 = expert(pe, i + 1, u + 1) if live(i + 1) else 0
                e2 = expert(pe, i - 1, u - 1) if live(i - 1) else 0
                t, q = i + 2, par
                if live(t):
                    pe.wait_ge(sem(f"z_in{q}"), (t - q) * 8 + 16)
                    if not early(t, 2):
                        pe.wait_ge(sem("zf_ready"), t - 1)
                    for k in range(2):
                        last = TE.transpose(ps_z[q][:, k], z_in[q][:, k * P:(k + 1) * P], ident[:, :])
                    last.then_inc(sem("tz_mm"), 1)
                t, q = i + 1, 1 - par
                if live(t):
                    if early(t):
                        pe.wait_ge(sem("w_low"), E)
                    pe.wait_ge(sem("z_split"), t + 1)
                    if not early(t, 2):
                        pe.wait_ge(sem("hb_ready"), t - 1)
                    n = 0
                    for k in range(2):
                        for a, c in ((0, 0), (0, 1), (1, 0)):
                            last = TE.matmul(ps_h[q], z_hl[q][:, a, k], w_at(e1, c, k * F, F), start=n == 0, stop=n == 5)
                            n += 1
                    last.then_inc(sem("l1_mm"), 1)
                t, q = i, par
                if live(t):
                    pe.wait_ge(sem("hg_ready"), t + 1)
                    if not early(t, 2):
                        pe.wait_ge(sem("h_split"), t - 1)
                    for k in range(4):
                        last = TE.transpose(ps_t[q][:, k], hg[q][:, k * P:(k + 1) * P], ident[:, :])
                    last.then_inc(sem("th_mm"), 1)
                t, q = i - 1, 1 - par
                if live(t):
                    pe.wait_ge(sem("h_split"), t + 1)
                    if not early(t, 2):
                        pe.wait_ge(sem("y_ready"), t - 1)
                    n = 0
                    for k in range(4):
                        for a, c in ((0, 0), (0, 1), (1, 0)):
                            last = TE.matmul(ps_y[q], h_hl[q][:, a, k], w_at(e2, c, 1024 + k * H, H), start=n == 0, stop=n == 11)
                            n += 1
                    last.then_inc(sem("l2_mm"), 1)

            pe.wait_ge(sem("tab_ready"), 1)
            tiles(pe, part)


MAGS = (QN, 0, PN)
SINES = (QN + PN, QN, 0, PN)
HIGH = {3: (0,), 4: (1,), 5: (2,), 6: (3,), 7: (4,), 9: (5,), 10: (6,)}
LOW = {9: (1,), 10: (2,), B + LAG: (4, 5, 6, 7)}
LOW_POOL = {9: (0,), B + LAG: (3,)}
USES = ("st_x", "st_o", "o_norm", "st_x1")


def consts():
    import numpy as np
    t = np.arange(T // 2)
    k = np.arange(T)
    ang = np.pi / 2048 * (((2 * k[None, :] + 1) * (2 * t[:, None] - 511)) % 4096)
    f = np.stack([np.cos(ang), -np.sin(ang)])
    fwd = f.reshape(2, 2, P, T).transpose(2, 0, 1, 3)
    inv = (f / T).transpose(0, 2, 1).reshape(2, KT, P, T // 2).transpose(2, 0, 1, 3)
    l = np.arange(T)
    a2 = np.pi / 1024 * (((2 * k[None, :] + 1) * l[:, None]) % 2048)
    g = np.stack([np.cos(a2), -np.sin(a2)])
    lag = g.reshape(2, KT, P, KT, P).transpose(2, 1, 0, 3, 4).reshape(P, KT, 2 * KT, P)
    s = np.concatenate([np.arange(QN), QN * np.arange(PN), QN * np.arange(PN)])
    scale = np.broadcast_to(s, (P, SLOTS))
    off = np.zeros((P, SLOTS))
    off[:N, :QN], off[N:, :QN] = .25, 0
    off[:N, QN:QN + PN], off[N:, QN:QN + PN] = .25, .5
    off[:N, QN + PN:], off[N:, QN + PN:] = .5, .75
    up = np.stack([np.triu(np.ones((P, P)), 1), np.ones((P, P))], 1)
    nt = TILES + 1
    tile = np.concatenate([np.tile(np.concatenate([np.tril(np.ones((E, E))).ravel(), np.arange(nt), P * np.arange(nt)]),
                                   (P, 1)), np.arange(P * B * 4).reshape(P, B * 4)], 1)
    return [np.ascontiguousarray(a, dtype=np.float32) for a in (fwd, inv, lag, scale, off, np.eye(P), up, tile)]


_INS = ["log_A_real", "A_imag", "C_re", "C_im", "log_dt", "D", "ln_w", "ln_b"]
_FFN = ["ln_g", "ln_b", "rW", "rb", "W1", "b1", "W2", "b2"]


def kernel(**inputs):
    import numpy as np
    import concourse.bacc as bacc
    from concourse.bass_utils import run_bass_kernel_spmd

    x = np.asarray(inputs["L0_attn_x"])
    half = [x[:, :T // 2], x[:, :T // 2 - 1:-1]]
    x = np.concatenate([a.reshape(B, 2, P, H) for a in half], 1).transpose(2, 0, 1, 3)
    arrays = [x, *consts()]
    arrays += [inputs[f"L0_attn_{n}"] for n in _INS] + [inputs[f"L0_ffn_{n}"] for n in _FFN]
    nc = bacc.Bacc("TRN2", target_bir_lowering=False, num_devices=1)
    given, args = {}, []
    for i, a in enumerate(arrays):
        name = f"in_{i}_dram"
        given[name] = np.ascontiguousarray(a)
        args.append(nc.dram_tensor(name, given[name].shape, mybir.dt.from_np(given[name].dtype), kind="ExternalInput").ap())
    out = nc.dram_tensor("out_dram", (P, B, 4, H), F32, kind="ExternalOutput").ap()
    program(nc, *args, out)
    r = run_bass_kernel_spmd(nc, [given], core_ids=[0])
    y = r.results[0]["out_dram"].transpose(1, 2, 0, 3)
    return np.concatenate([y[:, :2].reshape(B, T // 2, H), y[:, 2:].reshape(B, T // 2, H)[:, ::-1]], 1)
```

```python
import concourse.bass as bass
from concourse import mybir
from concourse.alu_op_type import AluOpType as ALU

F32 = mybir.dt.float32
F32R = mybir.dt.float32r
BF16 = mybir.dt.bfloat16
I32 = mybir.dt.int32
U32 = mybir.dt.uint32
ACT = mybir.ActivationFunctionType
AX = mybir.AxisListType

P = 128
B, T, H, N = 8, 512, 256, 64
E, F = 8, 512
EPS = 1e-5
KT = T // P
QN, PN = 32, 16
SLOTS = QN + 2 * PN
REGION = B * T + P
LAG = 3
TILES = 2 * B * T // P + E - 1
ROWS = E * REGION
ROUND = 12582912.0
TURN = 6.283185
W = H + 2
TRASH = 2 * B * T
UNROLL = 6
KB = 1024
BASE = 16512


class Seq:

    def __init__(self, eng, sem):
        self.eng, self.sem, self.n = eng, sem, 0

    def inc(self, ins):
        ins.then_inc(self.sem, 1)
        self.n += 1

    def wait(self):
        self.eng.wait_ge(self.sem, self.n)


TAB = E * E + 2 * (TILES + 1)


def program(nc, x, fwd_tab, inv_tab, lag_tab, slot_scale, slot_off, ident_in, upper_in, tile_tab, lar, aim, cre, cim,
            ldt, d_skip, ln_w, ln_b, ffn_g, ffn_b, r_w, r_b, w1, b1, w2, b2, out):
    sems = {}

    def sem(name):
        if name not in sems:
            sems[name] = nc.alloc_semaphore(name)
        return sems[name]

    def at(name, shape, dt, off):
        return nc.alloc_sbuf_tensor_at(name, shape, dt, offset=BASE + off)

    v = at("v", [P, SLOTS, H], F32, 0)
    mag_p = at("mag_p", [P, PN, H], F32, 64 * KB)
    mag_q = at("mag_q", [P, QN, H], F32, 96 * KB)
    mag = {QN: mag_p[:, :, :], 0: mag_q[:, 0:PN], PN: mag_q[:, PN:QN]}
    xs = [at(f"xs{b}", [P, 4, H], F32, k * KB) for b, k in enumerate((80, 84, 88, 92, 96, 100, 112, 116))]
    kf = at("kf", [P, 2, KT, H], F32, 104 * KB)
    zn = [at(f"zn{i}", [P, 4, W], F32, 120 * KB + 4 * i * 4 * W) for i in range(2)]
    o0 = 128 * KB + 64
    zn += [at(f"zn{i}", [P, 4, W], F32, o0 + 4 * (i - 2) * 4 * W) for i in (2, 3)]
    xn = at("xn", [P, 4, H], F32, o0)
    pm = [at(f"pm{i}", [P, 2, 2, H], F32, o0 + (4 + 4 * i) * KB) for i in range(2)]
    ft = at("ft", [P, 2, 2, T], F32, o0 + 12 * KB)
    it = at("it", [P, 2, KT, 2 * P], F32, o0 + 20 * KB)
    yf = [at(f"yf{i}", [P, 2, KT, H], F32, o0 + (28 + 8 * i) * KB) for i in range(2)]
    lag = at("lag", [P, KT, 2 * KT, P], F32, 64 * KB)
    tmp = [at(f"tmp{i}", [P, 2, 2, H], F32, o0 + (44 + 4 * i) * KB) for i in range(2)]
    s_sb = at("s_sb", [P, 2, H], F32, o0 + 52 * KB)
    r = at("r", [P, 4, H], F32, o0 + 54 * KB)
    o = at("o", [P, 4, H], F32, o0 + 58 * KB)
    dl = at("dl", [P, 4, H], F32, o0 + 62 * KB)
    zt = at("zt", [P, 2, T], F32, o0 + 66 * KB)
    lwb = at("lwb", [P, 2, H], F32, o0 + 70 * KB)
    k_sb = at("k_sb", [P, 64 * QN], F32, o0 + 44 * KB)
    kh = at("kh", [P, 2, T], F32, o0 + 54 * KB)
    k_t = at("k_t", [P, KT, H], F32, o0 + 58 * KB)
    sm = at("sm", [P, 8, 2, N], F32, o0 + 62 * KB)
    quant = at("quant", [P, 4, 2, 2, N], F32, o0 + 66 * KB)
    sm2 = at("sm2", [P, 14, 2, N], F32, 80 * KB)
    kr = [at(f"kr{i}", [P, PN, H], F32, k) for i, k in enumerate((80 * KB, o0 + 12 * KB))]
    qt = at("qt", [P, 4, H], F32, o0 + 0 * KB)
    raw = at("raw", [P, 4, 2, N], F32, o0 + 4 * KB)
    c0 = o0 + 73 * KB
    ident = at("ident", [P, P], F32, c0)
    upper = at("upper", [P, 2, P], BF16, c0 + 512)
    upper_f = at("upper_f", [P, 2, P], F32, o0 + 58 * KB)
    sc = at("sc", [P, SLOTS], F32, c0 + 1024)
    so = at("so", [P, SLOTS], F32, c0 + 1280)
    dtv = at("dtv", [P, 2, 2], F32, c0 + 1536)
    st = at("st", [P, 4, 4, 6], F32, c0 + 5568)
    mv = [at(f"mv{i}", [P, 4, 2], F32, c0 + 1664 + 32 * i) for i in range(4)]
    sd = at("sd", [P, 4, 4], F32, c0 + 1792)
    eps = at("eps", [P, 2], F32, c0 + 1856)
    rs = at("rs", [P, 4, 8], F32, c0 + 1920)
    gb = at("gb", [P, 2, 2], F32, c0 + 2048)
    rw_sb = at("rw_sb", [P, 2, E], F32, c0 + 2080)
    rb_sb = at("rb_sb", [P, E], F32, c0 + 2144)
    mi = at("mi", [P, 4, 8], U32, c0 + 2304)
    mif = at("mif", [P, 2, 4], F32, c0 + 2432)
    oh = at("oh", [P, 2, 4, E], F32, c0 + 2464)
    mask = at("mask", [P, 4, E], BF16, c0 + 2720)
    msum = at("msum", [P, E], F32, c0 + 2784)
    carry = at("carry", [P, E], F32, c0 + 2816)
    carry_b = at("carry_b", [P, E], BF16, c0 + 2848)
    posf = at("posf", [P, 4, E], F32, c0 + 2880)
    prod = at("prod", [P, 2, 4, E], F32, c0 + 3008)
    posr = at("posr", [P, 2, 4], F32, c0 + 3264)
    pos = [at(f"pos{i}", [P, 2, 4], U32, c0 + 3296 + 32 * i) for i in range(2)]
    iota8 = at("iota8", [P, 2, E], F32, c0 + 3360)
    lgs = at("lgs", [P, 4, E], F32, c0 + 3424)
    tok = at("tok", [P, B, 4], F32, c0 + 3552)
    stat1 = at("stat1", [P, B, 2, 4], F32, c0 + 3680)
    mx_all = at("mx_all", [P, B, 4, E], F32, c0 + 3936)
    tab = at("tab", [1, 2, TILES + 1], I32, c0 + 4960)
    d_rep = at("d_rep", [P, H], F32, o0 + 72 * KB)
    tab_e = at("tab_e", [P, TILES + 1], F32, c0 + 5952)
    dest = at("dest", [P, TILES + 1], U32, c0 + 6240)
    dst = [at(f"dst{i}", [P, 1], U32, c0 + 6528 + 32 * i) for i in range(2)]
    flag = at("flag", [P, 1], F32, c0 + 6592)
    ws = at("ws", [P, E, 2, 2048], F32R, 0)
    w_raw = [at(f"w_raw{e}", [P, 2048], F32, (16 * e + 8) * KB) for e in range(E)]
    x1m = at("x1m", [P, B, 4, H], F32, 112 * KB + 64)
    b2r = at("b2r", [P, E, H], F32, o0 + 16 * KB)
    z_in = [at(f"z_in{i}", [P, W], F32, o0 + 24 * KB + 1056 * i) for i in range(2)]
    z_f = at("z_f", [P, 2, P], F32, o0 + 27 * KB)
    b1r = at("b1r", [P, E, F], F32, o0 + 28 * KB)
    y_sb = [at(f"y_sb{i}", [P, H], F32, o0 + (44 + i) * KB) for i in range(2)]
    hb = at("hb", [P, F], F32, o0 + 46 * KB)
    z_hl = [at(f"z_hl{i}", [P, 2, 2, P], F32R, o0 + (53 + 2 * i) * KB) for i in range(2)]
    hg = [at(f"hg{i}", [P, F], F32, o0 + (57 + 2 * i) * KB) for i in range(2)]
    h_hl = [at(f"h_hl{i}", [P, 2, 4, P], F32R, o0 + (61 + 4 * i) * KB) for i in range(2)]
    m0 = o0 + 48 * KB
    cnt = at("cnt", [P, 8, E], F32, m0)
    tri = at("tri", [P, E, E], F32, m0 + 256)
    padi = at("padi", [1, E], I32, m0 + 512)
    padf = at("padf", [1, E], F32, m0 + 544)
    rm = at("rm", [P, 2, 4, 4], F32, m0 + 576)
    mvm = [at(f"mvm{i}", [P, 4, 2], F32, m0 + 704 + 32 * i) for i in range(2)]
    wsm = at("wsm", [P, B, 4, E], F32, m0 + KB)
    wgt = at("wgt", [P, 4, B, 4], F32, m0 + 2 * KB)
    rsm = at("rsm", [P, 4, B, 4], F32, m0 + 2 * KB + 512)
    zpad = at("zpad", [P, W], F32, m0 + 3 * KB)
    cmp_t = at("cmp_t", [P, TILES + 1, E], F32, o0 + 57 * KB)
    cmp_n = at("cmp_n", [P, TILES + 1, E], F32, o0 + 60 * KB)
    tf = at("tf", [P, 3, TILES + 1], F32, o0 + 63 * KB)
    iot = at("iot", [P, 2, TILES + 1], F32, o0 + 65 * KB)
    ya = at("ya", [P, B, 2, 4, H], F32, 0)
    diag = [at(f"diag{i}", [P, 2, 4, P], F32, o0 + (28 + 4 * i) * KB) for i in range(2)]
    acc = at("acc", [P, B, 4, H], F32, 64 * KB)
    psum = nc.alloc_psum_tensor("psum", [P, 8 * 512], F32)

    def bank(n, w=1):
        return psum[:, 512 * n:512 * (n + w)]

    fw = [[bank(2 * i + c).rearrange("p (k h) -> p k h", k=2) for c in range(2)] for i in range(2)]
    iv = [bank(4 + c) for c in range(2)]
    tp = [bank(6), bank(7)]
    tp_last = {B - 2: [bank(2), bank(3)], B - 1: [bank(0), bank(1)]}

    ps_z = [bank(7 * i)[:, 0:256].rearrange("p (k t) -> p k t", k=2) for i in range(2)]
    ps_h = [bank(1 + i) for i in range(2)]
    ps_t = [bank(3 + i).rearrange("p (k t) -> p k t", k=4) for i in range(2)]
    ps_y = [bank(5 + i)[:, 0:H] for i in range(2)]

    def w_at(e, c, at_, n):
        return ws[:, bass.ds(e, 1), c, at_:at_ + n].rearrange("p a n -> p (a n)")

    k_dram = nc.dram_tensor("k_dram", [4, PN, 64 * QN], F32, kind="Internal").ap()
    z_rows = nc.dram_tensor("z_rows", [ROWS, W], F32, kind="Internal").ap()
    y_rows = nc.dram_tensor("y_rows", [TRASH + P, H], F32, kind="Internal").ap()
    x1_dram = nc.dram_tensor("x1_dram", [P, B, 4, H], F32, kind="Internal").ap()

    def rep(a, parts=P):
        return bass.AP(a.tensor, a.offset, [[0, parts]] + [list(q) for q in a.ap])

    def hn(a):
        return a.rearrange("(t p) n -> p t n", p=P)

    def steps(step):
        for n in range(-1, B + LAG):
            step(n)

    def gate(eng):
        eng.sem_inc(sem(f"gate_{eng.engine.name}"), 1)

    class Row:

        def __init__(self, n, k):
            self.b, self.live, self.par = n + k, 0 <= n + k < B, (n + k) % 2

        def first(self, n=1):
            return self.b < n

    loaded = {}

    def tiles(eng, part):
        loaded[eng.engine.name] = {}
        for i in range(-2, 3):
            part(i, i % 2, i)
        with eng.Fori(0, (TILES - 5) // UNROLL) as j:
            loaded[eng.engine.name] = {}
            for u in range(UNROLL):
                part(j * UNROLL + (3 + u), (1 + u) % 2, u)
        loaded[eng.engine.name] = {}
        for i in range(TILES - 2, TILES + 1):
            part(i, i % 2, i)

    def load_expert(eng, e):
        eng.dma_start(w_raw[e][:, 0:1024].rearrange("p (k f) -> p k f", k=2),
                      w1[e].rearrange("(k p) f -> p k f", p=P)).then_inc(sem(f"in_w{e}"), 16)
        eng.dma_start(w_raw[e][:, 1024:2048].rearrange("p (k f) -> p k f", k=4),
                      w2[e].rearrange("(k p) f -> p k f", p=P)).then_inc(sem(f"in_w{e}"), 16)

    def back(n):
        return n * -1 + (B - 1)

    ps_mix = [bank(2 * i, 2) for i in range(2)]

    def route(b):
        return tp_last.get(b, tp)

    def buf(b):
        return b % 2 if b < 6 else b - 4

    def live(t):
        return not isinstance(t, int) or 0 <= t < TILES

    def expert(eng, t, u):
        if u not in loaded[eng.engine.name]:
            loaded[eng.engine.name][u] = eng.value_load(tab[0:1, 1, bass.ds(t, 1)], min_val=0, max_val=E - 1)
        return loaded[eng.engine.name][u]

    def early(t, n=1):
        return isinstance(t, int) and t < n

    with nc.Block() as block:

        @block.sync
        def _(sp):
            sp.dma_start(dtv[:, 0, :], ldt.rearrange("(t p) -> p t", p=P),
                         allow_slow_non_contiguous=True).then_inc(sem("in_modes"), 16)
            sp.dma_start(raw[:, 0], hn(lar)).then_inc(sem("in_modes"), 16)
            sp.dma_start(raw[:, 1], hn(aim)).then_inc(sem("in_modes"), 16)
            sp.dma_start(ident[:, :], ident_in).then_inc(sem("in_modes"), 16)
            sp.dma_start(so[:, :], slot_off).then_inc(sem("in_slots"), 16)
            sp.dma_start(sc[:, :], slot_scale).then_inc(sem("in_slots"), 16)
            sp.dma_start(raw[:, 2], hn(cre)).then_inc(sem("in_coef"), 16)
            sp.dma_start(raw[:, 3], hn(cim)).then_inc(sem("in_coef"), 16)
            sp.dma_start(upper_f[:, :, :], upper_in).then_inc(sem("in_upper"), 16)
            sp.dma_start(d_rep[:, :], rep(d_skip)).then_inc(sem("in_small"), 16)
            sp.dma_start(lwb[:, 0, :], rep(ln_w)).then_inc(sem("in_small"), 16)
            sp.dma_start(lwb[:, 1, :], rep(ln_b)).then_inc(sem("in_small"), 16)
            sp.dma_start(gb[:, 0, :], ffn_g.rearrange("(t p) -> p t", p=P),
                         allow_slow_non_contiguous=True).then_inc(sem("in_small"), 16)
            sp.dma_start(gb[:, 1, :], ffn_b.rearrange("(t p) -> p t", p=P),
                         allow_slow_non_contiguous=True).then_inc(sem("in_small"), 16)
            sp.dma_start(rw_sb[:, :, :], r_w.rearrange("(t p) e -> p t e", p=P)).then_inc(sem("in_small"), 16)
            sp.dma_start(rb_sb[:, :], rep(r_b)).then_inc(sem("in_small"), 16)
            sp.dma_start(tok[:, :, :], tile_tab[:, TAB:].rearrange("p (b k) -> p b k", b=B)).then_inc(sem("in_small"), 16)
            sp.wait_ge(sem("k_frac0"), 1)
            for b in (0, 1):
                sp.dma_start(xs[b][:, :, :], x[:, b]).then_inc(sem("in_x"), 16)
            sp.wait_ge(sem(f"k_frac{PN}"), 1)
            sp.wait_ge(sem(f"k_frac{QN + PN}"), 1)
            sp.dma_start(ft[:, :, :, :], fwd_tab).then_inc(sem("in_tab"), 16)
            sp.dma_start(it[:, :, :, :], inv_tab).then_inc(sem("in_tab"), 16)
            for b in (2, 3):
                sp.dma_start(xs[b][:, :, :], x[:, b]).then_inc(sem("in_x2"), 16)
            sp.wait_ge(sem("k_pf"), 2)
            sp.dma_start(lag[:, :, :, :], lag_tab).then_inc(sem("in_lag"), 16)
            sp.wait_ge(sem("k_qf"), 2)
            sp.wait_ge(sem("k_in0"), 32)
            sp.wait_ge(sem("k_in1"), 32)
            for b in range(4, B):
                sp.dma_start(xs[b][:, :, :], x[:, b]).then_inc(sem("in_x2"), 16)
            sp.wait_ge(sem("k_mm"), 2)
            for e in range(5):
                if e == 4:
                    sp.wait_ge(sem("kf_mm"), 2)
                load_expert(sp, e)

            def store_x1(lo, hi):
                for b in range(lo, hi):
                    sp.wait_ge(sem("x1_ready"), b + 1)
                    sp.dma_start(x1_dram[:, b], xs[b][:, :, :]).then_inc(sem("x1_stored"), 16)
                sp.wait_ge(sem("x1_stored"), 16 * hi)

            store_x1(0, 4)
            sp.wait_ge(sem("zn_ready"), 4)
            load_expert(sp, 5)
            store_x1(4, 6)
            sp.wait_ge(sem("zn_ready"), 6)
            sp.wait_ge(sem("mult_done"), 2 * B)
            load_expert(sp, 6)
            sp.wait_ge(sem("inv_mm"), B)
            for e in range(E):
                sp.dma_start(b1r[:, e], rep(b1[e])).then_inc(sem("in_b"), 16)
            for e in range(E):
                sp.dma_start(b2r[:, e], rep(b2[e])).then_inc(sem("in_b"), 16)
            store_x1(6, 8)
            sp.wait_ge(sem("zn_ready"), B)
            sp.wait_ge(sem("x1_ready"), B)
            sp.dma_start(tri[:, :, :], tile_tab[:, 0:E * E].rearrange("p (a b) -> p a b", a=E)).then_inc(sem("in_e"), 16)
            sp.dma_start(iot[:, :, :], tile_tab[:, E * E:TAB].rearrange("p (a b) -> p a b", a=2)).then_inc(sem("in_e"), 16)
            for par in range(2):
                sp.wait_ge(sem(f"scattered{par}"), 64 * 6)
            load_expert(sp, 7)
            sp.wait_ge(sem("pad_set"), 1)
            behind = [sp.value_load(padi[0:1, e:e + 1], min_val=0, max_val=ROWS - P) for e in range(E)]
            for i in (2, 3):
                sp.wait_ge(sem(f"scattered{i}"), 128)
            for e in range(E):
                sp.dma_start(z_rows[bass.ds(behind[e], P), :], zpad[:, :]).then_inc(sem("pads"), 16)

            def load_z(t, par):
                row = sp.value_load(tab[0:1, 0, bass.ds(t, 1)], min_val=0, max_val=ROWS - P)
                if not (isinstance(t, int) and t < 2):
                    sp.wait_ge(sem("tz_mm"), t - 1)
                    sp.wait_ge(sem("dest_ready"), t - 1)
                sp.dma_start(z_in[par][:, :], z_rows[bass.ds(row, P), :]).then_inc(sem(f"z_in{par}"), 16)

            sp.wait_ge(sem("tab_ready"), 1)
            sp.wait_ge(sem("pads"), 16 * E)
            load_z(0, 0)
            load_z(1, 1)
            sp.dma_start(x1m[:, 4:8], x1_dram[:, 4:8]).then_inc(sem("x1_in"), 16)
            with sp.Fori(0, (TILES - 3) // 2) as j:
                load_z(j * 2 + 2, 0)
                load_z(j * 2 + 3, 1)
            load_z(TILES - 1, 0)

            sp.wait_ge(sem("l2_mm"), TILES)
            sp.wait_ge(sem("x1_in"), 16)
            sp.wait_ge(sem("y_out0"), 16 * ((TILES + 1) // 2))
            sp.wait_ge(sem("y_out1"), 16 * (TILES // 2))
            y_tok = y_rows[0:TRASH, :].rearrange("(c p b k) h -> p b c (k h)", c=2, b=B, k=4)
            for n in range(B):
                if n >= 2:
                    sp.wait_ge(sem(f"y0_in{n % 2}"), 16 * (n // 2))
                    sp.wait_ge(sem(f"y1_in{n % 2}"), 16 * (n // 2))
                if n == 3:
                    sp.dma_start(x1m[:, 0:4], x1_dram[:, 0:4]).then_inc(sem("x1_in"), 16)
                for c in (1, 0):
                    sp.dma_start(ya[:, n, c], y_tok[:, B - 1 - n, c].rearrange("p (k h) -> p k h", k=4)).then_inc(
                        sem(f"y{c}_in{n % 2}"), 16)
            for n in range(B):
                sp.wait_ge(sem("m_out"), n + 1)
                sp.dma_start(out[:, B - 1 - n], acc[:, n]).then_inc(sem("stored"), 16)
            sp.wait_ge(sem("stored"), 16 * B)

        @block.scalar
        def _(act):
            seq = Seq(act, sem("act_seq"))
            def sigma(row, slot):
                act.wait_ge(sem(f"var{slot}"), row.b + 1)
                if not row.first():
                    act.wait_ge(sem(USES[slot]), row.b)
                nc.scalar.activation(sd[:, slot, :], mv[slot][:, :, 1], ACT.Sqrt, bias=eps[:, slot // 3:slot // 3 + 1],
                                     scale=1.0 + EPS if slot == 3 else 1.0).then_inc(sem(f"sd{slot}"), 1)

            def normalise(new):
                act.wait_ge(sem("st_x"), new.b + 1)
                if not new.first():
                    act.wait_ge(sem("pm_ready"), 2 * new.b)
                for k in range(4):
                    last = nc.scalar.activation(xn[:, k], xs[new.b][:, k], ACT.Identity, bias=rs[:, 0, 4 + k:5 + k],
                                                scale=rs[:, 0, k:k + 1])
                last.then_inc(sem("xn_ready"), 1)

            act.wait_ge(sem("in_modes"), 64)
            nc.scalar.activation(dtv[:, 1, :], dtv[:, 0, :], ACT.Exp)
            nc.scalar.activation(sm[:, 0], raw[:, 0], ACT.Exp).then_inc(sem("k_exp"), 1)
            act.wait_ge(sem("k_ua"), 1)
            nc.scalar.activation(sm[:, 1], quant[:, 1, :, 0, :], ACT.Tanh, scale=0.5).then_inc(sem("k_tanh"), 1)
            act.wait_ge(sem("k_half"), 1)
            nc.scalar.activation(sm[:, 4:6], sm[:, 2:4], ACT.Sin, scale=TURN).then_inc(sem("k_trig"), 1)
            act.wait_ge(sem("k_tr"), 1)
            nc.scalar.copy(qt[:, 0:2], bank(0).rearrange("p (q h) -> p q h", q=2)).then_inc(sem("k_qt"), 1)
            act.wait_ge(sem("k_qt"), 1)
            act.wait_ge(sem("in_slots"), 32)
            for q in range(QN):
                last = nc.scalar.activation(v[:, q], qt[:, 0], ACT.Identity, bias=so[:, 0:1], scale=float(q))
                if q % PN == PN - 1:
                    last.then_inc(sem("k_turned"), 1)
            for u, g in enumerate(MAGS):
                if g == 0:
                    for q in range(PN):
                        last = nc.scalar.activation(mag_q[:, q], qt[:, 1], ACT.Exp, scale=float(q))
                else:
                    act.wait_ge(sem("k_aq"), 1 + u // 2)
                    last = nc.scalar.activation(mag[g], mag[g], ACT.Exp)
                last.then_inc(sem("k_mag"), 1)
            for g in SINES:
                act.wait_ge(sem(f"k_frac{g}"), 1)
                nc.scalar.activation(v[:, g:g + PN], v[:, g:g + PN], ACT.Sin, scale=TURN).then_inc(sem("k_sin"), 1)
            act.wait_ge(sem("one"), 1)
            sigma(Row(-2, 2), 0)
            normalise(Row(-2, 2))
            for ht in range(2):
                act.wait_ge(sem("k_mm"), ht + 1)
                for j in (2 * ht, 2 * ht + 1):
                    nc.scalar.copy(k_sb[32 * j:32 * j + PN, :],
                                   psum[32 * j:32 * j + PN, 4 * 512:8 * 512]).then_inc(sem("k_evac"), 1)
                act.wait_ge(sem("k_evac"), 2 * ht + 2)
                for j in (2 * ht, 2 * ht + 1):
                    act.dma_start(k_dram[j], k_sb[32 * j:32 * j + PN, :]).then_inc(sem(f"k_out{ht}"), 16)
            sigma(Row(-1, 2), 0)
            normalise(Row(-1, 2))
            for ht in range(2):
                act.wait_ge(sem(f"k_out{ht}"), 32)
                for j in (2 * ht, 2 * ht + 1):
                    act.dma_start(kh[64 * (j % 2):64 * (j % 2) + 64, ht, :].rearrange("h (p q) -> h p q", p=PN),
                                  k_dram[j].rearrange("p (h q) -> h p q", q=QN)).then_inc(sem(f"k_in{ht}"), 16)
            act.wait_ge(sem("upper_set"), 1)
            act.wait_ge(sem("in_small"), 128)
            for ht in range(2):
                act.wait_ge(sem("kt_mm"), ht + 1)
                nc.scalar.copy(k_t[:, :, ht * P:ht * P + P],
                               tp[ht].rearrange("p (l h) -> p l h", l=KT)).then_inc(sem("kt_evac"), 1)

            def renormalise(mid):
                sigma(mid, 3)
                act.wait_ge(sem("st_x1"), mid.b + 1)
                if 2 <= mid.b < 6:
                    act.wait_ge(sem(f"scattered{mid.par}"), 64 * (mid.b - mid.par))
                elif mid.b == 6:
                    act.wait_ge(sem("fwd_mm"), 2 * B)
                for k in range(4):
                    last = nc.scalar.activation(zn[buf(mid.b)][:, k, 0:H], xs[mid.b][:, k],
                                                ACT.Identity, bias=rs[:, 3, 4 + k:5 + k], scale=rs[:, 3, k:k + 1])
                last.then_inc(sem("zn_ready"), 1)

            def split_high(e):
                act.wait_ge(sem(f"in_w{e}"), 32)
                nc.scalar.copy(ws[:, e, 0], w_raw[e][:, :]).then_inc(sem("w_high"), 1)

            def step(n):
                new, inv, cur, mid, tail = (Row(n, k) for k in (2, 0, -1, -2, -LAG))
                if cur.live:
                    sigma(cur, 2)
                if new.live and new.b > 1:
                    sigma(new, 0)
                if cur.live:
                    act.wait_ge(sem("st_r"), cur.b + 1)
                    for k in range(4):
                        last = nc.scalar.activation(r[:, k], r[:, k], ACT.Identity, bias=rs[:, 2, 4 + k:5 + k],
                                                    scale=rs[:, 2, k:k + 1])
                    last.then_inc(sem("r_norm"), 1)
                if tail.live:
                    act.wait_ge(sem("zt_mm"), tail.b + 1)
                    if not tail.first():
                        act.wait_ge(sem("lg_mm"), tail.b)
                    for k in range(2):
                        nc.scalar.activation(zt[:, k, :], route(tail.b)[k], ACT.Identity, bias=gb[:, 1, k:k + 1],
                                             scale=gb[:, 0, k:k + 1]).then_inc(sem("zt_ready"), 1)
                if new.live and new.b > 1:
                    normalise(new)
                if n == B:
                    renormalise(mid)
                if cur.live:
                    sigma(cur, 1)
                    act.wait_ge(sem("st_o"), cur.b + 1)
                    if not cur.first():
                        act.wait_ge(sem("x1_ready"), cur.b)
                    for k in range(4):
                        last = nc.scalar.activation(dl[:, k], o[:, k], ACT.Identity, bias=rs[:, 1, 4 + k:5 + k],
                                                    scale=rs[:, 1, k:k + 1])
                    last.then_inc(sem("dl_ready"), 1)
                if inv.live:
                    act.wait_ge(sem("inv_mm"), inv.b + 1)
                    if not inv.first():
                        act.wait_ge(sem("r_ready"), inv.b)
                    nc.scalar.copy(s_sb[:, :, :], iv[1].rearrange("p (j h) -> p j h", j=2)).then_inc(sem("s_copied"), 1)
                if mid.live and n != B:
                    renormalise(mid)
                for e in HIGH.get(n, ()):
                    split_high(e)

            for u in range(2):
                act.wait_ge(sem("kf_mm"), u + 1)
                nc.scalar.copy(kf[:, 1, 2 * u:2 * u + 2],
                               bank(6 + u).rearrange("p (k h) -> p k h", k=2)).then_inc(sem(f"kf_ready{u}"), 1)
            steps(step)

            act.wait_ge(sem("pad_set"), 1)
            nc.scalar.activation(rsm[:, 0], stat1[:, :, 1, :], ACT.Sqrt, bias=eps[:, 0:1]).then_inc(sem("rsm_sd"), 1)
            split_high(E - 1)
            act.wait_ge(sem("wsm_sub"), 1)
            nc.scalar.activation(wsm[:, :, :, :], wsm[:, :, :, :], ACT.Exp).then_inc(sem("wsm_exp"), 1)

            def part(i, par, u):
                t, q = i + 2, par
                if live(t):
                    act.wait_ge(sem("tz_mm"), t + 1)
                    if not early(t):
                        act.wait_ge(sem("z_split"), t)
                    for k in range(2):
                        last = nc.scalar.activation(z_f[:, k], ps_z[q][:, k], ACT.Identity, bias=gb[:, 1, k:k + 1],
                                                    scale=gb[:, 0, k:k + 1])
                    last.then_inc(sem("zf_ready"), 1)
                t, q = i, par
                if live(t):
                    act.wait_ge(sem("th_mm"), t + 1)
                    if not early(t, 2):
                        act.wait_ge(sem("l2_mm"), t - 1)
                    nc.scalar.copy(h_hl[q][:, 0], ps_t[q]).then_inc(sem("h_high"), 1)
                t, q = i + 1, 1 - par
                if live(t):
                    act.wait_ge(sem("hb_ready"), t + 1)
                    if not early(t, 2):
                        act.wait_ge(sem("th_mm"), t - 1)
                    nc.scalar.activation(hg[q][:, :], hb[:, :], ACT.Gelu).then_inc(sem("hg_ready"), 1)

            tiles(act, part)

            def base(n):
                b = back(n)
                for k in range(4):
                    last = nc.scalar.activation(acc[:, bass.ds(n, 1), k].rearrange("p a h -> p (a h)"),
                                                x1m[:, bass.ds(b, 1), k].rearrange("p a h -> p (a h)"), ACT.Identity,
                                                bias=rsm[:, 1, bass.ds(b, 1), k], scale=rsm[:, 0, bass.ds(b, 1), k])
                last.then_inc(sem("m_base"), 1)

            def close(b, par):
                act.wait_ge(sem("m_var"), b + 1)
                nc.scalar.activation(rm[:, par, 0, :], mvm[par][:, :, 1], ACT.Sqrt, bias=eps[:, 0:1]).then_inc(sem("m_sd"), 1)
                act.wait_ge(sem("m_rs"), b + 1)
                for k in range(4):
                    row = acc[:, bass.ds(b, 1), k].rearrange("p a h -> p (a h)")
                    last = nc.scalar.activation(row, row, ACT.Identity,
                                                bias=rm[:, par, 2, k:k + 1], scale=rm[:, par, 1, k:k + 1])
                last.then_inc(sem("m_fin"), 1)

            act.wait_ge(sem("rsm_ready"), 1)
            act.wait_ge(sem("l2_mm"), TILES)
            act.wait_ge(sem("x1_in"), 16)
            base(0)
            base(1)
            with act.Fori(0, 1) as j:
                base(j * 2 + 2)
                close(j * 2, 0)
                base(j * 2 + 3)
                close(j * 2 + 1, 1)
            act.wait_ge(sem("x1_in"), 32)
            with act.Fori(1, B // 2 - 1) as j:
                base(j * 2 + 2)
                close(j * 2, 0)
                base(j * 2 + 3)
                close(j * 2 + 1, 1)
            close(6, 0)
            close(7, 1)

        @block.vector
        def _(dve):
            seq = Seq(dve, sem("dve_seq"))
            V = nc.vector

            def do(ins, fill=iter(())):
                seq.inc(ins)
                for other in fill:
                    other()
                    break
                seq.wait()

            def stats(src, slot):
                for k in range(4):
                    last = V.bn_stats(st[:, slot, k, :], src(k))
                do(last)
                for k in range(4):
                    last = V.bn_aggr(mv[slot][:, k, :], st[:, slot, k, :])
                last.then_inc(sem(f"var{slot}"), 1)

            V.memset(eps[:, 0:1], EPS)
            V.memset(eps[:, 1:2], EPS * EPS).then_inc(sem("one"), 1)
            V.memset(carry[:, :], 0.0)
            seq.inc(V.memset(carry_b[:, :], 0.0))
            for e in range(E):
                V.memset(iota8[:, 0, e:e + 1], float(e))
                V.memset(iota8[:, 1, e:e + 1], float(e * REGION))
            dve.wait_ge(sem("k_exp"), 1)
            for ht in range(2):
                for dup in range(2):
                    V.tensor_scalar(quant[:, 0, ht, dup], raw[:, 1, ht], dtv[:, 1, ht:ht + 1], 0.15915494309189535,
                                    ALU.mult, ALU.mult)
                    last = V.tensor_scalar(quant[:, 1, ht, dup], sm[:, 0, ht], dtv[:, 1, ht:ht + 1], -1.0,
                                           ALU.mult, ALU.mult)
            last.then_inc(sem("k_ua"), 1)
            dve.wait_ge(sem("k_ua"), 1)
            do(V.tensor_scalar(sm[:, 2], quant[:, 0, :, 0], 0.5, None, ALU.mult))
            do(V.tensor_scalar(sm[:, 3], sm[:, 2], 0.25, None, ALU.add))
            do(V.tensor_scalar(sm2[:, 0:2], sm[:, 2:4], ROUND, ROUND, ALU.add, ALU.subtract))
            V.tensor_tensor(sm[:, 2:4], sm[:, 2:4], sm2[:, 0:2], ALU.subtract).then_inc(sem("k_half"), 1)
            dve.wait_ge(sem("k_tanh"), 1)
            em1, t1, t2, t3 = sm2[:, 2], sm2[:, 3], sm2[:, 4], sm2[:, 5]
            do(V.tensor_scalar(t1, sm[:, 1], -1.0, 1.0, ALU.mult, ALU.add))
            do(V.reciprocal(t2, t1))
            do(V.scalar_tensor_tensor(em1, sm[:, 1], 2.0, t2, ALU.mult, ALU.mult))
            ea, ai, cr, ci = sm[:, 0], raw[:, 1], raw[:, 2], raw[:, 3]
            dve.wait_ge(sem("k_trig"), 1)
            sn, cs = sm[:, 4], sm[:, 5]
            ere, eim, nre, nim = sm2[:, 6], sm2[:, 7], sm2[:, 8], sm2[:, 9]
            do(V.tensor_tensor(t1, sn, sn, ALU.mult))
            do(V.tensor_scalar(t2, t1, -2.0, 1.0, ALU.mult, ALU.add))
            do(V.tensor_tensor(t2, em1, t2, ALU.mult))
            do(V.scalar_tensor_tensor(ere, t1, -2.0, t2, ALU.mult, ALU.add))
            do(V.tensor_tensor(t3, sn, cs, ALU.mult))
            do(V.scalar_tensor_tensor(t1, em1, 1.0, t3, ALU.add, ALU.mult))
            do(V.tensor_scalar(eim, t1, 2.0, None, ALU.mult))
            dve.wait_ge(sem("in_coef"), 32)
            do(V.tensor_tensor(t1, cr, ere, ALU.mult))
            do(V.tensor_tensor(t2, ci, eim, ALU.mult))
            do(V.tensor_tensor(nre, t1, t2, ALU.subtract))
            do(V.tensor_tensor(t1, cr, eim, ALU.mult))
            do(V.tensor_tensor(t2, ci, ere, ALU.mult))
            do(V.tensor_tensor(nim, t1, t2, ALU.add))
            do(V.tensor_tensor(t1, ea, ea, ALU.mult))
            do(V.tensor_tensor(t2, ai, ai, ALU.mult))
            do(V.tensor_tensor(t1, t1, t2, ALU.add))
            do(V.reciprocal(t3, t1))
            do(V.tensor_tensor(t1, nim, ai, ALU.mult))
            do(V.tensor_tensor(t2, nre, ea, ALU.mult))
            do(V.tensor_tensor(t1, t1, t2, ALU.subtract))
            for dup in range(2):
                do(V.scalar_tensor_tensor(quant[:, 2, :, dup], t1, 2.0, t3, ALU.mult, ALU.mult))
            do(V.tensor_tensor(t1, nim, ea, ALU.mult))
            do(V.tensor_tensor(t2, nre, ai, ALU.mult))
            do(V.tensor_tensor(t1, t1, t2, ALU.add))
            for dup in range(2):
                last = V.scalar_tensor_tensor(quant[:, 3, :, dup], t1, -2.0, t3, ALU.mult, ALU.mult)
            last.then_inc(sem("k_quant"), 1)
            G1, G2 = QN, QN + PN
            dve.wait_ge(sem("k_qt"), 1)
            dve.wait_ge(sem("in_slots"), 32)

            def turns(g):
                for p in range(PN):
                    last = V.tensor_scalar(v[:, g + p], qt[:, 0], float(QN * p), so[:, g:g + 1], ALU.mult, ALU.add)
                do(last)

            def whole(g, i):
                V.tensor_scalar(kr[i][:, :, :], v[:, g:g + PN], ROUND, ROUND, ALU.add,
                                ALU.subtract).then_inc(sem(f"k_round{g}"), 1)

            def fraction(g, i):
                dve.wait_ge(sem(f"k_round{g}"), 1)
                V.tensor_tensor(v[:, g:g + PN], v[:, g:g + PN], kr[i][:, :, :], ALU.subtract).then_inc(sem(f"k_frac{g}"), 1)

            def wide(q, hs=slice(0, H)):
                return qt[:, q, hs].unsqueeze(1).to_broadcast([P, PN, hs.stop - hs.start])

            turns(G2)
            whole(G2, 1)
            turns(G1)
            whole(G1, 0)
            fraction(G1, 0)
            dve.wait_ge(sem("k_tr"), 2)
            V.tensor_copy(qt[:, 2:4], bank(1).rearrange("p (q h) -> p q h", q=2)).then_inc(sem("k_qt"), 1)
            dve.wait_ge(sem("k_frac%d" % G1), 1)
            dve.wait_ge(sem("k_turned"), 1)
            whole(0, 0)
            fraction(0, 0)
            dve.wait_ge(sem("k_frac%d" % G2), 1)
            dve.wait_ge(sem("k_turned"), 2)
            whole(PN, 1)
            fraction(PN, 1)
            dve.wait_ge(sem("k_qt"), 2)
            dve.wait_ge(sem("k_sin"), SINES.index(G1) + 1)
            do(V.tensor_tensor(v[:, G1:G2], v[:, G1:G2], wide(2), ALU.mult))
            dve.wait_ge(sem("k_sin"), SINES.index(0) + 1)
            dve.wait_ge(sem("k_mag"), MAGS.index(0) + 1)
            V.tensor_tensor(v[:, 0:PN], v[:, 0:PN], mag[0], ALU.mult)
            dve.wait_ge(sem("k_g2"), 1)
            do(V.tensor_tensor(v[:, G1:G2], v[:, G1:G2], v[:, G2:SLOTS], ALU.add))
            dve.wait_ge(sem("k_mag"), MAGS.index(G1) + 1)
            for ht in range(2):
                hs = slice(ht * P, ht * P + P)
                V.tensor_tensor(v[:, G1:G2, hs], v[:, G1:G2, hs], mag_p[:, :, hs], ALU.mult).then_inc(sem("k_pf"), 1)
            dve.wait_ge(sem("in_upper"), 16)
            V.tensor_copy(upper[:, :, :], upper_f[:, :, :]).then_inc(sem("upper_set"), 1)
            def mult(row, u):
                if row.first():
                    dve.wait_ge(sem("kf_mm"), u + 1)
                    for k in range(2):
                        last = V.tensor_tensor(kf[:, 0, 2 * u + k], bank(4 + u)[:, k * H:(k + 1) * H], d_rep[:, :], ALU.add)
                    last.then_inc(sem(f"kf_ready{u}"), 1)
                    dve.wait_ge(sem(f"kf_ready{u}"), 2)
                n, par = row.b * 2 + u, row.par
                dve.wait_ge(sem("fwd_mm"), n + 1)
                if not row.first():
                    dve.wait_ge(sem("yf_ready"), 2 * n - 2)
                if not row.first(2):
                    dve.wait_ge(sem("inv_mm"), row.b - 1)
                re, im = fw[u]
                ks = slice(2 * u, 2 * u + 2)
                V.tensor_tensor(yf[par][:, 0, ks], re, kf[:, 0, ks], ALU.mult)
                V.tensor_tensor(tmp[u][:, 0], im, kf[:, 1, ks], ALU.mult)
                V.tensor_tensor(yf[par][:, 1, ks], re, kf[:, 1, ks], ALU.mult)
                V.tensor_tensor(tmp[u][:, 1], im, kf[:, 0, ks], ALU.mult).then_inc(sem("mult_done"), 1)

            def inverse(row, slot):
                dve.wait_ge(sem(f"sd{slot}"), row.b + 1)
                return V.reciprocal(rs[:, slot, 0:4], sd[:, slot, :])

            def scales(new):
                if not new.first():
                    dve.wait_ge(sem("xn_ready"), new.b)
                do(inverse(new, 0))
                V.scalar_tensor_tensor(rs[:, 0, 4:8], mv[0][:, :, 0], -1.0, rs[:, 0, 0:4], ALU.mult,
                                       ALU.mult).then_inc(sem("st_x"), 1)

            def split_low(e):
                dve.wait_ge(sem("w_high"), e + 1)
                V.tensor_tensor(ws[:, e, 1], w_raw[e][:, :], ws[:, e, 0].bitcast(F32), ALU.subtract).then_inc(sem("w_low"), 1)

            def choose(row, fill):
                dve.wait_ge(sem("lg_mm"), row.b + 1)
                do(V.tensor_tensor(lgs[:, :, :], route(row.b)[1][:, 0:32].rearrange("p (k e) -> p k e", k=4),
                                   rb_sb[:, :].unsqueeze(1).to_broadcast([P, 4, E]), ALU.add), fill)
                for k in range(4):
                    last = V.max(mx_all[:, row.b, k], lgs[:, k])
                do(last, fill)
                for k in range(4):
                    last = V.max_index(mi[:, k], mx_all[:, row.b, k], lgs[:, k])
                do(last, fill)
                do(V.tensor_copy(mif[:, :, :], mi[:, :, 0:2].rearrange("p t c -> p c t")), fill)
                for c in range(2):
                    last = V.tensor_tensor(oh[:, c], iota8[:, 0].unsqueeze(1).to_broadcast([P, 4, E]),
                                           mif[:, c].unsqueeze(2).to_broadcast([P, 4, E]), ALU.is_equal)
                do(last)
                V.tensor_tensor(mask[:, :, :], oh[:, 0], oh[:, 1], ALU.add).then_inc(sem("mask_ready"), 1)

            def place(row):
                dve.wait_ge(sem("rank_mm"), row.b + 1)
                V.tensor_reduce(msum[:, :], mask[:, :, :].rearrange("p t e -> p e t"), AX.X, ALU.add)
                do(V.tensor_tensor(posf[:, :, :], route(row.b)[1][:, 64:96].rearrange("p (t e) -> p t e", t=4),
                                   iota8[:, 1].unsqueeze(1).to_broadcast([P, 4, E]), ALU.add))
                V.tensor_tensor(carry[:, :], carry[:, :], msum[:, :], ALU.add)
                for c in range(2):
                    last = V.tensor_tensor(prod[:, c], oh[:, c], posf[:, :, :], ALU.mult)
                do(last)
                V.tensor_copy(carry_b[:, :], carry[:, :]).then_inc(sem("carry_ready"), 1)
                do(V.tensor_reduce(posr[:, :, :], prod[:, :, :, :], AX.X, ALU.add))
                if not row.first(2):
                    dve.wait_ge(sem(f"scattered{row.par}"), 64 * min(row.b - row.par, 6))
                V.tensor_copy(zn[buf(row.b)][:, :, H], tok[:, row.b])
                V.tensor_copy(zn[buf(row.b)][:, :, H + 1], mif[:, 1])
                V.tensor_copy(pos[row.par][:, :, :], posr[:, :, :]).then_inc(sem("pos_ready"), 1)

            def step(n):
                new, nxt, cur, mid, tail = (Row(n, k) for k in (2, 1, -1, -2, -LAG))
                def mid_statistics():
                    for k in range(4):
                        last = V.bn_aggr(mv[3][:, k, :], st[:, 3, k, :])
                    last.then_inc(sem("var3"), 1)

                def mid_scales():
                    if not mid.first():
                        dve.wait_ge(sem("zn_ready"), mid.b)
                    do(inverse(mid, 3))
                    V.tensor_copy(stat1[:, mid.b], mv[3][:, :, :].rearrange("p k c -> p c k"))
                    V.scalar_tensor_tensor(rs[:, 3, 4:8], mv[3][:, :, 0], -1.0, rs[:, 3, 0:4], ALU.mult,
                                           ALU.mult).then_inc(sem("st_x1"), 1)

                def mid_now():
                    dve.wait_ge(sem("x1_ready"), mid.b + 1)
                    for k in range(4):
                        last = V.bn_stats(st[:, 3, k, :], xs[mid.b][:, k])
                    do(last)
                    mid_statistics()
                    mid_scales()

                if cur.live:
                    dve.wait_ge(sem("s_copied"), cur.b + 1)
                    c = iv[0].rearrange("p (j h) -> p j h", j=2)
                    V.tensor_tensor(r[:, 0:2], c, s_sb[:, :, :], ALU.add)
                    V.tensor_tensor(r[:, 2:4], c, s_sb[:, :, :], ALU.subtract).then_inc(sem("r_ready"), 1)
                    dve.wait_ge(sem("r_ready"), cur.b + 1)
                    stats(lambda k: r[:, k], 2)
                if new.live and new.b > 1:
                    if new.b == 2:
                        dve.wait_ge(sem("in_x2"), 96)
                    stats(lambda k: xs[new.b][:, k], 0)
                if cur.live:
                    do(inverse(cur, 2))
                    V.scalar_tensor_tensor(rs[:, 2, 4:8], mv[2][:, :, 0], -1.0, rs[:, 2, 0:4], ALU.mult,
                                           ALU.mult).then_inc(sem("st_r"), 1)
                if new.live and new.b > 1:
                    scales(new)
                if nxt.live:
                    mult(nxt, 0)
                if n == B:
                    mid_now()
                if cur.live:
                    dve.wait_ge(sem("r_norm"), cur.b + 1)
                    if not cur.first():
                        dve.wait_ge(sem("dl_ready"), cur.b)
                    do(V.tensor_tensor(o[:, :, :], r[:, :, :], lwb[:, 0].unsqueeze(1).to_broadcast([P, 4, H]), ALU.mult))
                    do(V.tensor_tensor(o[:, :, :], o[:, :, :], lwb[:, 1].unsqueeze(1).to_broadcast([P, 4, H]), ALU.add))
                    stats(lambda k: o[:, k], 1)
                if nxt.live:
                    mult(nxt, 1)
                if cur.live:
                    do(inverse(cur, 1))
                    V.scalar_tensor_tensor(rs[:, 1, 4:8], mv[1][:, :, 0], -1.0, rs[:, 1, 0:4], ALU.mult,
                                           ALU.mult).then_inc(sem("st_o"), 1)
                fill = []
                if mid.live and n < B and tail.live:
                    dve.wait_ge(sem("x1_ready"), mid.b + 1)
                    fill = [lambda k=k: V.bn_stats(st[:, 3, k, :], xs[mid.b][:, k]) for k in range(4)]
                elif mid.live and n != B:
                    mid_now()
                for e in LOW.get(n, ()):
                    split_low(e)
                if tail.live:
                    choose(tail, iter(fill))
                    if fill:
                        mid_statistics()
                    place(tail)
                    if fill:
                        mid_scales()

            dve.wait_ge(sem("in_small"), 128)
            seq.inc(V.tensor_scalar(d_rep[:, :], d_rep[:, :], 1.0, None, ALU.add))
            dve.wait_ge(sem("in_x"), 32)
            for n in (-2, -1):
                stats(lambda k: xs[n + 2][:, k], 0)
                scales(Row(n, 2))
            steps(step)

            dve.wait_ge(sem("zn_ready"), B)
            dve.wait_ge(sem("cnt_mm"), 1)
            do(V.tensor_copy(cnt[:, 0], tp[1][:, 0:E]))
            V.memset(zpad[:, 0:H], 0.0)
            V.memset(zpad[:, H + 1:W], -1.0)
            V.tensor_scalar(zpad[:, H:H + 1], tok[:, 0, 0:1], 1.0 / (4 * B), float(TRASH), ALU.mult, ALU.add)
            V.tensor_scalar(cnt[:, 1], cnt[:, 0], 1.0 / P, (P - 1) / (2.0 * P), ALU.mult, ALU.add)
            V.tensor_tensor(padf[:, :], cnt[0:1, 0], iota8[0:1, 1], ALU.add)
            V.tensor_tensor(padi[:, :], cnt[0:1, 0], iota8[0:1, 1], ALU.add).then_inc(sem("pad_set"), 1)
            dve.wait_ge(sem("pad_set"), 1)
            do(V.tensor_scalar(cnt[:, 1], cnt[:, 1], ROUND, ROUND, ALU.add, ALU.subtract))
            dve.wait_ge(sem("in_e"), 32)
            do(V.tensor_tensor(tri[:, :, :], tri[:, :, :], cnt[:, 1].unsqueeze(1).to_broadcast([P, E, E]), ALU.mult))
            do(V.tensor_reduce(cnt[:, 2], tri[:, :, :], AX.X, ALU.add))
            NT = TILES + 1
            do(V.tensor_tensor(cmp_t[:, :, :], cnt[:, 2].unsqueeze(1).to_broadcast([P, NT, E]),
                               iot[:, 0].unsqueeze(2).to_broadcast([P, NT, E]), ALU.is_le))
            do(V.tensor_tensor(cmp_n[:, :, :], cmp_t[:, :, :], cnt[:, 1].unsqueeze(1).to_broadcast([P, NT, E]), ALU.mult))
            V.tensor_reduce(tf[:, 0], cmp_t[:, :, :], AX.X, ALU.add)
            do(V.tensor_reduce(tf[:, 1], cmp_n[:, :, :], AX.X, ALU.add))
            V.tensor_scalar(tab[:, 1], tf[0:1, 0], float(E - 1), None, ALU.min)
            V.tensor_scalar(tab_e[:, :], tf[:, 0], float(E - 1), None, ALU.min)
            do(V.scalar_tensor_tensor(tf[:, 2], tf[:, 0], float(REGION), iot[:, 1], ALU.mult, ALU.add))
            do(V.scalar_tensor_tensor(tf[0:1, 0], tf[0:1, 1], -float(P), tf[0:1, 2], ALU.mult, ALU.add))
            V.tensor_scalar(tab[:, 0], tf[0:1, 0], padf[:, E - 1:E], None, ALU.min).then_inc(sem("tab_ready"), 1)
            for e in LOW[B + LAG]:
                split_low(e)
            V.tensor_tensor(wsm[:, :, :, :], mx_all[:, :, :, :], mx_all[:, :, :, 0:1].to_broadcast([P, B, 4, E]),
                            ALU.subtract).then_inc(sem("wsm_sub"), 1)
            dve.wait_ge(sem("rsm_sd"), 1)
            do(V.reciprocal(rsm[:, 0], rsm[:, 0]))
            do(V.scalar_tensor_tensor(rsm[:, 1], stat1[:, :, 0, :], -1.0, rsm[:, 0], ALU.mult, ALU.mult))
            dve.wait_ge(sem("wsm_exp"), 1)
            do(V.tensor_reduce(rsm[:, 2], wsm[:, :, :, :], AX.X, ALU.add))
            do(V.reciprocal(rsm[:, 3], rsm[:, 2]))
            for c in range(2):
                last = V.tensor_tensor(wgt[:, c], wsm[:, :, :, c], rsm[:, 3], ALU.mult)
            do(last)
            do(V.tensor_tensor(wgt[:, 2], wgt[:, 0], wgt[:, 1], ALU.add))
            do(V.tensor_scalar(wgt[:, 2], wgt[:, 2], 1e-8, None, ALU.max))
            do(V.reciprocal(wgt[:, 3], wgt[:, 2]))
            for c in range(2):
                last = V.tensor_tensor(wgt[:, c], wgt[:, c], wgt[:, 3], ALU.mult)
            last.then_inc(sem("rsm_ready"), 1)
            dve.wait_ge(sem("rsm_ready"), 1)

            dve.wait_ge(sem("in_b"), 32 * E)

            def part(i, par, u):
                t, q = i + 2, par
                if live(t):
                    dve.wait_ge(sem(f"z_in{q}"), (t - q) * 8 + 16)
                    V.tensor_scalar(flag[:, :], z_in[q][:, H + 1:W], tab_e[:, bass.ds(t, 1)], float(B * T),
                                    ALU.is_equal, ALU.mult).then_inc(sem("flag_set"), 1)
                    dve.wait_ge(sem("flag_set"), t + 1)
                    V.tensor_tensor(dest[:, bass.ds(t, 1)], z_in[q][:, H:H + 1], flag[:, :],
                                    ALU.add).then_inc(sem("dest_ready"), 1)
                    dve.wait_ge(sem("zf_ready"), t + 1)
                    if not early(t, 2):
                        dve.wait_ge(sem("l1_mm"), t - 1)
                    V.tensor_copy(z_hl[q][:, 0], z_f[:, :, :]).then_inc(sem("z_high"), 1)
                    dve.wait_ge(sem("z_high"), t + 1)
                    V.tensor_tensor(z_hl[q][:, 1], z_f[:, :, :], z_hl[q][:, 0].bitcast(F32),
                                    ALU.subtract).then_inc(sem("z_split"), 1)
                t, q = i + 1, 1 - par
                if live(t):
                    e = expert(dve, t, u + 1)
                    dve.wait_ge(sem("l1_mm"), t + 1)
                    if not early(t):
                        dve.wait_ge(sem("hg_ready"), t)
                    V.tensor_tensor(hb[:, :], ps_h[q], b1r[:, bass.ds(e, 1)].rearrange("p a f -> p (a f)"),
                                    ALU.add).then_inc(sem("hb_ready"), 1)
                t, q = i, par
                if live(t):
                    dve.wait_ge(sem("h_high"), t + 1)
                    V.tensor_tensor(h_hl[q][:, 1], ps_t[q], h_hl[q][:, 0].bitcast(F32),
                                    ALU.subtract).then_inc(sem("h_split"), 1)
                t, q = i - 1, 1 - par
                if live(t):
                    e = expert(dve, t, u - 1)
                    dve.wait_ge(sem("l2_mm"), t + 1)
                    if not early(t, 2):
                        dve.wait_ge(sem(f"y_out{q}"), (t - q) * 8)
                    gate(dve)
                    V.tensor_copy(dst[q][:, :], dest[:, bass.ds(t, 1)])
                    V.tensor_tensor(y_sb[q][:, :], ps_y[q], b2r[:, bass.ds(e, 1)].rearrange("p a f -> p (a f)"),
                                    ALU.add).then_inc(sem("y_ready"), 1)

            tiles(dve, part)

            def mix(b, par):
                dve.wait_ge(sem("m_base"), b + 1)
                dve.wait_ge(sem("m_sum"), b + 1)
                row = acc[:, bass.ds(b, 1)].rearrange("p a k h -> p (a k h)")
                V.tensor_tensor(row, row, ps_mix[par], ALU.add).then_inc(sem("m_mixed"), 1)
                dve.wait_ge(sem("m_mixed"), b + 1)
                gate(dve)
                for k in range(4):
                    last = V.bn_stats(st[:, par, k, :], acc[:, bass.ds(b, 1), k].rearrange("p a h -> p (a h)"))
                last.then_inc(sem("m_stat"), 1)
                dve.wait_ge(sem("m_stat"), b + 1)
                gate(dve)
                for k in range(4):
                    last = V.bn_aggr(mvm[par][:, k, :], st[:, par, k, :])
                last.then_inc(sem("m_var"), 1)

            def scale(b, par):
                dve.wait_ge(sem("m_sd"), b + 1)
                V.reciprocal(rm[:, par, 1, :], rm[:, par, 0, :]).then_inc(sem("m_inv"), 1)
                dve.wait_ge(sem("m_inv"), b + 1)
                V.scalar_tensor_tensor(rm[:, par, 2, :], mvm[par][:, :, 0], -1.0, rm[:, par, 1, :], ALU.mult,
                                       ALU.mult).then_inc(sem("m_rs"), 1)

            def add(n):
                dve.wait_ge(sem("m_fin"), n + 1)
                row = acc[:, bass.ds(n, 1)]
                V.tensor_tensor(row, row, x1m[:, bass.ds(back(n), 1)], ALU.add).then_inc(sem("m_out"), 1)

            mix(0, 0)
            for n in range(3):
                mix(n + 1, (n + 1) % 2)
                scale(n, n % 2)
                if n:
                    add(n - 1)
            dve.wait_ge(sem("x1_in"), 32)
            with dve.Fori(1, B // 2 - 1) as j:
                mix(j * 2 + 2, 0)
                scale(j * 2 + 1, 1)
                add(j * 2)
                mix(j * 2 + 3, 1)
                scale(j * 2 + 2, 0)
                add(j * 2 + 1)
            scale(B - 1, 1)
            add(B - 2)
            add(B - 1)

        @block.gpsimd
        def _(pool):
            G = nc.gpsimd
            G2 = QN + PN
            pool.wait_ge(sem("k_qt"), 1)
            pool.wait_ge(sem("in_slots"), 32)
            for g in (QN, PN):
                G.tensor_tensor(mag[g], qt[:, 1].unsqueeze(1).to_broadcast([P, PN, H]),
                                sc[:, g:g + PN].unsqueeze(2).to_broadcast([P, PN, H]), ALU.mult).then_inc(sem("k_aq"), 1)
            pool.wait_ge(sem(f"k_round{G2}"), 1)
            G.tensor_tensor(v[:, G2:SLOTS], v[:, G2:SLOTS], kr[1][:, :, :],
                            ALU.subtract).then_inc(sem(f"k_frac{G2}"), 1)
            pool.wait_ge(sem("k_sin"), SINES.index(G2) + 1)
            pool.wait_ge(sem("k_qt"), 2)
            G.tensor_tensor(v[:, G2:SLOTS], v[:, G2:SLOTS], qt[:, 3].unsqueeze(1).to_broadcast([P, PN, H]),
                            ALU.mult).then_inc(sem("k_g2"), 1)
            pool.wait_ge(sem("k_sin"), SINES.index(PN) + 1)
            pool.wait_ge(sem("k_mag"), MAGS.index(PN) + 1)
            for ht in range(2):
                hs = slice(ht * P, ht * P + P)
                G.tensor_tensor(v[:, PN:QN, hs], v[:, PN:QN, hs], mag_q[:, PN:QN, hs], ALU.mult).then_inc(sem("k_qf"), 1)

            def combine(row, u):
                n, par = row.b * 2 + u, row.par
                pool.wait_ge(sem("mult_done"), n + 1)
                ks = slice(2 * u, 2 * u + 2)
                G.tensor_tensor(yf[par][:, 0, ks], yf[par][:, 0, ks], tmp[u][:, 0],
                                ALU.subtract).then_inc(sem("yf_ready"), 1)
                G.tensor_tensor(yf[par][:, 1, ks], yf[par][:, 1, ks], tmp[u][:, 1],
                                ALU.add).then_inc(sem("yf_ready"), 1)

            def fold(new):
                pool.wait_ge(sem("xn_ready"), new.b + 1)
                if not new.first(2):
                    pool.wait_ge(sem("fwd_mm"), 2 * (new.b - 1))
                G.tensor_tensor(pm[new.par][:, 0], xn[:, 0:2], xn[:, 2:4], ALU.add).then_inc(sem("pm_ready"), 1)
                G.tensor_tensor(pm[new.par][:, 1], xn[:, 0:2], xn[:, 2:4], ALU.subtract).then_inc(sem("pm_ready"), 1)

            def split_low(e):
                pool.wait_ge(sem("w_high"), e + 1)
                G.tensor_tensor(ws[:, e, 1], w_raw[e][:, :], ws[:, e, 0].bitcast(F32), ALU.subtract).then_inc(sem("w_low"), 1)

            def step(n):
                new, nxt, cur, tail = (Row(n, k) for k in (2, 1, -1, -LAG))
                if nxt.live:
                    combine(nxt, 0)
                if new.live and new.b > 1:
                    fold(new)
                if nxt.live:
                    combine(nxt, 1)
                if cur.live:
                    pool.wait_ge(sem("dl_ready"), cur.b + 1)
                    G.tensor_tensor(xs[cur.b][:, :, :], xs[cur.b][:, :, :], dl[:, :, :], ALU.add).then_inc(sem("x1_ready"), 1)
                for e in LOW_POOL.get(n, ()):
                    split_low(e)
                if tail.live:
                    pool.wait_ge(sem("pos_ready"), tail.b + 1)
                    pool.wait_ge(sem("zn_ready"), tail.b + 1)
                    for c in range(2):
                        for k in range(4):
                            pool.indirect_dma_start(
                                z_rows, bass.IndirectOffsetOnAxis(ap=pos[tail.par][:, c, k:k + 1], axis=0),
                                zn[buf(tail.b)][:, k], None).then_inc(sem(f"scattered{buf(tail.b)}"), 16)

            fold(Row(-2, 2))
            fold(Row(-1, 2))
            steps(step)

            for e in LOW_POOL[B + LAG]:
                split_low(e)

            def scatter_y(t, q):
                pool.wait_ge(sem("y_ready"), t + 1)
                if not early(t):
                    pool.wait_ge(sem(f"y_out{1 - q}"), (t + q) * 8)
                gate(pool)
                pool.indirect_dma_start(y_rows, bass.IndirectOffsetOnAxis(ap=dst[q][:, 0:1], axis=0),
                                        y_sb[q][:, :], None).then_inc(sem(f"y_out{q}"), 16)

            scatter_y(0, 0)
            with pool.Fori(0, (TILES - 1) // 2) as j:
                scatter_y(j * 2 + 1, 1)
                scatter_y(j * 2 + 2, 0)

            def weights(n, par):
                if not early(n, 2):
                    pool.wait_ge(sem("m_sum"), n - 1)
                w = wgt[:, 0:2, bass.ds(back(n), 1)].rearrange("p c a k -> p c (a k)")
                G.tensor_tensor(diag[par][:, :, :, :], ident[:, :].unsqueeze(1).unsqueeze(1).to_broadcast([P, 2, 4, P]),
                                w.unsqueeze(3).to_broadcast([P, 2, 4, P]), ALU.mult).then_inc(sem("m_diag"), 1)

            pool.wait_ge(sem("rsm_ready"), 1)
            pool.wait_ge(sem("hb_ready"), TILES)
            weights(0, 0)
            weights(1, 1)
            with pool.Fori(1, B // 2) as j:
                weights(j * 2, 0)
                weights(j * 2 + 1, 1)

        @block.tensor
        def _(pe):
            TE = nc.tensor
            for q in range(4):
                if q % 2 == 0:
                    pe.wait_ge(sem("k_quant" if q else "k_ua"), 1)
                for ht in range(2):
                    last = TE.transpose(bank(0, 2)[:, q * H + ht * P:q * H + ht * P + P],
                                        quant[:, q, ht].rearrange("p d n -> p (d n)"), ident[:, :])
                if q % 2:
                    last.then_inc(sem("k_tr"), 1)
            for ht in range(2):
                pe.wait_ge(sem("k_pf"), ht + 1)
                pe.wait_ge(sem("k_qf"), ht + 1)
                for hh in range(P):
                    j, i = 2 * ht + hh // 64, hh % 64
                    last = TE.matmul(psum[32 * j:32 * j + PN, 2048 + i * QN:2048 + (i + 1) * QN],
                                     v[:, QN:QN + PN, ht * P + hh], v[:, 0:QN, ht * P + hh], start=True, stop=True)
                last.then_inc(sem("k_mm"), 1)
            def fwd(row, u):
                n = row.b * 2 + u
                pe.wait_ge(sem("pm_ready"), 2 * row.b + 2)
                if not row.first():
                    pe.wait_ge(sem("mult_done"), n - 1)
                for c in range(2):
                    for k in range(2):
                        kt = 2 * u + k
                        for t in range(2):
                            last = TE.matmul(fw[u][c][:, k], ft[:, c, t, kt * P:(kt + 1) * P], pm[row.par][:, c, t],
                                             start=t == 0, stop=t == 1)
                last.then_inc(sem("fwd_mm"), 1)

            pe.wait_ge(sem("in_tab"), 32)
            fwd(Row(-1, 1), 0)
            fwd(Row(-1, 1), 1)
            pe.wait_ge(sem("k_evac"), 4)
            for ht in range(2):
                pe.wait_ge(sem(f"k_in{ht}"), 32)
                for l in range(KT):
                    last = TE.transpose(tp[ht][:, l * P:(l + 1) * P], kh[:, ht, l * P:(l + 1) * P], ident[:, :])
                last.then_inc(sem("kt_mm"), 1)
            pe.wait_ge(sem("in_lag"), 16)
            pe.wait_ge(sem("kt_evac"), 2)
            for u, ht in ((0, 0), (0, 1), (1, 0), (1, 1)):
                for g in (2 * u, 2 * u + 1, KT + 2 * u, KT + 2 * u + 1):
                    for l in range(KT):
                        last = TE.matmul(bank(4, 4)[:, g * H + ht * P:g * H + ht * P + P], lag[:, l, g, :],
                                         k_t[:, l, ht * P:ht * P + P], start=l == 0, stop=l == KT - 1)
                if ht:
                    last.then_inc(sem("kf_mm"), 1)

            def inverse(row, j):
                if row.first():
                    for u in range(2):
                        pe.wait_ge(sem(f"kf_ready{u}"), 2)
                pe.wait_ge(sem("yf_ready"), 4 * row.b + 4)
                if not row.first():
                    pe.wait_ge(sem("r_ready"), row.b)
                for c in range(2):
                    for k in range(KT):
                        last = TE.matmul(iv[c][:, j * H:(j + 1) * H], it[:, c, k, j * P:(j + 1) * P],
                                         yf[row.par][:, c, k], start=k == 0, stop=k == KT - 1)
                if j == 1:
                    last.then_inc(sem("inv_mm"), 1)

            def turn(row):
                pe.wait_ge(sem("zn_ready"), row.b + 1)
                if 0 < row.b < B - 2:
                    pe.wait_ge(sem("pos_ready"), row.b)
                for k in range(2):
                    for q in range(4):
                        last = TE.transpose(route(row.b)[k][:, q * P:(q + 1) * P],
                                            zn[buf(row.b)][:, q, k * P:(k + 1) * P], ident[:, :])
                last.then_inc(sem("zt_mm"), 1)

            def step(n):
                nxt, cur, tail = Row(n, 1), Row(n, 0), Row(n, -LAG)
                if nxt.live and nxt.b:
                    fwd(nxt, 0)
                if tail.live and tail.b < B - 1:
                    turn(tail)
                if nxt.live and nxt.b:
                    fwd(nxt, 1)
                if cur.live:
                    inverse(cur, 0)
                if tail.live:
                    pe.wait_ge(sem("zt_ready"), 2 * tail.b + 2)
                    for q in range(4):
                        for k in range(2):
                            last = TE.matmul(route(tail.b)[1][:, q * E:(q + 1) * E], zt[:, k, q * P:(q + 1) * P], rw_sb[:, k, :],
                                             start=k == 0, stop=k == 1)
                    last.then_inc(sem("lg_mm"), 1)
                if cur.live:
                    inverse(cur, 1)
                if n == B + 1:
                    turn(Row(n, -2))
                if tail.live:
                    pe.wait_ge(sem("mask_ready"), tail.b + 1)
                    rank = route(tail.b)[1][:, 64:96]
                    m = mask[:, :, :].rearrange("p t e -> p (t e)")
                    TE.matmul(rank, upper[:, 0, :], m, start=True, stop=False)
                    for q in range(1, 4):
                        TE.matmul(rank[:, q * E:4 * E], upper[:, 1, :], m[:, 0:(4 - q) * E], start=False, stop=False)
                    if not tail.first():
                        pe.wait_ge(sem("carry_ready"), tail.b)
                    TE.matmul(rank.rearrange("p (t e) -> p t e", t=4), upper[:, 1, :],
                              carry_b[:, :].unsqueeze(1).to_broadcast([P, 4, E]), start=False,
                              stop=True).then_inc(sem("rank_mm"), 1)

            steps(step)
            pe.wait_ge(sem("pos_ready"), B)
            pe.wait_ge(sem("carry_ready"), B)
            TE.matmul(tp[1][:, 0:E], upper[:, 1, :], carry_b[:, :], start=True, stop=True).then_inc(sem("cnt_mm"), 1)

            def part(i, par, u):
                e1 = expert(pe, i + 1, u + 1) if live(i + 1) else 0
                e2 = expert(pe, i - 1, u - 1) if live(i - 1) else 0
                t, q = i + 2, par
                if live(t):
                    pe.wait_ge(sem(f"z_in{q}"), (t - q) * 8 + 16)
                    if not early(t, 2):
                        pe.wait_ge(sem("zf_ready"), t - 1)
                    for k in range(2):
                        last = TE.transpose(ps_z[q][:, k], z_in[q][:, k * P:(k + 1) * P], ident[:, :])
                    last.then_inc(sem("tz_mm"), 1)
                t, q = i + 1, 1 - par
                if live(t):
                    if early(t):
                        pe.wait_ge(sem("w_low"), E)
                    pe.wait_ge(sem("z_split"), t + 1)
                    if not early(t, 2):
                        pe.wait_ge(sem("hb_ready"), t - 1)
                    n = 0
                    for k in range(2):
                        for a, c in ((0, 0), (0, 1), (1, 0)):
                            last = TE.matmul(ps_h[q], z_hl[q][:, a, k], w_at(e1, c, k * F, F), start=n == 0, stop=n == 5)
                            n += 1
                    last.then_inc(sem("l1_mm"), 1)
                t, q = i, par
                if live(t):
                    pe.wait_ge(sem("hg_ready"), t + 1)
                    if not early(t, 2):
                        pe.wait_ge(sem("h_split"), t - 1)
                    for k in range(4):
                        last = TE.transpose(ps_t[q][:, k], hg[q][:, k * P:(k + 1) * P], ident[:, :])
                    last.then_inc(sem("th_mm"), 1)
                t, q = i - 1, 1 - par
                if live(t):
                    pe.wait_ge(sem("h_split"), t + 1)
                    if not early(t, 2):
                        pe.wait_ge(sem("y_ready"), t - 1)
                    n = 0
                    for k in range(4):
                        for a, c in ((0, 0), (0, 1), (1, 0)):
                            last = TE.matmul(ps_y[q], h_hl[q][:, a, k], w_at(e2, c, 1024 + k * H, H), start=n == 0, stop=n == 11)
                            n += 1
                    last.then_inc(sem("l2_mm"), 1)

            pe.wait_ge(sem("tab_ready"), 1)
            tiles(pe, part)

            def mix(n, par):
                pe.wait_ge(sem("m_diag"), n + 1)
                pe.wait_ge(sem(f"y1_in{par}"), n * 8 + 16 - 8 * par)
                pe.wait_ge(sem(f"y0_in{par}"), n * 8 + 16 - 8 * par)
                if not early(n, 2):
                    pe.wait_ge(sem("m_mixed"), n - 1)
                for k in range(4):
                    for c in (1, 0):
                        last = TE.matmul(ps_mix[par][:, k * H:(k + 1) * H], diag[par][:, c, k],
                                         ya[:, bass.ds(n, 1), c, k].rearrange("p a h -> p (a h)"),
                                         start=c == 1, stop=c == 0)
                last.then_inc(sem("m_sum"), 1)

            pe.wait_ge(sem("y_ready"), TILES)
            mix(0, 0)
            mix(1, 1)
            with pe.Fori(1, B // 2) as j:
                mix(j * 2, 0)
                mix(j * 2 + 1, 1)


MAGS = (QN, 0, PN)
SINES = (QN + PN, QN, 0, PN)
HIGH = {3: (0,), 4: (1,), 5: (2,), 6: (3,), 7: (4,), 9: (5,), 10: (6,)}
LOW = {9: (0,), 10: (1,), B + LAG: (4, 5, 6, 7)}
LOW_POOL = {B + LAG: (2, 3)}
USES = ("st_x", "st_o", "st_r", "st_x1")


def consts():
    import numpy as np
    t = np.arange(T // 2)
    k = np.arange(T)
    ang = np.pi / 2048 * (((2 * k[None, :] + 1) * (2 * t[:, None] - 511)) % 4096)
    f = np.stack([np.cos(ang), -np.sin(ang)])
    fwd = f.reshape(2, 2, P, T).transpose(2, 0, 1, 3)
    inv = (f / T).transpose(0, 2, 1).reshape(2, KT, P, T // 2).transpose(2, 0, 1, 3)
    l = np.arange(T)
    a2 = np.pi / 1024 * (((2 * k[None, :] + 1) * l[:, None]) % 2048)
    g = np.stack([np.cos(a2), -np.sin(a2)])
    lag = g.reshape(2, KT, P, KT, P).transpose(2, 1, 0, 3, 4).reshape(P, KT, 2 * KT, P)
    s = np.concatenate([np.arange(QN), QN * np.arange(PN), QN * np.arange(PN)])
    scale = np.broadcast_to(s, (P, SLOTS))
    off = np.zeros((P, SLOTS))
    off[:N, :QN], off[N:, :QN] = .25, 0
    off[:N, QN:QN + PN], off[N:, QN:QN + PN] = .25, .5
    off[:N, QN + PN:], off[N:, QN + PN:] = .5, .75
    up = np.stack([np.triu(np.ones((P, P)), 1), np.ones((P, P))], 1)
    nt = TILES + 1
    tile = np.concatenate([np.tile(np.concatenate([np.tril(np.ones((E, E))).ravel(), np.arange(nt), P * np.arange(nt)]),
                                   (P, 1)), np.arange(P * B * 4).reshape(P, B * 4)], 1)
    return [np.ascontiguousarray(a, dtype=np.float32) for a in (fwd, inv, lag, scale, off, np.eye(P), up, tile)]


_INS = ["log_A_real", "A_imag", "C_re", "C_im", "log_dt", "D", "ln_w", "ln_b"]
_FFN = ["ln_g", "ln_b", "rW", "rb", "W1", "b1", "W2", "b2"]


def kernel(**inputs):
    import numpy as np
    import concourse.bacc as bacc
    from concourse.bass_utils import run_bass_kernel_spmd

    x = np.asarray(inputs["L0_attn_x"])
    half = [x[:, :T // 2], x[:, :T // 2 - 1:-1]]
    x = np.concatenate([a.reshape(B, 2, P, H) for a in half], 1).transpose(2, 0, 1, 3)
    arrays = [x, *consts()]
    arrays += [inputs[f"L0_attn_{n}"] for n in _INS] + [inputs[f"L0_ffn_{n}"] for n in _FFN]
    nc = bacc.Bacc("TRN2", target_bir_lowering=False, num_devices=1)
    given, args = {}, []
    for i, a in enumerate(arrays):
        name = f"in_{i}_dram"
        given[name] = np.ascontiguousarray(a)
        args.append(nc.dram_tensor(name, given[name].shape, mybir.dt.from_np(given[name].dtype), kind="ExternalInput").ap())
    out = nc.dram_tensor("out_dram", (P, B, 4, H), F32, kind="ExternalOutput").ap()
    program(nc, *args, out)
    r = run_bass_kernel_spmd(nc, [given], core_ids=[0])
    y = r.results[0]["out_dram"].transpose(1, 2, 0, 3)
    return np.concatenate([y[:, :2].reshape(B, T // 2, H), y[:, 2:].reshape(B, T // 2, H)[:, ::-1]], 1)
```
